# Optimizing a Trainium2 kernel written in Bass

```python
import numpy as np
import jax
import jax.numpy as jnp

def _softmax(x, axis=-1):
    return jax.nn.softmax(x, axis=axis)

def _gelu(x):
    return jax.nn.gelu(x, approximate=True)

def _silu(x):
    return jax.nn.silu(x)

def _sigmoid(x):
    return jax.nn.sigmoid(x)

def _layernorm(x, axis=-1, eps=1e-05):
    m = jnp.mean(x, axis=axis, keepdims=True)
    v = jnp.var(x, axis=axis, keepdims=True)
    return (x - m) / jnp.sqrt(v + eps)

def _scatter_add(tgt, idx, src, axis=0):
    return tgt.at[idx].add(src)

def _segment_sum(src, seg, n):
    return jax.ops.segment_sum(src, seg, n)
kernel_name = 'mk_decoder_postln_d2_seqx_r8_0d206c'

def setup_inputs(seed: int=0):
    np.random.seed(seed)
    _w = jnp.asarray

    def _rec_inputs():
        import jax
        import jax.numpy as jnp
        _rk = jax.random.key(seed)
        x = 7.22e-05 + 1 * jax.random.normal(jax.random.fold_in(_rk, 1), (2, 512, 128), jnp.float32)
        _lenS = 512 - jax.random.randint(jax.random.fold_in(_rk, 7), (2,), 0, max(1, 512 // 4) + 1, jnp.int32)
        _lenS2 = 32 - jax.random.randint(jax.random.fold_in(_rk, 8), (2,), 0, max(1, 32 // 4) + 1, jnp.int32)
        _ctx_768P = jax.random.normal(jax.random.fold_in(_rk, 11), (2, 16, 96), jnp.float32)
        _ctx_768c = jax.random.dirichlet(jax.random.fold_in(_rk, 511), 0.3 * jnp.ones((16,), jnp.float32), (2, 32))
        _ctx_768t = jnp.einsum('bsk,bkd->bsd', _ctx_768c, _ctx_768P)
        _ctx_768t = _ctx_768t * jax.lax.rsqrt(jnp.mean(jnp.square(_ctx_768t)) + 1e-12) * 0.953939
        ctx_768 = -0.000191848 + 0.999787 * (_ctx_768t + 0.3 * jax.random.normal(jax.random.fold_in(_rk, 611), (2, 32, 96), jnp.float32))
        _validS = jnp.arange(512)[None, :] < _lenS[:, None]
        _validS2 = jnp.arange(32)[None, :] < _lenS2[:, None]
        _causal = jnp.tril(jnp.ones((512, 512), dtype=bool))
        mask_BxS2_bk0 = jnp.logical_not(jnp.broadcast_to(_validS2[:, :], (2, 32)))
        mask_BxS_bf1 = jnp.ones((2, 512), dtype=bool)
        mask_BxS2_bf1 = jnp.ones((2, 32), dtype=bool)
        return (x, ctx_768, mask_BxS2_bk0, mask_BxS_bf1, mask_BxS2_bf1)
    x, ctx_768, mask_BxS2_bk0, mask_BxS_bf1, mask_BxS2_bf1 = _rec_inputs()

    def _L0_attn_setup():
        import jax, jax.numpy as jnp
        import numpy as np
        from jax import lax
        DIM = 128
        EXP = 2
        GMLP_EXP = 2
        K = 4
        HID = DIM * EXP
        GHID = DIM * GMLP_EXP
        ALPHA_LOG_SCALE = -8.0

        def init_forget_gate(size, a=0.001, b=0.1, lo=-9.0, hi=-4.323):
            x = np.log(np.expm1(np.linspace(a, b, size, dtype=np.float64)))
            x = (x - x.min()) / (x.max() - x.min())
            x = x * abs(hi - lo) + lo
            return jnp.asarray(x, dtype=jnp.float32)

        def _rmsnorm(x, gamma):
            n = jnp.sqrt(jnp.sum(x * x, axis=-1, keepdims=True))
            return gamma * jnp.sqrt(jnp.float32(x.shape[-1])) * (x / n)

        def _linear_recurrence(alpha, x):

            def combine(e1, e2):
                a1, b1 = e1
                a2, b2 = e2
                return (a1 * a2, a2 * b1 + b2)
            _, h = lax.associative_scan(combine, (alpha, x), axis=1)
            return h

        def _hawk_block(x, W_in, conv_w, conv_b, W_gates, b_gates, forget_base, W_out, gamma1, gamma2, W_grow, W_shrink):
            B, T, _ = x.shape
            xn = _rmsnorm(x, gamma1)
            z = xn @ W_in.T
            gate, xc = (z[..., :HID], z[..., HID:])
            xc_t = jnp.pad(xc.transpose(0, 2, 1), ((0, 0), (0, 0), (K - 1, 0)))
            xc = lax.conv_general_dilated(xc_t, conv_w, window_strides=(1,), padding='VALID', dimension_numbers=('NCH', 'OIH', 'NCH'), feature_group_count=HID)
            xc = (xc + conv_b[None, :, None]).transpose(0, 2, 1)
            g = xc @ W_gates.T + b_gates
            forget, inp = (g[..., :HID], g[..., HID:])
            alpha = jnp.exp(ALPHA_LOG_SCALE * jax.nn.softplus(forget_base) * jax.nn.sigmoid(forget))
            beta = jnp.sqrt(1.0 - alpha ** 2 + 1e-06)
            xs = beta * jax.nn.sigmoid(inp) * xc
            h = _linear_recurrence(alpha, xs)
            rglru_out = jax.nn.gelu(gate, approximate=False) * h @ W_out.T
            x = x + rglru_out
            xn2 = _rmsnorm(x, gamma2)
            gz = xn2 @ W_grow.T
            mgate, mx = (gz[..., :GHID], gz[..., GHID:])
            mlp_out = jax.nn.gelu(mgate, approximate=False) * mx @ W_shrink.T
            return x + mlp_out
        key = jax.random.key(seed)
        ks = jax.random.split(key, 10)
        B, T = (4, 256)
        x = jax.random.normal(ks[0], (B, T, DIM), dtype=jnp.float32)
        W_in = jax.random.normal(ks[1], (2 * HID, DIM), dtype=jnp.float32) * DIM ** (-0.5)
        conv_w = jax.random.normal(ks[2], (HID, 1, K), dtype=jnp.float32) * (1.0 / K) ** 0.5
        conv_b = jnp.zeros((HID,), dtype=jnp.float32)
        W_gates = jax.random.normal(ks[3], (2 * HID, HID), dtype=jnp.float32) * HID ** (-0.5)
        b_gates = jnp.zeros((2 * HID,), dtype=jnp.float32)
        forget_base = init_forget_gate(HID)
        W_out = jax.random.normal(ks[4], (DIM, HID), dtype=jnp.float32) * HID ** (-0.5)
        gamma1 = jnp.ones((DIM,), dtype=jnp.float32)
        gamma2 = jnp.ones((DIM,), dtype=jnp.float32)
        W_grow = jax.random.normal(ks[5], (2 * GHID, DIM), dtype=jnp.float32) * DIM ** (-0.5)
        W_shrink = jax.random.normal(ks[6], (DIM, GHID), dtype=jnp.float32) * GHID ** (-0.5)
        return {'x': x, 'W_in': W_in, 'conv_w': conv_w, 'conv_b': conv_b, 'W_gates': W_gates, 'b_gates': b_gates, 'forget_base': forget_base, 'W_out': W_out, 'gamma1': gamma1, 'gamma2': gamma2, 'W_grow': W_grow, 'W_shrink': W_shrink}
    _L0_attn_all = _L0_attn_setup()
    _L0_attn_in = {k: v for k, v in _L0_attn_all.items() if k in ('W_in', 'conv_w', 'conv_b', 'W_gates', 'b_gates', 'forget_base', 'W_out', 'gamma1', 'gamma2', 'W_grow', 'W_shrink')}
    del _L0_attn_all

    def _L0_xattn_setup():
        import jax, jax.numpy as jnp
        import numpy as np
        HEADS = 8
        DIM_HEAD = 64
        QUERY_DIM = 128
        CONTEXT_DIM = 96
        INNER = HEADS * DIM_HEAD
        key = jax.random.key(seed)
        ks = jax.random.split(key, 8)
        b, n, j = (4, 256, 256)
        x = jax.random.normal(ks[0], (b, n, QUERY_DIM), dtype=jnp.float32)
        context = jax.random.normal(ks[1], (b, j, CONTEXT_DIM), dtype=jnp.float32)
        mask = jax.random.randint(ks[2], (b, j), 0, 2).astype(jnp.bool_)
        W_q = jax.random.normal(ks[3], (QUERY_DIM, INNER), dtype=jnp.float32) / np.sqrt(QUERY_DIM)
        W_k = jax.random.normal(ks[4], (CONTEXT_DIM, INNER), dtype=jnp.float32) / np.sqrt(CONTEXT_DIM)
        W_v = jax.random.normal(ks[5], (CONTEXT_DIM, INNER), dtype=jnp.float32) / np.sqrt(CONTEXT_DIM)
        W_o = jax.random.normal(ks[6], (INNER, QUERY_DIM), dtype=jnp.float32) / np.sqrt(INNER)
        b_o = jax.random.normal(ks[7], (QUERY_DIM,), dtype=jnp.float32) * 0.01
        return {'x': x, 'context': context, 'mask': mask, 'W_q': W_q, 'W_k': W_k, 'W_v': W_v, 'W_o': W_o, 'b_o': b_o}
    _L0_xattn_all = _L0_xattn_setup()
    _L0_xattn_in = {k: v for k, v in _L0_xattn_all.items() if k in ('W_q', 'W_k', 'W_v', 'W_o', 'b_o')}
    del _L0_xattn_all

    def _L0_ffn_setup():
        import jax, jax.numpy as jnp
        import numpy as np
        H = 128
        NH = 16
        HD = H // NH
        HH = HD // 2
        L = H // 4
        I = int(H * 1.0)
        ER = 7
        TOPK = 2
        BASE = 10000.0
        EPS = 1e-05

        def rmsnorm(x, w):
            norm = jnp.sqrt(jnp.mean(x * x, axis=-1, keepdims=True)) + EPS
            return x / norm * w

        def rope_tables(seq_len):
            inv_freq = 1.0 / BASE ** (jnp.arange(0, HH, 2, dtype=jnp.float32) / HH)
            t = jnp.arange(seq_len, dtype=jnp.float32)
            freqs = jnp.einsum('i,j->ij', t, inv_freq)
            emb = jnp.concatenate([freqs, freqs], axis=-1)
            cos = jnp.cos(emb)[None, :, None, :]
            sin = jnp.sin(emb)[None, :, None, :]
            return (cos, sin)

        def rotate_half(x):
            x1, x2 = jnp.split(x, 2, axis=-1)
            return jnp.concatenate([-x2, x1], axis=-1)

        def silu(x):
            return x * jax.nn.sigmoid(x)

        def mla(xn, W_kvd, W_qd, W_ku, W_qu, W_vu, W_ropeq, W_ropek, W_o):
            B, S, _ = xn.shape
            kv_lat = xn @ W_kvd
            q_lat = xn @ W_qd
            k = (kv_lat @ W_ku).reshape(B, S, NH, HH)
            q = (q_lat @ W_qu).reshape(B, S, NH, HH)
            v = (kv_lat @ W_vu).reshape(B, S, NH, HD)
            q_rope = (q_lat @ W_ropeq).reshape(B, S, NH, HH)
            k_rope = (xn @ W_ropek).reshape(B, S, NH, HH)
            cos, sin = rope_tables(S)
            k_rope = k_rope * cos + rotate_half(k_rope) * sin
            q_rope = q_rope * cos + rotate_half(q_rope) * sin
            kk = jnp.concatenate([k, k_rope], axis=-1)
            qq = jnp.concatenate([q, q_rope], axis=-1)
            scale = 1.0 / jnp.sqrt(jnp.float32(HD))
            scores = jnp.einsum('bqhd,bkhd->bhqk', qq, kk) * scale
            causal = jnp.tril(jnp.ones((S, S), dtype=bool))
            scores = jnp.where(causal[None, None], scores, jnp.finfo(scores.dtype).min)
            probs = jax.nn.softmax(scores, axis=-1)
            y = jnp.einsum('bhqk,bkhd->bqhd', probs, v).reshape(B, S, H)
            return y @ W_o

        def moe(xn, Wg_s, Wu_s, Wd_s, Wg_r, Wu_r, Wd_r, W_router, routing_bias):
            B, S, _ = xn.shape
            xt = xn.reshape(B * S, H)
            shared = silu(xt @ Wg_s) * (xt @ Wu_s) @ Wd_s
            logits = xt @ W_router + routing_bias
            probs = jax.nn.sigmoid(logits)
            scores, idx = jax.lax.top_k(probs, TOPK)
            scores = scores / jnp.sum(scores, axis=-1, keepdims=True)
            wts = jnp.sum(jax.nn.one_hot(idx, ER, dtype=xt.dtype) * scores[..., None], axis=1)
            g = jnp.einsum('th,ehi->tei', xt, Wg_r)
            u = jnp.einsum('th,ehi->tei', xt, Wu_r)
            hmid = silu(g) * u
            combined = jnp.einsum('tei,eih,te->th', hmid, Wd_r, wts)
            return (shared + combined).reshape(B, S, H)
        key = jax.random.key(seed)
        ks = jax.random.split(key, 20)
        s = 0.02
        r = lambda k, shp: jax.random.normal(k, shp, dtype=jnp.float32) * s
        return {'x': jax.random.normal(ks[0], (4, 128, H), dtype=jnp.float32), 'w_ln1': jnp.ones((H,), jnp.float32), 'w_ln2': jnp.ones((H,), jnp.float32), 'W_kvd': r(ks[1], (H, L)), 'W_qd': r(ks[2], (H, L)), 'W_ku': r(ks[3], (L, NH * HH)), 'W_qu': r(ks[4], (L, NH * HH)), 'W_vu': r(ks[5], (L, H)), 'W_ropeq': r(ks[6], (L, H // 2)), 'W_ropek': r(ks[7], (H, H // 2)), 'W_o': r(ks[8], (H, H)), 'Wg_s': r(ks[9], (H, I)), 'Wu_s': r(ks[10], (H, I)), 'Wd_s': r(ks[11], (I, H)), 'Wg_r': r(ks[12], (ER, H, I)), 'Wu_r': r(ks[13], (ER, H, I)), 'Wd_r': r(ks[14], (ER, I, H)), 'W_router': r(ks[15], (H, ER)), 'routing_bias': jnp.zeros((ER,), jnp.float32)}
    _L0_ffn_all = _L0_ffn_setup()
    _L0_ffn_in = {k: v for k, v in _L0_ffn_all.items() if k in ('w_ln1', 'w_ln2', 'W_kvd', 'W_qd', 'W_ku', 'W_qu', 'W_vu', 'W_ropeq', 'W_ropek', 'W_o', 'Wg_s', 'Wu_s', 'Wd_s', 'Wg_r', 'Wu_r', 'Wd_r', 'W_router', 'routing_bias')}
    del _L0_ffn_all

    def _L1_attn_setup():
        import jax, jax.numpy as jnp
        import numpy as np
        D_MODEL = 128
        D_STATE = 16
        key = jax.random.key(seed)
        ks = jax.random.split(key, 8)
        x = jax.random.normal(ks[0], (2, 256, D_MODEL), dtype=jnp.float32)
        A = -jnp.abs(jax.random.normal(ks[1], (D_MODEL, D_STATE), dtype=jnp.float32))
        s = 1.0 / np.sqrt(D_MODEL)
        Wd = jax.random.uniform(ks[2], (D_MODEL, D_MODEL), jnp.float32, -s, s)
        bd = jax.random.uniform(ks[3], (D_MODEL,), jnp.float32, -s, s)
        Wb = jax.random.uniform(ks[4], (D_STATE, D_MODEL), jnp.float32, -s, s)
        bb = jax.random.uniform(ks[5], (D_STATE,), jnp.float32, -s, s)
        Wc = jax.random.uniform(ks[6], (D_STATE, D_MODEL), jnp.float32, -s, s)
        bc = jax.random.uniform(ks[7], (D_STATE,), jnp.float32, -s, s)
        return {'x': x, 'A': A, 'Wd': Wd, 'bd': bd, 'Wb': Wb, 'bb': bb, 'Wc': Wc, 'bc': bc}
    _L1_attn_all = _L1_attn_setup()
    _L1_attn_in = {k: v for k, v in _L1_attn_all.items() if k in ('A', 'Wd', 'bd', 'Wb', 'bb', 'Wc', 'bc')}
    del _L1_attn_all

    def _L1_xattn_setup():
        import jax, jax.numpy as jnp
        import numpy as np
        B, T, DT, G, DV = (16, 64, 128, 72, 96)
        H, DH = (4, 32)
        INNER = H * DH
        HID = 4 * DT
        N_STATE = 64
        K_TOP = 32

        def layernorm(x, g, b, eps=1e-05):
            m = x.mean(-1, keepdims=True)
            v = x.var(-1, keepdims=True)
            return (x - m) * jax.lax.rsqrt(v + eps) * g + b

        def s4d(x, log_dt, A_re, A_im, C_re, C_im, D_skip):
            Bb, L, D = x.shape
            dt = jnp.exp(log_dt)
            A = A_re + 1j * A_im
            C = C_re + 1j * C_im
            dtA = dt[:, None] * A
            dC = C * (jnp.exp(dtA) - 1.0) / A
            powers = jnp.exp(dtA[:, :, None] * jnp.arange(L))
            K = 2.0 * jnp.einsum('dn,dnl->dl', dC, powers).real
            n = 2 * L
            Kf = jnp.fft.rfft(K, n=n, axis=-1)
            xf = jnp.fft.rfft(x, n=n, axis=1)
            y = jnp.fft.irfft(xf * Kf.T[None], n=n, axis=1)[:, :L]
            return y + x * D_skip
        key = jax.random.key(seed)
        ks = jax.random.split(key, 16)
        s = 0.02
        inp = {'x_text': jax.random.normal(ks[0], (B, T, DT), jnp.float32), 'x_vision': jax.random.normal(ks[1], (B, G, DV), jnp.float32), 'text_mask': jnp.ones((B, T), bool), 'vision_mask': jnp.ones((B, G), bool), 'Wq': jax.random.normal(ks[2], (DT, INNER), jnp.float32) * s, 'Wk': jax.random.normal(ks[3], (DV, INNER), jnp.float32) * s, 'Wv': jax.random.normal(ks[4], (DV, DT), jnp.float32) * s, 'W_film_in': jax.random.normal(ks[5], (DT, 2 * DT), jnp.float32) * s, 'b_film_in': jnp.zeros((2 * DT,), jnp.float32), 'W_film_out': jax.random.normal(ks[6], (DT, 2 * DT), jnp.float32) * s, 'b_film_out': jnp.zeros((2 * DT,), jnp.float32), 'g_norm_in': jnp.ones((DT,), jnp.float32), 'b_norm_in': jnp.zeros((DT,), jnp.float32), 'g_norm_out': jnp.ones((DT,), jnp.float32), 'b_norm_out': jnp.zeros((DT,), jnp.float32), 'g_ffn': jnp.ones((DT,), jnp.float32), 'b_ffn': jnp.zeros((DT,), jnp.float32), 'W1': jax.random.normal(ks[7], (DT, HID), jnp.float32) * s, 'b1': jnp.zeros((HID,), jnp.float32), 'W2': jax.random.normal(ks[8], (HID, DT), jnp.float32) * s, 'b2': jnp.zeros((DT,), jnp.float32), 'log_dt': jnp.log(0.001) + jax.random.uniform(ks[9], (DT,), jnp.float32) * (jnp.log(0.1) - jnp.log(0.001)), 'A_re': -0.5 * jnp.ones((DT, N_STATE), jnp.float32), 'A_im': jnp.tile(jnp.pi * jnp.arange(N_STATE, dtype=jnp.float32), (DT, 1)), 'C_re': jax.random.normal(ks[10], (DT, N_STATE), jnp.float32) * 0.5 ** 0.5, 'C_im': jax.random.normal(ks[11], (DT, N_STATE), jnp.float32) * 0.5 ** 0.5, 'D_skip': jax.random.normal(ks[12], (DT,), jnp.float32), 'mod_gate': jnp.array(0.5, jnp.float32)}
        return inp
    _L1_xattn_all = _L1_xattn_setup()
    _L1_xattn_in = {k: v for k, v in _L1_xattn_all.items() if k in ('Wq', 'Wk', 'Wv', 'W_film_in', 'b_film_in', 'W_film_out', 'b_film_out', 'g_norm_in', 'b_norm_in', 'g_norm_out', 'b_norm_out', 'g_ffn', 'b_ffn', 'W1', 'b1', 'W2', 'b2', 'log_dt', 'A_re', 'A_im', 'C_re', 'C_im', 'D_skip', 'mod_gate')}
    del _L1_xattn_all

    def _L1_ffn_setup():
        import jax, jax.numpy as jnp
        import numpy as np
        HIDDEN = 128
        N_EXPERTS = 8
        TOP_K = 2
        INTER = 176
        N_SHARED = 2
        SCALE = 1.0
        key = jax.random.key(seed)
        ks = jax.random.split(key, 9)
        s_h = 1.0 / np.sqrt(HIDDEN)
        s_i = 1.0 / np.sqrt(INTER)
        x = jax.random.normal(ks[0], (2, 256, HIDDEN), dtype=jnp.float32)
        gate_w = jax.random.uniform(ks[1], (N_EXPERTS, HIDDEN), jnp.float32, -s_h, s_h)
        wg = jax.random.uniform(ks[2], (N_EXPERTS, HIDDEN, INTER), jnp.float32, -s_h, s_h)
        wu = jax.random.uniform(ks[3], (N_EXPERTS, HIDDEN, INTER), jnp.float32, -s_h, s_h)
        wd = jax.random.uniform(ks[4], (N_EXPERTS, INTER, HIDDEN), jnp.float32, -s_i, s_i)
        si = INTER * N_SHARED
        s_si = 1.0 / np.sqrt(si)
        swg = jax.random.uniform(ks[5], (HIDDEN, si), jnp.float32, -s_h, s_h)
        swu = jax.random.uniform(ks[6], (HIDDEN, si), jnp.float32, -s_h, s_h)
        swd = jax.random.uniform(ks[7], (si, HIDDEN), jnp.float32, -s_si, s_si)
        return {'x': x, 'gate_w': gate_w, 'wg': wg, 'wu': wu, 'wd': wd, 'swg': swg, 'swu': swu, 'swd': swd}
    _L1_ffn_all = _L1_ffn_setup()
    _L1_ffn_in = {k: v for k, v in _L1_ffn_all.items() if k in ('gate_w', 'wg', 'wu', 'wd', 'swg', 'swu', 'swd')}
    del _L1_ffn_all
    return {'x': x, 'ctx_768': ctx_768, 'mask_BxS2_bk0': mask_BxS2_bk0, 'mask_BxS_bf1': mask_BxS_bf1, 'mask_BxS2_bf1': mask_BxS2_bf1, 'L0_attn_W_in': _L0_attn_in['W_in'], 'L0_attn_conv_w': _L0_attn_in['conv_w'], 'L0_attn_conv_b': _L0_attn_in['conv_b'], 'L0_attn_W_gates': _L0_attn_in['W_gates'], 'L0_attn_b_gates': _L0_attn_in['b_gates'], 'L0_attn_forget_base': _L0_attn_in['forget_base'], 'L0_attn_W_out': _L0_attn_in['W_out'], 'L0_attn_gamma1': _L0_attn_in['gamma1'], 'L0_attn_gamma2': _L0_attn_in['gamma2'], 'L0_attn_W_grow': _L0_attn_in['W_grow'], 'L0_attn_W_shrink': _L0_attn_in['W_shrink'], 'L0_xattn_W_q': _L0_xattn_in['W_q'], 'L0_xattn_W_k': _L0_xattn_in['W_k'], 'L0_xattn_W_v': _L0_xattn_in['W_v'], 'L0_xattn_W_o': _L0_xattn_in['W_o'], 'L0_xattn_b_o': _L0_xattn_in['b_o'], 'L0_ffn_w_ln1': _L0_ffn_in['w_ln1'], 'L0_ffn_w_ln2': _L0_ffn_in['w_ln2'], 'L0_ffn_W_kvd': _L0_ffn_in['W_kvd'], 'L0_ffn_W_qd': _L0_ffn_in['W_qd'], 'L0_ffn_W_ku': _L0_ffn_in['W_ku'], 'L0_ffn_W_qu': _L0_ffn_in['W_qu'], 'L0_ffn_W_vu': _L0_ffn_in['W_vu'], 'L0_ffn_W_ropeq': _L0_ffn_in['W_ropeq'], 'L0_ffn_W_ropek': _L0_ffn_in['W_ropek'], 'L0_ffn_W_o': _L0_ffn_in['W_o'], 'L0_ffn_Wg_s': _L0_ffn_in['Wg_s'], 'L0_ffn_Wu_s': _L0_ffn_in['Wu_s'], 'L0_ffn_Wd_s': _L0_ffn_in['Wd_s'], 'L0_ffn_Wg_r': _L0_ffn_in['Wg_r'], 'L0_ffn_Wu_r': _L0_ffn_in['Wu_r'], 'L0_ffn_Wd_r': _L0_ffn_in['Wd_r'], 'L0_ffn_W_router': _L0_ffn_in['W_router'], 'L0_ffn_routing_bias': _L0_ffn_in['routing_bias'], 'L1_attn_A': _L1_attn_in['A'], 'L1_attn_Wd': _L1_attn_in['Wd'], 'L1_attn_bd': _L1_attn_in['bd'], 'L1_attn_Wb': _L1_attn_in['Wb'], 'L1_attn_bb': _L1_attn_in['bb'], 'L1_attn_Wc': _L1_attn_in['Wc'], 'L1_attn_bc': _L1_attn_in['bc'], 'L1_xattn_Wq': _L1_xattn_in['Wq'], 'L1_xattn_Wk': _L1_xattn_in['Wk'], 'L1_xattn_Wv': _L1_xattn_in['Wv'], 'L1_xattn_W_film_in': _L1_xattn_in['W_film_in'], 'L1_xattn_b_film_in': _L1_xattn_in['b_film_in'], 'L1_xattn_W_film_out': _L1_xattn_in['W_film_out'], 'L1_xattn_b_film_out': _L1_xattn_in['b_film_out'], 'L1_xattn_g_norm_in': _L1_xattn_in['g_norm_in'], 'L1_xattn_b_norm_in': _L1_xattn_in['b_norm_in'], 'L1_xattn_g_norm_out': _L1_xattn_in['g_norm_out'], 'L1_xattn_b_norm_out': _L1_xattn_in['b_norm_out'], 'L1_xattn_g_ffn': _L1_xattn_in['g_ffn'], 'L1_xattn_b_ffn': _L1_xattn_in['b_ffn'], 'L1_xattn_W1': _L1_xattn_in['W1'], 'L1_xattn_b1': _L1_xattn_in['b1'], 'L1_xattn_W2': _L1_xattn_in['W2'], 'L1_xattn_b2': _L1_xattn_in['b2'], 'L1_xattn_log_dt': _L1_xattn_in['log_dt'], 'L1_xattn_A_re': _L1_xattn_in['A_re'], 'L1_xattn_A_im': _L1_xattn_in['A_im'], 'L1_xattn_C_re': _L1_xattn_in['C_re'], 'L1_xattn_C_im': _L1_xattn_in['C_im'], 'L1_xattn_D_skip': _L1_xattn_in['D_skip'], 'L1_xattn_mod_gate': _L1_xattn_in['mod_gate'], 'L1_ffn_gate_w': _L1_ffn_in['gate_w'], 'L1_ffn_wg': _L1_ffn_in['wg'], 'L1_ffn_wu': _L1_ffn_in['wu'], 'L1_ffn_wd': _L1_ffn_in['wd'], 'L1_ffn_swg': _L1_ffn_in['swg'], 'L1_ffn_swu': _L1_ffn_in['swu'], 'L1_ffn_swd': _L1_ffn_in['swd']}

def reference(x, ctx_768, mask_BxS2_bk0, mask_BxS_bf1, mask_BxS2_bf1, L0_attn_W_in, L0_attn_conv_w, L0_attn_conv_b, L0_attn_W_gates, L0_attn_b_gates, L0_attn_forget_base, L0_attn_W_out, L0_attn_gamma1, L0_attn_gamma2, L0_attn_W_grow, L0_attn_W_shrink, L0_xattn_W_q, L0_xattn_W_k, L0_xattn_W_v, L0_xattn_W_o, L0_xattn_b_o, L0_ffn_w_ln1, L0_ffn_w_ln2, L0_ffn_W_kvd, L0_ffn_W_qd, L0_ffn_W_ku, L0_ffn_W_qu, L0_ffn_W_vu, L0_ffn_W_ropeq, L0_ffn_W_ropek, L0_ffn_W_o, L0_ffn_Wg_s, L0_ffn_Wu_s, L0_ffn_Wd_s, L0_ffn_Wg_r, L0_ffn_Wu_r, L0_ffn_Wd_r, L0_ffn_W_router, L0_ffn_routing_bias, L1_attn_A, L1_attn_Wd, L1_attn_bd, L1_attn_Wb, L1_attn_bb, L1_attn_Wc, L1_attn_bc, L1_xattn_Wq, L1_xattn_Wk, L1_xattn_Wv, L1_xattn_W_film_in, L1_xattn_b_film_in, L1_xattn_W_film_out, L1_xattn_b_film_out, L1_xattn_g_norm_in, L1_xattn_b_norm_in, L1_xattn_g_norm_out, L1_xattn_b_norm_out, L1_xattn_g_ffn, L1_xattn_b_ffn, L1_xattn_W1, L1_xattn_b1, L1_xattn_W2, L1_xattn_b2, L1_xattn_log_dt, L1_xattn_A_re, L1_xattn_A_im, L1_xattn_C_re, L1_xattn_C_im, L1_xattn_D_skip, L1_xattn_mod_gate, L1_ffn_gate_w, L1_ffn_wg, L1_ffn_wu, L1_ffn_wd, L1_ffn_swg, L1_ffn_swu, L1_ffn_swd):
    import jax
    import jax.numpy as jnp

    def _L0_attn_ref(x, W_in, conv_w, conv_b, W_gates, b_gates, forget_base, W_out, gamma1, gamma2, W_grow, W_shrink):
        import jax, jax.numpy as jnp
        import numpy as np
        from jax import lax
        DIM = 128
        EXP = 2
        GMLP_EXP = 2
        K = 4
        HID = DIM * EXP
        GHID = DIM * GMLP_EXP
        ALPHA_LOG_SCALE = -8.0

        def init_forget_gate(size, a=0.001, b=0.1, lo=-9.0, hi=-4.323):
            x = np.log(np.expm1(np.linspace(a, b, size, dtype=np.float64)))
            x = (x - x.min()) / (x.max() - x.min())
            x = x * abs(hi - lo) + lo
            return jnp.asarray(x, dtype=jnp.float32)

        def _rmsnorm(x, gamma):
            n = jnp.sqrt(jnp.sum(x * x, axis=-1, keepdims=True))
            return gamma * jnp.sqrt(jnp.float32(x.shape[-1])) * (x / n)

        def _linear_recurrence(alpha, x):

            def combine(e1, e2):
                a1, b1 = e1
                a2, b2 = e2
                return (a1 * a2, a2 * b1 + b2)
            _, h = lax.associative_scan(combine, (alpha, x), axis=1)
            return h

        def _hawk_block(x, W_in, conv_w, conv_b, W_gates, b_gates, forget_base, W_out, gamma1, gamma2, W_grow, W_shrink):
            B, T, _ = x.shape
            xn = _rmsnorm(x, gamma1)
            z = xn @ W_in.T
            gate, xc = (z[..., :HID], z[..., HID:])
            xc_t = jnp.pad(xc.transpose(0, 2, 1), ((0, 0), (0, 0), (K - 1, 0)))
            xc = lax.conv_general_dilated(xc_t, conv_w, window_strides=(1,), padding='VALID', dimension_numbers=('NCH', 'OIH', 'NCH'), feature_group_count=HID)
            xc = (xc + conv_b[None, :, None]).transpose(0, 2, 1)
            g = xc @ W_gates.T + b_gates
            forget, inp = (g[..., :HID], g[..., HID:])
            alpha = jnp.exp(ALPHA_LOG_SCALE * jax.nn.softplus(forget_base) * jax.nn.sigmoid(forget))
            beta = jnp.sqrt(1.0 - alpha ** 2 + 1e-06)
            xs = beta * jax.nn.sigmoid(inp) * xc
            h = _linear_recurrence(alpha, xs)
            rglru_out = jax.nn.gelu(gate, approximate=False) * h @ W_out.T
            x = x + rglru_out
            xn2 = _rmsnorm(x, gamma2)
            gz = xn2 @ W_grow.T
            mgate, mx = (gz[..., :GHID], gz[..., GHID:])
            mlp_out = jax.nn.gelu(mgate, approximate=False) * mx @ W_shrink.T
            return x + mlp_out
        return _hawk_block(x, W_in, conv_w, conv_b, W_gates, b_gates, forget_base, W_out, gamma1, gamma2, W_grow, W_shrink)

    def _L0_xattn_ref(x, context, mask, W_q, W_k, W_v, W_o, b_o):
        import jax, jax.numpy as jnp
        import numpy as np
        HEADS = 8
        DIM_HEAD = 64
        QUERY_DIM = 128
        CONTEXT_DIM = 96
        INNER = HEADS * DIM_HEAD
        b, n, _ = x.shape
        j = context.shape[1]
        scale = DIM_HEAD ** (-0.5)
        q = (x @ W_q).reshape(b, n, HEADS, DIM_HEAD)
        k = (context @ W_k).reshape(b, j, HEADS, DIM_HEAD)
        v = (context @ W_v).reshape(b, j, HEADS, DIM_HEAD)
        sim = jnp.einsum('bihd,bjhd->bhij', q, k) * scale
        max_neg = -jnp.finfo(sim.dtype).max
        sim = jnp.where(mask[:, None, None, :], sim, max_neg)
        attn = jax.nn.softmax(sim, axis=-1)
        out = jnp.einsum('bhij,bjhd->bihd', attn, v).reshape(b, n, INNER)
        return out @ W_o + b_o

    def _L0_ffn_ref(x, w_ln1, w_ln2, W_kvd, W_qd, W_ku, W_qu, W_vu, W_ropeq, W_ropek, W_o, Wg_s, Wu_s, Wd_s, Wg_r, Wu_r, Wd_r, W_router, routing_bias):
        import jax, jax.numpy as jnp
        import numpy as np
        H = 128
        NH = 16
        HD = H // NH
        HH = HD // 2
        L = H // 4
        I = int(H * 1.0)
        ER = 7
        TOPK = 2
        BASE = 10000.0
        EPS = 1e-05

        def rmsnorm(x, w):
            norm = jnp.sqrt(jnp.mean(x * x, axis=-1, keepdims=True)) + EPS
            return x / norm * w

        def rope_tables(seq_len):
            inv_freq = 1.0 / BASE ** (jnp.arange(0, HH, 2, dtype=jnp.float32) / HH)
            t = jnp.arange(seq_len, dtype=jnp.float32)
            freqs = jnp.einsum('i,j->ij', t, inv_freq)
            emb = jnp.concatenate([freqs, freqs], axis=-1)
            cos = jnp.cos(emb)[None, :, None, :]
            sin = jnp.sin(emb)[None, :, None, :]
            return (cos, sin)

        def rotate_half(x):
            x1, x2 = jnp.split(x, 2, axis=-1)
            return jnp.concatenate([-x2, x1], axis=-1)

        def silu(x):
            return x * jax.nn.sigmoid(x)

        def mla(xn, W_kvd, W_qd, W_ku, W_qu, W_vu, W_ropeq, W_ropek, W_o):
            B, S, _ = xn.shape
            kv_lat = xn @ W_kvd
            q_lat = xn @ W_qd
            k = (kv_lat @ W_ku).reshape(B, S, NH, HH)
            q = (q_lat @ W_qu).reshape(B, S, NH, HH)
            v = (kv_lat @ W_vu).reshape(B, S, NH, HD)
            q_rope = (q_lat @ W_ropeq).reshape(B, S, NH, HH)
            k_rope = (xn @ W_ropek).reshape(B, S, NH, HH)
            cos, sin = rope_tables(S)
            k_rope = k_rope * cos + rotate_half(k_rope) * sin
            q_rope = q_rope * cos + rotate_half(q_rope) * sin
            kk = jnp.concatenate([k, k_rope], axis=-1)
            qq = jnp.concatenate([q, q_rope], axis=-1)
            scale = 1.0 / jnp.sqrt(jnp.float32(HD))
            scores = jnp.einsum('bqhd,bkhd->bhqk', qq, kk) * scale
            causal = jnp.tril(jnp.ones((S, S), dtype=bool))
            scores = jnp.where(causal[None, None], scores, jnp.finfo(scores.dtype).min)
            probs = jax.nn.softmax(scores, axis=-1)
            y = jnp.einsum('bhqk,bkhd->bqhd', probs, v).reshape(B, S, H)
            return y @ W_o

        def moe(xn, Wg_s, Wu_s, Wd_s, Wg_r, Wu_r, Wd_r, W_router, routing_bias):
            B, S, _ = xn.shape
            xt = xn.reshape(B * S, H)
            shared = silu(xt @ Wg_s) * (xt @ Wu_s) @ Wd_s
            logits = xt @ W_router + routing_bias
            probs = jax.nn.sigmoid(logits)
            scores, idx = jax.lax.top_k(probs, TOPK)
            scores = scores / jnp.sum(scores, axis=-1, keepdims=True)
            wts = jnp.sum(jax.nn.one_hot(idx, ER, dtype=xt.dtype) * scores[..., None], axis=1)
            g = jnp.einsum('th,ehi->tei', xt, Wg_r)
            u = jnp.einsum('th,ehi->tei', xt, Wu_r)
            hmid = silu(g) * u
            combined = jnp.einsum('tei,eih,te->th', hmid, Wd_r, wts)
            return (shared + combined).reshape(B, S, H)
        x = x + mla(rmsnorm(x, w_ln1), W_kvd, W_qd, W_ku, W_qu, W_vu, W_ropeq, W_ropek, W_o)
        x = x + moe(rmsnorm(x, w_ln2), Wg_s, Wu_s, Wd_s, Wg_r, Wu_r, Wd_r, W_router, routing_bias)
        return x

    def _L1_attn_ref(x, A, Wd, bd, Wb, bb, Wc, bc):
        import jax, jax.numpy as jnp
        import numpy as np
        D_MODEL = 128
        D_STATE = 16
        delta = jax.nn.softplus(jnp.einsum('bld,ed->ble', x, Wd) + bd)
        Bmat = jnp.einsum('bld,nd->bln', x, Wb) + bb
        Cmat = jnp.einsum('bld,nd->bln', x, Wc) + bc
        A_bar = jnp.exp(delta[..., None] * A)
        Bx = (delta * x)[..., None] * Bmat[:, :, None, :]
        h0 = jnp.zeros((x.shape[0], x.shape[2], A.shape[1]), x.dtype)

        def step(h, inp):
            a_t, bx_t, c_t = inp
            h = a_t * h + bx_t
            y = jnp.einsum('bdn,bn->bd', h, c_t)
            return (h, y)
        xs = (jnp.swapaxes(A_bar, 0, 1), jnp.swapaxes(Bx, 0, 1), jnp.swapaxes(Cmat, 0, 1))
        _, ys = jax.lax.scan(step, h0, xs)
        return jnp.swapaxes(ys, 0, 1)

    def _L1_xattn_ref(x_text, x_vision, text_mask, vision_mask, Wq, Wk, Wv, W_film_in, b_film_in, W_film_out, b_film_out, g_norm_in, b_norm_in, g_norm_out, b_norm_out, g_ffn, b_ffn, W1, b1, W2, b2, log_dt, A_re, A_im, C_re, C_im, D_skip, mod_gate):
        import jax, jax.numpy as jnp
        import numpy as np
        B, T, DT, G, DV = (16, 64, 128, 72, 96)
        H, DH = (4, 32)
        INNER = H * DH
        HID = 4 * DT
        N_STATE = 64
        K_TOP = 32

        def layernorm(x, g, b, eps=1e-05):
            m = x.mean(-1, keepdims=True)
            v = x.var(-1, keepdims=True)
            return (x - m) * jax.lax.rsqrt(v + eps) * g + b

        def s4d(x, log_dt, A_re, A_im, C_re, C_im, D_skip):
            Bb, L, D = x.shape
            dt = jnp.exp(log_dt)
            A = A_re + 1j * A_im
            C = C_re + 1j * C_im
            dtA = dt[:, None] * A
            dC = C * (jnp.exp(dtA) - 1.0) / A
            powers = jnp.exp(dtA[:, :, None] * jnp.arange(L))
            K = 2.0 * jnp.einsum('dn,dnl->dl', dC, powers).real
            n = 2 * L
            Kf = jnp.fft.rfft(K, n=n, axis=-1)
            xf = jnp.fft.rfft(x, n=n, axis=1)
            y = jnp.fft.irfft(xf * Kf.T[None], n=n, axis=1)[:, :L]
            return y + x * D_skip
        Bb, Tt, D = x_text.shape
        Gg = x_vision.shape[1]
        Q = (x_text @ Wq).reshape(Bb, Tt, H, DH)
        K = (x_vision @ Wk).reshape(Bb, Gg, H, DH)
        scores = jnp.einsum('bthd,bghd->bhtg', Q, K) / np.sqrt(DH).astype(np.float32)
        scores = jnp.where(vision_mask[:, None, None, :], scores, -jnp.inf)
        topv, topi = jax.lax.top_k(scores, K_TOP)
        probs = jax.nn.softmax(topv, axis=-1)
        bi = jnp.arange(Bb)[:, None, None, None]
        hi = jnp.arange(H)[None, :, None, None]
        ti = jnp.arange(Tt)[None, None, :, None]
        attn = jnp.zeros_like(scores).at[bi, hi, ti, topi].set(probs)
        attn_mean = attn.mean(axis=1)
        V = x_vision @ Wv
        c_t = jnp.einsum('btg,bgd->btd', attn_mean, V)
        c_t = c_t * text_mask[..., None]
        x = layernorm(x_text, g_norm_in, b_norm_in)
        scale_in, shift_in = jnp.split(c_t @ W_film_in + b_film_in, 2, axis=-1)
        x = x * (1.0 + mod_gate * scale_in) + mod_gate * shift_in
        y = s4d(x, log_dt, A_re, A_im, C_re, C_im, D_skip)
        scale_out, shift_out = jnp.split(c_t @ W_film_out + b_film_out, 2, axis=-1)
        y = y * (1.0 + mod_gate * scale_out) + mod_gate * shift_out
        xt = x_text + y
        h = layernorm(xt, g_ffn, b_ffn)
        h = jax.nn.gelu(h @ W1 + b1, approximate=False) @ W2 + b2
        xt = xt + h
        return layernorm(xt, g_norm_out, b_norm_out)

    def _L1_ffn_ref(x, gate_w, wg, wu, wd, swg, swu, swd):
        import jax, jax.numpy as jnp
        import numpy as np
        HIDDEN = 128
        N_EXPERTS = 8
        TOP_K = 2
        INTER = 176
        N_SHARED = 2
        SCALE = 1.0
        B, S, H = x.shape
        xf = x.reshape(-1, H)
        T = xf.shape[0]
        logits = xf.astype(jnp.float32) @ gate_w.astype(jnp.float32).T
        scores = jax.nn.softmax(logits, axis=-1)
        topw, topi = jax.lax.top_k(scores, TOP_K)
        denom = topw.sum(axis=-1, keepdims=True) + 1e-20
        topw = topw / denom * SCALE
        wdense = jnp.zeros((T, N_EXPERTS), jnp.float32).at[jnp.arange(T)[:, None], topi].set(topw)
        hg = jnp.einsum('th,ehi->eti', xf, wg)
        hu = jnp.einsum('th,ehi->eti', xf, wu)
        eo = jnp.einsum('eti,eih->eth', jax.nn.silu(hg) * hu, wd)
        y = jnp.einsum('te,eth->th', wdense, eo)
        shared = jax.nn.silu(xf @ swg) * (xf @ swu) @ swd
        return (y + shared).reshape(B, S, H)
    x = _layernorm(x + _L0_attn_ref(x, L0_attn_W_in, L0_attn_conv_w, L0_attn_conv_b, L0_attn_W_gates, L0_attn_b_gates, L0_attn_forget_base, L0_attn_W_out, L0_attn_gamma1, L0_attn_gamma2, L0_attn_W_grow, L0_attn_W_shrink), axis=-1)
    x = _layernorm(x + _L0_xattn_ref(x, ctx_768, mask_BxS2_bk0, L0_xattn_W_q, L0_xattn_W_k, L0_xattn_W_v, L0_xattn_W_o, L0_xattn_b_o), axis=-1)
    x = _layernorm(x + _L0_ffn_ref(x, L0_ffn_w_ln1, L0_ffn_w_ln2, L0_ffn_W_kvd, L0_ffn_W_qd, L0_ffn_W_ku, L0_ffn_W_qu, L0_ffn_W_vu, L0_ffn_W_ropeq, L0_ffn_W_ropek, L0_ffn_W_o, L0_ffn_Wg_s, L0_ffn_Wu_s, L0_ffn_Wd_s, L0_ffn_Wg_r, L0_ffn_Wu_r, L0_ffn_Wd_r, L0_ffn_W_router, L0_ffn_routing_bias), axis=-1)
    x = _layernorm(x + _L1_attn_ref(x, L1_attn_A, L1_attn_Wd, L1_attn_bd, L1_attn_Wb, L1_attn_bb, L1_attn_Wc, L1_attn_bc), axis=-1)
    x = _layernorm(x + _L1_xattn_ref(x, ctx_768, mask_BxS_bf1, mask_BxS2_bf1, L1_xattn_Wq, L1_xattn_Wk, L1_xattn_Wv, L1_xattn_W_film_in, L1_xattn_b_film_in, L1_xattn_W_film_out, L1_xattn_b_film_out, L1_xattn_g_norm_in, L1_xattn_b_norm_in, L1_xattn_g_norm_out, L1_xattn_b_norm_out, L1_xattn_g_ffn, L1_xattn_b_ffn, L1_xattn_W1, L1_xattn_b1, L1_xattn_W2, L1_xattn_b2, L1_xattn_log_dt, L1_xattn_A_re, L1_xattn_A_im, L1_xattn_C_re, L1_xattn_C_im, L1_xattn_D_skip, L1_xattn_mod_gate), axis=-1)
    x = _layernorm(x + _L1_ffn_ref(x, L1_ffn_gate_w, L1_ffn_wg, L1_ffn_wu, L1_ffn_wd, L1_ffn_swg, L1_ffn_swu, L1_ffn_swd), axis=-1)
    return x

_drawn_inputs = setup_inputs


def setup_inputs(seed=0):
    import zlib

    import numpy as np

    out = dict(_drawn_inputs(seed))
    spreads = {'L0_attn_conv_b': (0.0, 0.1),
     'L0_attn_b_gates': (0.0, 0.444),
     'L0_attn_gamma1': (1.0, 0.2),
     'L0_attn_gamma2': (1.0, 0.2),
     'L0_ffn_w_ln1': (1.0, 0.6),
     'L0_ffn_w_ln2': (1.0, 0.6),
     'L0_ffn_routing_bias': (0.0, 0.8),
     'L1_xattn_b_film_in': (0.0, 0.1),
     'L1_xattn_b_film_out': (0.0, 0.1),
     'L1_xattn_g_norm_in': (1.0, 0.2),
     'L1_xattn_b_norm_in': (0.0, 0.1),
     'L1_xattn_g_norm_out': (1.0, 0.2),
     'L1_xattn_b_norm_out': (0.0, 0.1),
     'L1_xattn_g_ffn': (1.0, 0.6),
     'L1_xattn_b_ffn': (0.0, 2.0),
     'L1_xattn_b1': (0.0, 0.768),
     'L1_xattn_b2': (0.0, 0.1),
     'L1_xattn_A_re': (-0.5, 0.2)}
    factors = {'L0_ffn_W_kvd': 8.0,
     'L0_ffn_W_qd': 8.0,
     'L0_ffn_W_ku': 8.0,
     'L0_ffn_W_qu': 8.0,
     'L0_ffn_W_vu': 8.0,
     'L0_ffn_W_ropeq': 8.0,
     'L0_ffn_W_ropek': 8.0,
     'L0_ffn_W_o': 8.0,
     'L0_ffn_Wg_s': 8.0,
     'L0_ffn_Wu_s': 8.0,
     'L0_ffn_Wd_s': 8.0,
     'L0_ffn_Wg_r': 8.0,
     'L0_ffn_Wu_r': 8.0,
     'L0_ffn_Wd_r': 8.0,
     'L0_ffn_W_router': 8.0,
     'L1_attn_bd': 2.767,
     'L1_xattn_Wq': 8.0,
     'L1_xattn_Wk': 8.0,
     'L1_xattn_Wv': 3.843,
     'L1_xattn_W_film_in': 4.554,
     'L1_xattn_W_film_out': 6.889}
    for name, (base, spread) in spreads.items():
        noise = np.random.default_rng([zlib.crc32(name.encode()), seed]).standard_normal(out[name].shape)
        drawn = base * np.exp(spread * noise) if base else spread * noise
        out[name] = jnp.asarray(drawn.astype(out[name].dtype))
    for name, factor in factors.items():
        out[name] = (out[name] * factor).astype(out[name].dtype)
    return out
```

```python
import math
from contextlib import ExitStack

import concourse.bass as bass
import numpy as np
from concourse import mybir

F32 = mybir.dt.float32
BF16 = mybir.dt.bfloat16
U8 = mybir.dt.uint8
U32 = mybir.dt.uint32
ALU = mybir.AluOpType
ACT = mybir.ActivationFunctionType
X = mybir.AxisListType.X

B, T, D = 2, 512, 128
NT = T // 128
J = 32
CD = 96
H0, H1 = 8, 4
NH, HD = 16, 8
GH = 8
E0, E1 = 7, 8
U0 = E0 + 1
I1 = 176
R1 = E1 * I1
N1 = R1 + 2 * I1
UB1 = -(-N1 // 128)
RB1 = R1 // 128
NS = 16
PA, PB_ = 16, 32
NF = 512
NFB = NF // 128
BIG = 2.0 ** 100
TWO_PI = 6.2831845
ROUND = 1.5 * 2.0 ** 23
C6 = 6
KROWS = C6 * HD + 3


def _ln(t):
    return [f"{t}.sq", f"{t}.l", f"{t}.r"]


_U = list(range(U0))
_N = list(range(NS))
_K = list(range(UB1))
_HP = list(range(NH // 2))
_ATT_PE = [x for h in range(NH // 2) for x in
           [f"st{h}.X", f"st{h}.Y", f"st{h}.Z"] + ([f"vp{h - 1}"] if h else [])] + [f"vp{NH // 2 - 1}"]
STEPS = {
    "pe": [
        "h1.ss", "z0", "z1", "z2", "z3", "g0", "g1", "g2", "g3", "rg", "h4.ss", "gr0", "gr1", "gr2", "gr3", "shr",
        "ln1.c", "ln1.v", "xa.s0", "xa.s1", "xa.t0", "xa.t1", "xa.o", "ln2.c", "ln2.v",
        "m1.ss", "lat", "kf", "q0", "q1", "v",
        *[f"mx{h}.{u}" for h in _HP for u in "ABCDE"], "nmt",
        *_ATT_PE, "yt", "mo",
        "f1.ss", "rt", "wt", *[f"{n}{u}" for u in range(U0 + 1) for n in ("fg", "fu", "fw", "fd")
                               if not (u == 0 and n == "fd") and not (u == U0 and n != "fd")
                               and not (u == U0 - 1 and n == "fw")],
        "ln3.c", "ln3.v", "bc", "de", *[f"{n}{i}" for i in range(NS + 1) for n in ("bn", "cn", "yn")
                                        if not (i == 0 and n == "yn") and not (i == NS and n != "yn")],
        "ln4.c", "ln4.v", "xb.s", "xb.t", "fl0", "fl1", "fl2", "fl3", "lni.c", "lni.v", "xit",
        "inv", "lnf.c", "lnf.v", "w10", "w11", "w12", "w13", "w2", "lno.c", "lno.v", "ln5.c", "ln5.v",
        "rt1", "wt1", *[f"{n}{k}" for k in range(UB1 + 1) for n in ("eg", "eu", "ew", "ed")
                        if not (k == 0 and n == "ed") and not (k == UB1 and n != "ed")
                        and not (k >= RB1 and n == "ew")],
        "ln6.c", "ln6.v"],
    "act": [
        "h1.sq", "h1.l", "h1.r", "cv0", "cv1", "gg0", "gg1", "tf0", "tf1", "ti0", "ti1",
        "al0", "al1", "sa0", "sa1", "lb0", "lb1", "hb0", "hb1", "h4.sq", "h4.l", "h4.r", "gm0", "gm1", *_ln("ln1"),
        "xa.e0", "xa.e1", "xa.a0", "xa.a1", *_ln("ln2"), "m1.sq", "m1.l", "m1.n", "m1.m", "m1.r", "lat",
        "kh", "km", "qh", "qm", "v", "nmt", *[f"st{h}.{u}" for h in _HP for u in "XYZ"], "yt",
        "f1.sq", "f1.l", "f1.n", "f1.m", "f1.r", "rt", "wt", *[f"sl{u}" for u in _U], *_ln("ln3"),
        "bc", "ab", "ex", "sp", *[f"{n}{i}" for i in _N for n in ("aa", "bb")], *_ln("ln4"),
        "xb.e", "xb.a", "s0", "s1", "s2", "s3", *_ln("lni"), "lni.g", "xit", *_ln("lnf"), "lnf.g",
        "u0", "u1", "u2", "u3", *_ln("lno"), "lno.g", *_ln("ln5"), "rt1", "wt1", *[f"el{k}" for k in _K],
        *_ln("ln6")],
    "dve": [
        "xn1", "cw0.2", "cw1.2", "cw0.1", "cw1.1", "cw0.0", "cw1.0", "in0", "in1", "xs0", "xs1", "h0", "h1",
        "gh0", "gh1", "x1", "xx", "xn2", "hm0", "hm1", "s1", "X1",
        "xa.m0", "xa.d0", "xa.m1", "xa.d1", "xa.u0", "xa.i0", "xa.p0", "xa.u1", "xa.i1", "xa.p1", "s2", "X2",
        "xm", "k1", "k2", "kk", "kr", "kl", "q1", "q2", "qq", "qr", "ql",
        *[f"mx{h}.{u}" for h in _HP for u in "ABCDE"], "nh", "nr", "nm", "nl",
        *[f"{n}{g}" for g in range(NH // GH) for n in ("ri", "y")], "x2a", "x2x",
        "xf", "lg", "pd", "pr", "gt", "ge", "gx", "gm", "rk", "we", "ws", "wi", "wn", "wh", "wr", "wm", "wl",
        *[f"{n}{u}" for u in _U for n in ("hu", "hw") if not (u == U0 - 1 and n == "hw")], "s3", "X3",
        "bh", "br", "bm", "bs", "bl", "rl", *[f"{n}{i}" for i in _N for n in ("sc", "hc")], "s4", "X4",
        "xb.m", "xb.d", "xb.u", "xb.i", "xb.k", "xb.p", "lni.x", "sk", "fo", "fp", "xt",
        "lnf.x", "xt2", "lno.x", "s5", "X5",
        "mx", "ms", "su", "iv", "pr1", "gt1", "ge1", "gx1", "gm1", "rk1", "we1", "ws1", "wa1", "wi1", "wn1",
        "wh1", "wr1", "wm1", "wl1",
        *[f"{n}{k}" for k in _K for n in ("eu", "ew") if not (k >= RB1 and n == "ew")], "s6", "X6"],
    "pool": ["dl", "dx", *[f"by{i}" for i in _N], "lni.z", "xin"],
}
_HALF = (0, 1)
STEPS_W = {
    "pe": ["kv", "m0", "v0", "k1", "m1", "f0", "f1", *[f"kp{c}" for c in range(8)], "kt", "kf0", "kf1",
           *[f"xf{c}{i}" for c in _HALF for i in _HALF]],
    "act": ["fb.a", "fb.e", "fb.l", "kv0", "kv", "v0", "k1", "vr", "dt", "th", "sh", "sy",
            *[f"{n}{c}" for c in _HALF for n in ("eQ", "eP", "sQ", "s1", "s2")], *[f"kp{c}" for c in range(8)],
            "kl", "kf0", "kf1"],
    "dve": ["km", "kb0", "kb1", "tm", "m0a", "m0b", "m1", "VF0", "VF1", *[f"dc{i}" for i in range(1, 27)],
            *[f"{n}{c}" for c in _HALF for n in ("rr", "ii", "ri", "ir", "yr", "yi")]],
    "pool": ["va0", "va1", "fb.r", "fb.s", "fb.c", "bh", "bf", "bf1", "zr", "zi", "u",
             "u2", "ka", "kb", "kc", "kd", "ke", "kf",
             *[f"{n}{c}" for c in _HALF for n in ("tQ", "aQ", "tP", "aP", "kQ", "mQ", "gQ", "k1", "n1", "g1",
                                                   "k2", "n2", "g2", "Q", "T1", "T2", "U1", "U2", "P")]],
}


def layouts():
    groups = {
        "vec": [("g1", 1), ("g2", 1), ("cw", 8), ("cb", 2), ("bg", 4), ("fb", 2), ("bo", 1), ("wl1", 1), ("wl2", 1),
                ("A", NS), ("bd", 1), ("bBC", 1), ("gni", 1), ("bni", 1), ("gff", 1), ("bff", 1), ("gno", 1),
                ("bno", 1), ("b1", 4), ("b2", 1), ("bfi", 4), ("Ds", 1), ("mg", 1), ("eps", 1), ("q25", 1),
                ("one", 1), ("phq", 1), ("ph1", 1), ("ph2", 1), ("rb", NT * E0), ("tri0", E0 * E0),
                ("tri1", E1 * E1)],
        "hawk": [("Win", 512), ("Wga", 1024), ("Wou", 256), ("Wgr", 512), ("Wsh", 256)],
        "xa0": [("Wk", 512), ("Wv", 512), ("WqT", 512), ("Wo", 512), ("ctx", B * J)],
        "sq": [("Cm", 128), ("ones", 128), ("id", 128)],
        "mla": [("lat", 64), ("kx", 128), ("kr", 128), ("ks", 128), ("q", 128), ("qs", 128), ("v", 128), ("o", 128),
                ("COSk", T), ("SINk", T), ("COSq", T), ("SINq", T)],
        "moe0": [("g", 128 * U0), ("u", 128 * U0), ("d", 128 * U0), ("r", E0)],
        "late": [("Wd", 128), ("WBC", 96), ("WqT", 128), ("Wk", 128), ("Wv", 128), ("film", 512), ("W1", 512),
                 ("W2", 512), ("gate", E1)],
        "s4d": [("Are", 128), ("Aim", 128), ("Cre", 128), ("Cim", 128), ("ldt", 128), ("lb", PB_), ("la", PA)],
        "dft": [("F", NT * 2 * NF), ("G", 2 * NF // 128 * T)],
        "ffn1": [("g", 128 * UB1), ("u", 128 * UB1), ("d", 128 * UB1)],
        "bf": [("id", 128), ("mS", 128), ("mT", 128), ("one", 128)],
        "sel0": [("s", 128 * E0)],
        "selA": [("s", 128 * 2 * NS)],
        "sel1": [("s", 128 * RB1)],
    }
    out = {}
    for g, items in groups.items():
        at, d = 0, {}
        for name, n in items:
            d[name] = (at, n)
            at += n
        out[g] = (d, at)
    return out


BF_GROUPS = ("bf", "sel0", "selA", "sel1")


def build(nc, dram, out):
    lay = layouts()
    with ExitStack() as ctx:
        def sb(name, shape, dt=F32):
            return ctx.enter_context(nc.sbuf_tensor(name, shape, dt))

        lanes = (0, 1, "w")
        sems = {(e, l): ctx.enter_context(nc.semaphore(f"{e}_steps_{l}")) for e in STEPS for l in lanes}
        order = {(e, l): (STEPS_W if l == "w" else STEPS)[e] for e in STEPS for l in lanes}
        place = {k: {n: i + 1 for i, n in enumerate(v)} for k, v in order.items()}
        for k, v in order.items():
            assert len(place[k]) == len(v), k
        said = {k: 0 for k in order}

        def done(engine, lane, name):
            k = (engine, lane)
            assert place[k][name] == said[k] + 1, (k, name, "expected", order[k][said[k]])
            said[k] += 1
            return sems[k], 1

        def after(engine, lane, name):
            return sems[engine, lane], place[engine, lane][name]

        loads = {n: ctx.enter_context(nc.semaphore(f"load_{n}")) for n in
                 ["x0", "x1", "vec", "hawk", "xa0", "sq", "mla", "moe0", "late", "s4d", "dft", "ffn1", "bf", "sel0",
                  "selA", "sel1", "km", "kr", "tm"]}
        stack = {(w, b): ctx.enter_context(nc.semaphore(f"stack_{w}{b}")) for w in "kqm" for b in range(B)}
        kshuf = ctx.enter_context(nc.semaphore("kernel_rows_moved"))
        stored = ctx.enter_context(nc.semaphore("stored"))

        PS = ctx.enter_context(nc.psum_tensor("PS", [128, 8, T], F32))
        RA = sb("RA", [128, lay["hawk"][1] + lay["xa0"][1]])
        RR = sb("RR", [128, 16384])
        SL = 16
        AR = [sb(f"AR{b}", [128, SL, T]) for b in range(B)]

        def flat(b, i, j):
            return AR[b][:, i:j, :].rearrange("p a t -> p (a t)")

        tiles = {}
        for g, (d, n) in lay.items():
            if g == "hawk":
                tiles[g] = RA[:, 0:n]
            elif g == "xa0":
                tiles[g] = RA[:, lay["hawk"][1]:lay["hawk"][1] + n]
            elif g == "moe0":
                tiles[g] = RA[:, 0:n]
            elif g == "sel0":
                at = lay["moe0"][1] + 1
                tiles[g] = RA[:, at:at + n // 2]
            elif g == "dft":
                tiles[g] = RR[:, 0:n]
            elif g == "ffn1":
                tiles[g] = RR[:, 8192:8192 + n]
            elif g == "selA":
                tiles[g] = RR[:, 13600:13600 + n // 2]
            elif g == "sel1":
                tiles[g] = RR[:, 15648:15648 + n // 2]
            elif g == "s4d":
                tiles[g] = flat(1, 14, 16)[:, 0:n]
            else:
                tiles[g] = sb(f"W_{g}", [128, n // (2 if g in BF_GROUPS else 1)])[:, :]

        def w(group, name, a=0, n=None):
            c, full = lay[group][0][name]
            t = tiles[group].bitcast(BF16) if group in BF_GROUPS else tiles[group]
            return t[:, c + a:c + a + (full if n is None else n)]

        def vec(name, i=0):
            return w("vec", name, i, 1)

        Xin = [sb(f"x_in{b}", [128, T]) for b in range(B)]
        kmask_w, krow_w, tmask_w = (sb("kmask", [128, B * H0 * J // 4], U32), sb("krow", [1, B * (H0 + H1) * J // 4], U32),
                                    sb("tmask", [128, B * NT // 4], U32))
        kmask, krow, tmask = (m[:, :].bitcast(U8) for m in (kmask_w, krow_w, tmask_w))
        tmaskf = sb("tmaskf", [128, B * NT])
        krowb = sb("krowb", [1, B * (H0 + H1) * J], BF16)
        pre = flat(0, 11, 14)
        kmaskf, KTs, VTs, K1s, Vrep = (pre[:, 0:512], pre[:, 512:768], pre[:, 768:1024], pre[:, 1024:1088],
                                       pre[:, 1088:1344])
        M0 = sb("M0", [128, B, H0 * J])
        V0 = sb("V0", [128, B, 2, 128])
        M1 = sb("M1", [128, B, H1 * J])
        VF = sb("VF", [128, B, 512])
        small = sb("small", [128, 64])
        fcoef, bhalf, bfilm = small[:, 0:2], small[:, 2:6], small[:, 6:10]
        fb_r, fb_a, fb_e, fb_l = small[:, 10:12], small[:, 12:14], small[:, 14:16], small[:, 16:18]
        st = [sb(f"stats{b}", [128, 1024]) for b in range(B)]
        spb = [sb(f"parts{b}", [128, NT, 48], BF16) for b in range(B)]
        wT = [sb(f"wT{b}", [48, T], BF16) for b in range(B)]
        Vaug = [sb(f"Vaug{b}", [128, NT, NH, HD + 1]) for b in range(B)]
        KL = sb("KL", [128, NT, 128])
        Kf = sb("Kf", [128, 2, NFB, 128])

        QT = RR[:, 0:4096].rearrange("p (d l) -> p d l", l=PB_)
        PT = RR[:, 4096:6144].rearrange("p (d l) -> p d l", l=PA)
        Ksb = RR[0:PA, 6144:10240]
        Kdl = RR[:, 10240:10752]

        KV = [[RR[:, (2 * b + i) * 4096:(2 * b + i + 1) * 4096].bitcast(BF16).rearrange("p (h t) -> p h t", h=NH)
               for b in range(B)] for i in range(2)]
        Kst, Qst = KV
        P = [flat(s_, 11, 16) for s_ in range(2)]
        XT = flat(0, 11, 13).rearrange("p (j b d) -> p j b d", j=NT, b=B)
        Yf = flat(1, 11, 15).rearrange("p (c f n) -> p c f n", c=2, f=NFB)
        Zt = flat(0, 13, 15).rearrange("p (c n) -> p c n", c=2)

        def A(b, i):
            return AR[b][:, i, :]

        def S(b, c, n):
            return st[b][:, c:c + n]

        def dct(i):
            return flat(1, 11, 14)[:, 128 * i:128 * i + 128]

        def tb(name):
            at, l = {"tQ": (6144, PB_), "gQ": (8192, PB_), "eQ": (10240, PB_),
                     "tP": (12288, PA), "g1": (13312, PA), "g2": (14336, PA), "eP": (15360, PA)}[name]
            return RR[:, at:at + 64 * l].rearrange("p (d l) -> p d l", l=l)

        def bank(i):
            return PS[:, i, :]

        def own(b, i):
            return PS[:, 4 * b + i, :]

        def grid(ap, k):
            return ap.rearrange("p (a k) -> p a k", k=k)

        def over(ap, shape, at):
            return ap.unsqueeze(at).to_broadcast(shape)

        half = [[flat(b, 8, 11)[:, 256 * i:256 * i + 256].bitcast(BF16) for i in range(6)] for b in range(B)]
        KP = [half[b][0:3] for b in range(B)]
        QP = [half[b][3:6] for b in range(B)]

        block = ctx.enter_context(nc.Block())

        @block.sync
        def _(sp):
            def load(name, dst, src=None):
                sp.dma_start(dst, dram[name] if src is None else src).then_inc(loads[name], 16)

            load("x0", Xin[0][:, :], dram["x"][:, 0:T])
            load("vec", tiles["vec"])
            load("sq", tiles["sq"])
            load("hawk", tiles["hawk"])
            load("x1", Xin[1][:, :], dram["x"][:, T:2 * T])
            load("s4d", tiles["s4d"])
            load("km", kmask_w[:, :])
            load("kr", krow_w[:, :])
            load("tm", tmask_w[:, :])
            load("xa0", tiles["xa0"])
            load("late", tiles["late"])
            load("bf", tiles["bf"])
            load("mla", tiles["mla"])

            def parts(which, b):
                dst, hi, mid, lo, rows = {
                    "k": (Kst[b], KP[b][0], KP[b][1], KP[b][2], "hmhlhm"),
                    "q": (Qst[b], QP[b][0], QP[b][1], QP[b][2], "hhmhlm")}[which]
                for c, part in enumerate(rows):
                    src = {"h": hi, "m": mid, "l": lo}[part]
                    sp.dma_start(dst[c * HD:(c + 1) * HD, :, :], src).then_inc(stack[which, b], 16)

            sp.wait_ge(*after("act", "w", "kp7"))
            for a in range(PA):
                sp.dma_start(Kdl[:, PB_ * a:PB_ * a + PB_], Ksb[a:a + 1, :].rearrange("p (d l) -> p d l", l=PB_))\
                    .then_inc(kshuf, 16)
            for b in range(B):
                sp.wait_ge(*after("pe", "w", "kt"))
                if b == 0:
                    for q in range(B):
                        sp.dma_start(RR[C6 * HD:KROWS, 8192 * q:8192 * q + 4096], dram["ones"])\
                            .then_inc(stack["k", q], 16)
                sp.wait_ge(*after("dve", b, "kl"))
                parts("k", b)
                sp.wait_ge(*after("dve", b, "ql"))
                parts("q", b)
            for b in range(B):
                sp.wait_ge(*after("pe", b, "xa.o"))
            load("moe0", tiles["moe0"])
            load("sel0", tiles["sel0"])
            for b in range(B):
                sp.wait_ge(*after("act", b, "nmt"))
                sp.dma_start(Qst[b][C6 * HD:KROWS, :, :], wT[b][:, :]).then_inc(stack["m", b], 16)
            for b in range(B):
                sp.wait_ge(*after("pe", b, f"st{NH // 2 - 1}.Z"))
            load("selA", tiles["selA"])
            load("dft", tiles["dft"])
            load("ffn1", tiles["ffn1"])
            load("sel1", tiles["sel1"])
            for b in range(B):
                sp.wait_ge(*after("dve", b, "X6"))
                sp.dma_start(out[:, b * T:(b + 1) * T], Xin[b][:, :]).then_inc(stored, 16)
            sp.wait_ge(stored, 16 * B)

        @block.tensor
        def _(pe):
            mm, tr = nc.tensor.matmul, nc.tensor.transpose

            def layernorm(b, t, ready, i=0):
                pe.wait_ge(*ready)
                mm(own(b, i), w("sq", "Cm"), A(b, 0), start=True, stop=True).then_inc(*done("pe", b, f"{t}.c"))
                pe.wait_ge(*after("act", b, f"{t}.sq"))
                mm(own(b, i + 1), w("sq", "ones"), A(b, 1), start=True, stop=True).then_inc(*done("pe", b, f"{t}.v"))

            def squares(b, t, i):
                pe.wait_ge(*after("act", b, f"{t}.sq"))
                mm(own(b, i), w("sq", "ones"), A(b, 1), start=True, stop=True).then_inc(*done("pe", b, f"{t}.ss"))

            pe.wait_ge(loads["xa0"], 16)
            ctxT = w("xa0", "ctx")
            for i, name in enumerate(("Wk", "Wv")):
                for blk in range(4):
                    last = mm(bank(i)[:, blk * 64:blk * 64 + 64], w("xa0", name, 128 * blk, 128)[0:CD, :],
                              ctxT[0:CD, :], start=True, stop=True)
            last.then_inc(*done("pe", "w", "kv"))
            pe.wait_ge(*after("act", "w", "kv"))
            for par in range(2):
                p0 = 64 * par
                for b in range(B):
                    for blk in range(4):
                        last = mm(bank(2 + par)[:, b * 128 + blk * J:b * 128 + blk * J + J],
                                  w("xa0", "WqT", 128 * blk, 128)[p0:p0 + 64, :],
                                  grid(KTs, 64)[p0:p0 + 64, blk, b * J:b * J + J], start=True, stop=True)
            last.then_inc(*done("pe", "w", "m0"))
            for par in range(2):
                p0 = 64 * par
                for b in range(B):
                    for blk in range(4):
                        q = 32 * ((2 * blk + par) % 4)
                        c = (b * 2 + blk // 2) * 128
                        last = mm(bank(4 + par)[q:q + 32, c:c + 128],
                                  grid(VTs, 64)[p0:p0 + 64, blk, b * J:b * J + J],
                                  w("xa0", "Wo", 128 * blk, 128)[p0:p0 + 64, :], start=True, stop=True)
            last.then_inc(*done("pe", "w", "v0"))
            pe.wait_ge(loads["late"], 16)
            pe.wait_ge(*after("act", "w", "kv"))
            mm(bank(0)[:, 0:64], w("late", "Wk")[0:CD, :], ctxT[0:CD, :], start=True, stop=True)
            mm(bank(0)[:, 64:128], w("late", "Wv")[0:CD, :], ctxT[0:CD, :], start=True, stop=True)\
                .then_inc(*done("pe", "w", "k1"))
            pe.wait_ge(*after("act", "w", "k1"))
            pe.wait_ge(*after("act", "w", "v0"))
            pe.wait_ge(*after("dve", "w", "m0b"))
            for h in range(H1):
                p0 = 32 * h
                last = mm(bank(1 + h)[:, 0:64] if h < 3 else bank(7)[:, 0:64],
                          w("late", "WqT")[p0:p0 + 32, :], K1s[p0:p0 + 32, :], start=True, stop=True)
            last.then_inc(*done("pe", "w", "m1"))
            pe.wait_ge(*after("act", "w", "vr"))
            for b in range(B):
                mm(bank(5 + b), Vrep[:, 128 * b:128 * b + 128], w("late", "film"), start=True, stop=True)\
                    .then_inc(*done("pe", "w", f"f{b}"))

            pe.wait_ge(loads["sq"], 16)
            pe.wait_ge(*after("dve", "w", "m1"))
            pe.wait_ge(*after("dve", "w", "VF1"))
            for b in range(B):
                squares(b, "h1", 0)
            pe.wait_ge(loads["hawk"], 16)
            for b in range(B):
                pe.wait_ge(*after("dve", b, "xn1"))
                for i, blk in enumerate((2, 3, 0, 1)):
                    mm(own(b, i), w("hawk", "Win", 128 * blk, 128), A(b, 2), start=True, stop=True)\
                        .then_inc(*done("pe", b, f"z{i}"))
            for b in range(B):
                pe.wait_ge(*after("dve", b, "cw1.0"))
                for o in range(4):
                    if o == 2:
                        pe.wait_ge(*after("act", b, "gg1"))
                    for k in range(2):
                        last = mm(own(b, o), w("hawk", "Wga", 512 * k + 128 * o, 128), A(b, 5 + k),
                                  start=(k == 0), stop=(k == 1))
                    last.then_inc(*done("pe", b, f"g{o}"))
            for b in range(B):
                pe.wait_ge(*after("act", b, "ti1"))
                for k in range(2):
                    pe.wait_ge(*after("dve", b, f"gh{k}"))
                    last = mm(own(b, 0), w("hawk", "Wou", 128 * k, 128), A(b, 3 + k), start=(k == 0), stop=(k == 1))
                last.then_inc(*done("pe", b, "rg"))
            for b in range(B):
                squares(b, "h4", 1)
            for b in range(B):
                pe.wait_ge(*after("dve", b, "xn2"))
                for i, blk in enumerate((0, 1, 2, 3)):
                    mm(own(b, i), w("hawk", "Wgr", 128 * blk, 128), A(b, 2), start=True, stop=True)\
                        .then_inc(*done("pe", b, f"gr{i}"))
            for b in range(B):
                for k in range(2):
                    pe.wait_ge(*after("dve", b, f"hm{k}"))
                    last = mm(own(b, 0), w("hawk", "Wsh", 128 * k, 128), A(b, 3 + k), start=(k == 0), stop=(k == 1))
                last.then_inc(*done("pe", b, "shr"))
            for b in range(B):
                layernorm(b, "ln1", after("dve", b, "s1"), 1)

            pe.wait_ge(loads["bf"], 16)
            pe.wait_ge(*after("dve", "w", "kb1"))
            for b in range(B):
                pe.wait_ge(*after("dve", b, "X1"))
                for p in range(2):
                    for i in range(2):
                        c = own(b, p)[:, 256 * i:256 * i + 256]
                        mm(c, Xin[b][:, 128 * (2 * p + i):128 * (2 * p + i) + 128], M0[:, b, :], start=True, stop=False)
                        last = mm(c, w("bf", "one")[0:1, :], krowb[:, 256 * b:256 * b + 256], start=False, stop=True)
                    last.then_inc(*done("pe", b, f"xa.s{p}"))
            for b in range(B):
                for p in range(2):
                    pe.wait_ge(*after("dve", b, f"xa.p{p}"))
                    for g in range(2):
                        for i in range(2):
                            tt = 128 * (2 * p + i)
                            last = tr(own(b, 2 + g)[:, tt:tt + 128],
                                      A(b, 2 + p)[:, 256 * i + 128 * g:256 * i + 128 * g + 128], w("sq", "id"))
                    last.then_inc(*done("pe", b, f"xa.t{p}"))
            for b in range(B):
                for g in range(2):
                    pe.wait_ge(*after("act", b, f"xa.a{g}"))
                    last = mm(own(b, 0), V0[:, b, g, :], A(b, 4 + g), start=(g == 0), stop=(g == 1))
                last.then_inc(*done("pe", b, "xa.o"))
            for b in range(B):
                layernorm(b, "ln2", after("dve", b, "s2"), 1)

            for b in range(B):
                pe.wait_ge(*after("dve", b, "X2"))
            pe.wait_ge(*after("pool", "w", "P1"))
            for c in range(8):
                for i in range(16):
                    d = 16 * c + i
                    last = mm(bank(c)[0:PA, PB_ * i:PB_ * i + PB_], PT[:, d, :], QT[:, d, :], start=True, stop=True)
                last.then_inc(*done("pe", "w", f"kp{c}"))
            pe.wait_ge(kshuf, 16 * PA)
            pe.wait_ge(*after("act", "w", "kp0"))
            for j in range(NT):
                last = tr(bank(0)[:, 128 * j:128 * j + 128], Kdl[:, 128 * j:128 * j + 128], w("sq", "id"))
            last.then_inc(*done("pe", "w", "kt"))

            pe.wait_ge(loads["mla"], 16)
            pe.wait_ge(*after("act", "w", "kl"))
            pe.wait_ge(*after("act", "w", "kp7"))
            for b in range(B):
                squares(b, "m1", 0)
            for b in range(B):
                pe.wait_ge(*after("dve", b, "xm"))
                mm(own(b, 1)[0:64, :], w("mla", "lat"), A(b, 2), start=True, stop=True).then_inc(*done("pe", b, "lat"))
                mm(own(b, 2), w("mla", "kr"), A(b, 2), start=True, stop=False)
                mm(own(b, 3), w("mla", "ks"), A(b, 2), start=True, stop=True)
                pe.wait_ge(*after("act", b, "lat"))
                mm(own(b, 2), w("mla", "kx")[0:32, :], A(b, 3)[0:32, :], start=False, stop=True)\
                    .then_inc(*done("pe", b, "kf"))
                mm(own(b, 0), w("mla", "q")[32:64, :], A(b, 3)[32:64, :], start=True, stop=True)\
                    .then_inc(*done("pe", b, "q0"))
                mm(own(b, 1), w("mla", "qs")[32:64, :], A(b, 3)[32:64, :], start=True, stop=True)\
                    .then_inc(*done("pe", b, "q1"))
                pe.wait_ge(*after("dve", b, "k2"))
                for i in range(NT):
                    last = mm(own(b, 3)[:, 128 * i:128 * i + 128], A(b, 3)[0:32, 128 * i:128 * i + 128],
                              w("mla", "v")[0:32, :], start=True, stop=True)
                last.then_inc(*done("pe", b, "v"))

            def max_unit(b, pair, u):
                hs = (2 * pair, 2 * pair + 1)
                n = 5 * pair + "ABCDE".index(u)
                ring = bank(n % 2)
                if n >= 2:
                    pe.wait_ge(*after("dve", b, f"mx{(n - 2) // 5}.{'ABCDE'[(n - 2) % 5]}"))
                segs = {"A": [(hs[0], 3, 0)], "B": [(hs[0], 2, 0), (hs[0], 0, 384)],
                        "C": [(hs[1], 3, 0)], "D": [(hs[1], 2, 0), (hs[1], 0, 384)],
                        "E": [(hs[0], 1, 0), (hs[1], 1, 256)]}[u]
                rows = C6 * HD
                for h, qt, c in segs:
                    n_ = 128 * (qt + 1)
                    mm(ring[:, c:c + n_], Qst[b][0:rows, h, 128 * qt:128 * qt + 128], Kst[b][0:rows, h, 0:n_],
                       start=True, stop=False)
                    last = mm(ring[:, c + n_ - 128:c + n_], w("bf", "id"), w("bf", "mS"), start=False, stop=True)
                last.then_inc(*done("pe", b, f"mx{pair}.{u}"))

            def score_unit(b, pair, u):
                hs = (2 * pair, 2 * pair + 1)
                first = {"X": 2, "Y": 4, "Z": 6}[u]
                if pair:
                    pe.wait_ge(*after("act", b, f"st{pair - 1}.{u}"))
                segs = {"X": [(hs[0], 0, 0), (hs[0], 1, 512), (hs[0], 3, 896)],
                        "Y": [(hs[1], 0, 0), (hs[1], 1, 512), (hs[1], 3, 896)],
                        "Z": [(hs[0], 2, 0), (hs[1], 2, 256)]}[u]
                for h, kb, c in segs:
                    n_ = T - 128 * kb
                    o = bank(first + c // T)[:, c % T:c % T + n_]
                    mm(o, Kst[b][0:KROWS, h, 128 * kb:128 * kb + 128], Qst[b][0:KROWS, h, 128 * kb:T],
                       start=True, stop=False)
                    last = mm(o[:, 0:128], w("bf", "id"), w("bf", "mT"), start=False, stop=True)
                last.then_inc(*done("pe", b, f"st{pair}.{u}"))

            def values(b, pair):
                g = 2 * pair // GH
                if 2 * pair % GH == 0:
                    if g:
                        pe.wait_ge(*after("dve", b, f"y{g - 1}"))
                    elif b:
                        pe.wait_ge(*after("dve", 0, f"y{NH // GH - 1}"))
                pe.wait_ge(*after("act", b, f"st{pair}.Z"))
                base = {0: (0, 0), 1: (512, 0), 3: (896, 0)}
                for i in range(2):
                    h = 2 * pair + i
                    for qt in range(NT):
                        for kb in range(qt + 1):
                            col = (2048 + 256 * i if kb == 2 else 1024 * i + base[kb][0]) + 128 * (qt - kb)
                            c = (qt * GH + h % GH) * (HD + 1)
                            last = mm(bank(7)[:, c:c + HD + 1], P[pair % 2][:, col:col + 128], Vaug[b][:, kb, h, :],
                                      start=(kb == 0), stop=(kb == qt))
                last.then_inc(*done("pe", b, f"vp{pair}"))

            def minus_max(b):
                pe.wait_ge(*after("dve", b, "nl"))
                for i in range(NT):
                    last = tr(bank(0).bitcast(BF16)[0:48, 128 * i:128 * i + 128], spb[b][:, i, :], w("bf", "id"))
                last.then_inc(*done("pe", b, "nmt"))

            def attention_out(b):
                for g in range(NH // GH):
                    pe.wait_ge(*after("dve", b, f"y{g}"))
                for i in range(NT):
                    last = tr(bank(0)[:, 128 * i:128 * i + 128], A(b, 4)[:, 128 * i:128 * i + 128], w("sq", "id"))
                last.then_inc(*done("pe", b, "yt"))
                pe.wait_ge(*after("act", b, "yt"))
                mm(bank(1), w("mla", "o"), A(b, 5), start=True, stop=True).then_inc(*done("pe", b, "mo"))

            for b in range(B):
                pe.wait_ge(*after("act", b, "v"))
                pe.wait_ge(*after("dve", b, "q2"))
            pe.wait_ge(stack["k", 0], 16 * 7)
            pe.wait_ge(stack["q", 0], 16 * 6)
            for pair in _HP:
                for u in "ABCDE":
                    max_unit(0, pair, u)
            minus_max(0)
            pe.wait_ge(stack["k", 1], 16 * 7)
            pe.wait_ge(stack["q", 1], 16 * 6)
            pe.wait_ge(*after("act", 0, "nmt"))
            for pair in _HP:
                if pair == 1:
                    pe.wait_ge(stack["m", 0], 16)
                for u in "ABCDE":
                    max_unit(1, pair, u)
                if pair >= 1:
                    for u in "XYZ":
                        score_unit(0, pair - 1, u)
                if pair >= 2:
                    values(0, pair - 2)
            minus_max(1)
            for u in "XYZ":
                score_unit(0, NH // 2 - 1, u)
            values(0, NH // 2 - 2)
            values(0, NH // 2 - 1)
            pe.wait_ge(*after("act", 1, "nmt"))
            attention_out(0)
            pe.wait_ge(stack["m", 1], 16)
            for u in "XYZ":
                pe.wait_ge(*after("act", 0, f"st{NH // 2 - 1}.{u}"))
            for pair in _HP:
                for u in "XYZ":
                    score_unit(1, pair, u)
                if pair >= 1:
                    values(1, pair - 1)
            values(1, NH // 2 - 1)
            pe.wait_ge(*after("dve", 0, "x2a"))
            attention_out(1)

            def route(b, r, group, name, n, i):
                for t in range(NT):
                    last = mm(own(b, i)[:, n * t:n * t + n], A(b, 2)[:, 128 * t:128 * t + 128], w(group, name),
                              start=True, stop=True)
                last.then_inc(*done("pe", b, r))

            def turn_weights(b, name, ready, n, i):
                pe.wait_ge(*ready)
                for t in range(NT):
                    last = tr(own(b, i).bitcast(BF16)[0:n, 128 * t:128 * t + 128], spb[b][:, t, 0:n], w("bf", "id"))
                last.then_inc(*done("pe", b, name))

            pe.wait_ge(loads["moe0"], 16)
            pe.wait_ge(loads["sel0"], 16)
            pe.wait_ge(*after("dve", 1, "x2a"))
            for b in range(B):
                squares(b, "f1", 0)
            for b in range(B):
                pe.wait_ge(*after("dve", b, "xf"))
                route(b, "rt", "moe0", "r", E0, 1)
            for b in range(B):
                turn_weights(b, "wt", after("dve", b, "wl"), 3 * E0, 2)

            def unit(b, k, last_k, routed, group, sel, rows, x, n):
                g, u, ww, d = n
                if k <= last_k:
                    if k:
                        pe.wait_ge(*after("act", b, f"{ {'fg': 'sl', 'eg': 'el'}[g] }{k - 1}"))
                    mm(own(b, 0), w(group, "g", 128 * k, 128), x, start=True, stop=True)\
                        .then_inc(*done("pe", b, f"{g}{k}"))
                    if k:
                        pe.wait_ge(*after("dve", b, f"{ {'fu': 'hu', 'eu': 'eu'}[u] }{k - 1}"))
                    mm(own(b, 1), w(group, "u", 128 * k, 128), x, start=True, stop=True)\
                        .then_inc(*done("pe", b, f"{u}{k}"))
                    if k < routed:
                        if k:
                            pe.wait_ge(*after("dve", b, f"{ {'fw': 'hw', 'ew': 'ew'}[ww] }{k - 1}"))
                        mm(own(b, 2), w(sel, "s", 128 * k, 128)[0:rows, :], wT[b][0:rows, :], start=True, stop=True)\
                            .then_inc(*done("pe", b, f"{ww}{k}"))
                if k:
                    j = k - 1
                    h = ({'fd': 'hw', 'ed': 'ew'} if j < routed else {'fd': 'hu', 'ed': 'eu'})[d]
                    pe.wait_ge(*after("dve", b, f"{h}{j}"))
                    mm(own(b, 3), w(group, "d", 128 * j, 128), A(b, 6 + j % 2), start=(j == 0), stop=(j == last_k))\
                        .then_inc(*done("pe", b, f"{d}{k}"))

            for b in range(B):
                pe.wait_ge(*after("act", b, "wt"))
            for k in range(U0 + 1):
                for b in range(B):
                    unit(b, k, U0 - 1, E0, "moe0", "sel0", 3 * E0, A(b, 2), ("fg", "fu", "fw", "fd"))
            for b in range(B):
                layernorm(b, "ln3", after("dve", b, "s3"), 0)

            pe.wait_ge(loads["selA"], 16)
            for b in range(B):
                pe.wait_ge(*after("dve", b, "X3"))
                mm(own(b, 0)[0:96, :], w("late", "WBC"), Xin[b][:, :], start=True, stop=True)\
                    .then_inc(*done("pe", b, "bc"))
                mm(own(b, 1), w("late", "Wd"), Xin[b][:, :], start=True, stop=True).then_inc(*done("pe", b, "de"))
            for b in range(B):
                pe.wait_ge(*after("dve", b, "bl"))
                pe.wait_ge(*after("dve", b, "rl"))
            for i in range(NS + 1):
                for b in range(B):
                    parts_bc = A(b, 3)[:, 0:256].bitcast(BF16)
                    if i < NS:
                        if i:
                            pe.wait_ge(*after("act", b, f"bb{i - 1}"))
                        mm(own(b, 0), w("selA", "s", 128 * i, 128)[0:96, :], parts_bc[0:96, :], start=True, stop=True)\
                            .then_inc(*done("pe", b, f"bn{i}"))
                        if i:
                            pe.wait_ge(*after("dve", b, f"hc{i - 1}"))
                        mm(own(b, 1), w("selA", "s", 128 * (NS + i), 128)[0:96, :], parts_bc[0:96, :], start=True,
                           stop=True).then_inc(*done("pe", b, f"cn{i}"))
                    if i:
                        pe.wait_ge(*after("dve", b, f"hc{i - 1}"))
                        mm(own(b, 2), w("sq", "id"), A(b, 12 + (i - 1) % 2), start=(i == 1), stop=(i == NS))\
                            .then_inc(*done("pe", b, f"yn{i}"))
            for b in range(B):
                layernorm(b, "ln4", after("dve", b, "s4"), 0)

            for b in range(B):
                pe.wait_ge(*after("dve", b, "X4"))
            pe.wait_ge(loads["dft"], 16)

            def forward(o, c, f, rhs):
                for j in range(NT):
                    last = mm(o, w("dft", "F", 1024 * j + 512 * c + 128 * f, 128), rhs(j), start=(j == 0),
                              stop=(j == NT - 1))
                return last

            for c in range(2):
                for f in range(NFB):
                    last = forward(bank(c)[:, 128 * f:128 * f + 128], c, f, lambda j: KL[:, j, :])
                last.then_inc(*done("pe", "w", f"kf{c}"))

            for b in range(B):
                for i in range(NT):
                    c = own(b, 2)[:, 128 * i:128 * i + 128]
                    mm(c, Xin[b][:, 128 * i:128 * i + 128], M1[:, b, :], start=True, stop=False)
                    last = mm(c, w("bf", "one")[0:1, :], krowb[:, 512 + 128 * b:640 + 128 * b], start=False, stop=True)
                last.then_inc(*done("pe", b, "xb.s"))
            for b in range(B):
                pe.wait_ge(*after("dve", b, "xb.p"))
                for i in range(NT):
                    last = tr(own(b, 3)[:, 128 * i:128 * i + 128], A(b, 2)[:, 128 * i:128 * i + 128], w("sq", "id"))
                last.then_inc(*done("pe", b, "xb.t"))
            pe.wait_ge(*after("act", "w", "kf1"))
            for b in range(B):
                pe.wait_ge(*after("act", b, "xb.a"))
                for o in range(4):
                    mm(own(b, o), VF[:, b, 128 * o:128 * o + 128], A(b, 3), start=True, stop=True)\
                        .then_inc(*done("pe", b, f"fl{o}"))
            for b in range(B):
                pe.wait_ge(*after("act", b, "s1"))
                mm(own(b, 0), w("sq", "Cm"), Xin[b][:, :], start=True, stop=True).then_inc(*done("pe", b, "lni.c"))
                pe.wait_ge(*after("act", b, "lni.sq"))
                mm(own(b, 1), w("sq", "ones"), A(b, 1), start=True, stop=True).then_inc(*done("pe", b, "lni.v"))
            for b in range(B):
                pe.wait_ge(*after("pool", b, "xin"))
                pe.wait_ge(*after("act", b, "s3"))
                for j in range(NT):
                    last = tr(own(b, 2)[:, 128 * j:128 * j + 128], A(b, 2)[:, 128 * j:128 * j + 128], w("sq", "id"))
                last.then_inc(*done("pe", b, "xit"))

            for b in range(B):
                pe.wait_ge(*after("act", b, "xit"))
                pe.wait_ge(*after("dve", b, "lni.x"))
            for h in range(2):
                for c in range(2):
                    for f in range(2):
                        last = forward(bank(4 * h + 2 * c)[:, 256 * f:256 * f + 256], c, 2 * h + f,
                                       lambda j: XT[:, j, :, :].rearrange("p b d -> p (b d)"))
                    last.then_inc(*done("pe", "w", f"xf{h}{c}"))
            pe.wait_ge(*after("dve", "w", "yi1"))
            for b in range(B):
                n = 0
                for c in range(2):
                    for f in range(NFB):
                        last = mm(own(b, 0), Yf[:, c, f, 128 * b:128 * b + 128],
                                  w("dft", "G", (NFB * c + f) * T, T), start=(n == 0), stop=(n == 2 * NFB - 1))
                        n += 1
                last.then_inc(*done("pe", b, "inv"))
            for b in range(B):
                layernorm(b, "lnf", after("dve", b, "xt"), 1)
            for b in range(B):
                pe.wait_ge(*after("act", b, "lnf.g"))
                for o in range(4):
                    mm(own(b, o), w("late", "W1", 128 * o, 128), A(b, 2), start=True, stop=True)\
                        .then_inc(*done("pe", b, f"w1{o}"))
            for b in range(B):
                for k in range(4):
                    pe.wait_ge(*after("act", b, f"u{k}"))
                    last = mm(own(b, 0), w("late", "W2", 128 * k, 128), A(b, 6 + k), start=(k == 0), stop=(k == 3))
                last.then_inc(*done("pe", b, "w2"))
            for b in range(B):
                layernorm(b, "lno", after("dve", b, "xt2"), 1)
            for b in range(B):
                layernorm(b, "ln5", after("dve", b, "s5"), 1)

            for b in range(B):
                pe.wait_ge(*after("dve", b, "X5"))
                for t in range(NT):
                    last = mm(own(b, 0)[:, E1 * t:E1 * t + E1], Xin[b][:, 128 * t:128 * t + 128], w("late", "gate"),
                              start=True, stop=True)
                last.then_inc(*done("pe", b, "rt1"))
            for b in range(B):
                turn_weights(b, "wt1", after("dve", b, "wl1"), 3 * E1, 1)
            pe.wait_ge(loads["ffn1"], 16)
            pe.wait_ge(loads["sel1"], 16)
            for b in range(B):
                pe.wait_ge(*after("act", b, "wt1"))
            for k in range(UB1 + 1):
                for b in range(B):
                    unit(b, k, UB1 - 1, RB1, "ffn1", "sel1", 3 * E1, Xin[b][:, :], ("eg", "eu", "ew", "ed"))
            for b in range(B):
                layernorm(b, "ln6", after("dve", b, "s6"), 0)

        @block.scalar
        def _(act):
            def f(out_, in_, func, step, bias=0.0, scale=1.0):
                nc.scalar.activation(out_, in_, func, bias=bias, scale=scale).then_inc(*done("act", *step))

            def inverse_deviation(b, t, src, stat):
                act.wait_ge(*after("pe", b, f"{t}.c"))
                f(A(b, 1), src, ACT.Square, (b, f"{t}.sq"))
                act.wait_ge(*after("pe", b, f"{t}.v"))
                f(A(b, 7), stat, ACT.Ln, (b, f"{t}.l"), scale=1.0 / D, bias=vec("eps"))
                act.wait_ge(*after("act", b, f"{t}.l"))
                f(A(b, 7), A(b, 7), ACT.Exp, (b, f"{t}.r"), scale=-0.5)

            def layernorm(t, i=0):
                for b in range(B):
                    inverse_deviation(b, t, own(b, i), own(b, i + 1))

            def root_mean_square(t, i, bias=None):
                for b in range(B):
                    act.wait_ge(*after("pe", b, f"{t}.ss"))
                    f(A(b, 7), own(b, i), ACT.Ln, (b, f"{t}.l"), scale=1.0 / D)
                    act.wait_ge(*after("act", b, f"{t}.l"))
                    if bias is None:
                        f(A(b, 7), A(b, 7), ACT.Exp, (b, f"{t}.r"), scale=-0.5)
                    else:
                        f(A(b, 7), A(b, 7), ACT.Exp, (b, f"{t}.n"), scale=0.5)
                        act.wait_ge(*after("act", b, f"{t}.n"))
                        f(A(b, 7), A(b, 7), ACT.Ln, (b, f"{t}.m"), bias=bias)
                        act.wait_ge(*after("act", b, f"{t}.m"))
                        f(A(b, 7), A(b, 7), ACT.Exp, (b, f"{t}.r"), scale=-1.0)

            for b in range(B):
                act.wait_ge(loads[f"x{b}"], 16)
                f(A(b, 1), Xin[b][:, :], ACT.Square, (b, "h1.sq"))
            act.wait_ge(loads["vec"], 16)
            f(fb_a, w("vec", "fb"), ACT.Abs, ("w", "fb.a"))
            act.wait_ge(*after("act", "w", "fb.a"))
            f(fb_e, fb_a, ACT.Exp, ("w", "fb.e"), scale=-1.0)
            act.wait_ge(*after("act", "w", "fb.e"))
            f(fb_l, fb_e, ACT.Ln, ("w", "fb.l"), bias=vec("one"))
            act.wait_ge(*after("pe", "w", "kv"))
            f(KTs, bank(0)[:, 0:256], ACT.Copy, ("w", "kv0"))
            f(VTs, bank(1)[:, 0:256], ACT.Copy, ("w", "kv"))
            act.wait_ge(*after("pe", "w", "v0"))
            for q in range(4):
                last = nc.scalar.activation(V0[32 * q:32 * q + 32, :, :, :].rearrange("p b g n -> p (b g n)"),
                                            bank(4 + q % 2)[32 * q:32 * q + 32, :], ACT.Copy)
            last.then_inc(*done("act", "w", "v0"))
            act.wait_ge(*after("pe", "w", "k1"))
            f(K1s, bank(0)[:, 0:64], ACT.Copy, ("w", "k1"))
            for b in range(B):
                last = nc.scalar.activation(Vrep[:, 128 * b:128 * b + 128].rearrange("p (h g) -> p h g", g=J),
                                            over(bank(0)[:, 64 + J * b:64 + J * b + J], [128, H1, J], 1), ACT.Copy)
            last.then_inc(*done("act", "w", "vr"))
            root_mean_square("h1", 0)

            for b in range(B):
                for k in range(2):
                    act.wait_ge(*after("pe", b, f"z{k}"))
                    f(A(b, 5 + k), own(b, k), ACT.Identity, (b, f"cv{k}"), scale=vec("cw", 4 * k + 3), bias=vec("cb", k))
                for k in range(2):
                    act.wait_ge(*after("pe", b, f"z{2 + k}"))
                    f(A(b, 3 + k), own(b, 2 + k), ACT.Gelu, (b, f"gg{k}"))
            act.wait_ge(*after("pool", "w", "bh"))
            act.wait_ge(*after("pool", "w", "fb.c"))
            for b in range(B):
                for o, name in enumerate(("tf0", "tf1", "ti0", "ti1")):
                    act.wait_ge(*after("pe", b, f"g{o}"))
                    f(A(b, 7 + o), own(b, o), ACT.Tanh, (b, name), scale=0.5, bias=bhalf[:, o:o + 1])
            for b in range(B):
                for k in range(2):
                    act.wait_ge(*after("act", b, f"tf{k}"))
                    f(A(b, 7 + k), A(b, 7 + k), ACT.Exp, (b, f"al{k}"), scale=fcoef[:, k:k + 1], bias=fcoef[:, k:k + 1])
                for k in range(2):
                    act.wait_ge(*after("act", b, f"al{k}"))
                    f(A(b, 1 + k), A(b, 7 + k), ACT.Square, (b, f"sa{k}"))
                for k in range(2):
                    act.wait_ge(*after("act", b, f"sa{k}"))
                    f(A(b, 1 + k), A(b, 1 + k), ACT.Ln, (b, f"lb{k}"), scale=-0.25, bias=vec("q25"))
                for k in range(2):
                    act.wait_ge(*after("act", b, f"lb{k}"))
                    f(A(b, 1 + k), A(b, 1 + k), ACT.Exp, (b, f"hb{k}"), scale=0.5)
            for b in range(B):
                act.wait_ge(*after("dve", b, "x1"))
                f(A(b, 1), A(b, 5), ACT.Square, (b, "h4.sq"))
            root_mean_square("h4", 1)
            for b in range(B):
                for k in range(2):
                    act.wait_ge(*after("pe", b, f"gr{k}"))
                    f(A(b, 3 + k), own(b, k), ACT.Gelu, (b, f"gm{k}"))
            layernorm("ln1", 1)

            for b in range(B):
                for p in range(2):
                    act.wait_ge(*after("dve", b, f"xa.d{p}"))
                    f(A(b, 2 + p), A(b, 2 + p), ACT.Exp, (b, f"xa.e{p}"))
            for b in range(B):
                act.wait_ge(*after("pe", b, "xa.t1"))
                for g in range(2):
                    f(A(b, 4 + g), own(b, 2 + g), ACT.Copy, (b, f"xa.a{g}"))
            layernorm("ln2", 1)

            act.wait_ge(loads["s4d"], 16)
            f(dct(0), w("s4d", "ldt"), ACT.Exp, ("w", "dt"))
            act.wait_ge(*after("pool", "w", "zr"))
            f(dct(3), dct(1), ACT.Tanh, ("w", "th"), scale=0.5)
            act.wait_ge(*after("pool", "w", "kf"))
            f(dct(6), dct(5), ACT.Sin, ("w", "sh"), scale=TWO_PI)
            f(dct(7), dct(7), ACT.Sin, ("w", "sy"), scale=TWO_PI)
            for c in _HALF:
                act.wait_ge(*after("pool", "w", f"aQ{c}"))
                f(tb("eQ"), tb("eQ"), ACT.Exp, ("w", f"eQ{c}"))
                act.wait_ge(*after("pool", "w", f"aP{c}"))
                f(tb("eP"), tb("eP"), ACT.Exp, ("w", f"eP{c}"))
                act.wait_ge(*after("pool", "w", f"g2{c}"))
                f(tb("gQ"), tb("gQ"), ACT.Sin, ("w", f"sQ{c}"), scale=TWO_PI)
                f(tb("g1"), tb("g1"), ACT.Sin, ("w", f"s1{c}"), scale=TWO_PI)
                f(tb("g2"), tb("g2"), ACT.Sin, ("w", f"s2{c}"), scale=TWO_PI)
            for c in range(8):
                act.wait_ge(*after("pe", "w", f"kp{c}"))
                f(Ksb[:, T * c:T * c + T], bank(c)[0:PA, :], ACT.Copy, ("w", f"kp{c}"))
            act.wait_ge(*after("pe", "w", "kt"))
            f(KL[:, :, :].rearrange("p j d -> p (j d)"), bank(0), ACT.Copy, ("w", "kl"))

            for b in range(B):
                f(A(b, 1), Xin[b][:, :], ACT.Square, (b, "m1.sq"))
            root_mean_square("m1", 0, vec("eps"))
            for b in range(B):
                act.wait_ge(*after("pe", b, "lat"))
                f(A(b, 3)[0:64, :], own(b, 1)[0:64, :], ACT.Copy, (b, "lat"))
            for b in range(B):
                act.wait_ge(*after("dve", b, "kk"))
                f(KP[b][0], A(b, 5), ACT.Copy, (b, "kh"))
                act.wait_ge(*after("dve", b, "kr"))
                f(KP[b][1], A(b, 6), ACT.Copy, (b, "km"))
                act.wait_ge(*after("dve", b, "qq"))
                f(QP[b][0], A(b, 4), ACT.Copy, (b, "qh"))
                act.wait_ge(*after("dve", b, "qr"))
                f(QP[b][1], A(b, 1), ACT.Copy, (b, "qm"))
                act.wait_ge(*after("pe", b, "v"))
                act.wait_ge(*after("pool", "w", f"va{b}"))
                f(Vaug[b][:, :, :, 0:HD], own(b, 3).rearrange("p (i h d) -> p i h d", i=NT, d=HD), ACT.Copy, (b, "v"))

            def parts_of_max(b):
                act.wait_ge(*after("pe", b, "nmt"))
                f(wT[b][0:48, :], bank(0).bitcast(BF16)[0:48, 0:T], ACT.Copy, (b, "nmt"))

            def probabilities(b, pair):
                s_ = pair % 2
                for u, (b0, n, c) in {"X": (2, 2, 0), "Y": (4, 2, 1024), "Z": (6, 1, 2048)}.items():
                    act.wait_ge(*after("pe", b, f"st{pair}.{u}"))
                    if u == "X":
                        if pair >= 2:
                            act.wait_ge(*after("pe", b, f"vp{pair - 2}"))
                        elif b:
                            act.wait_ge(*after("pe", 0, f"vp{NH // 2 - 2 + pair}"))
                    f(P[s_][:, c:c + n * T], PS[:, b0:b0 + n, :].rearrange("p a t -> p (a t)"), ACT.Exp,
                      (b, f"st{pair}.{u}"))

            parts_of_max(0)
            for pair in range(NH // 2 - 1):
                probabilities(0, pair)
            parts_of_max(1)
            probabilities(0, NH // 2 - 1)

            def attention_out(b):
                act.wait_ge(*after("pe", b, "yt"))
                f(A(b, 5), bank(0), ACT.Copy, (b, "yt"))

            attention_out(0)
            for pair in _HP:
                probabilities(1, pair)
            attention_out(1)

            for b in range(B):
                act.wait_ge(*after("dve", b, "x2a"))
                f(A(b, 1), A(b, 3), ACT.Square, (b, "f1.sq"))
            root_mean_square("f1", 0, vec("eps"))
            for b in range(B):
                act.wait_ge(*after("dve", b, "lg"))
                f(S(b, 288, 28), S(b, 256, 28), ACT.Exp, (b, "rt"), scale=-1.0)
            for b in range(B):
                act.wait_ge(*after("pe", b, "wt"))
                f(wT[b][0:3 * E0, :], own(b, 2).bitcast(BF16)[0:3 * E0, 0:T], ACT.Copy, (b, "wt"))
            for k in range(U0):
                for b in range(B):
                    act.wait_ge(*after("pe", b, f"fg{k}"))
                    if k >= 2:
                        act.wait_ge(*after("dve", b, f"hu{k - 2}"))
                    f(A(b, 4 + k % 2), own(b, 0), ACT.Silu, (b, f"sl{k}"))
            layernorm("ln3")

            for b in range(B):
                act.wait_ge(*after("pe", b, "bc"))
                f(A(b, 2)[0:96, :], own(b, 0)[0:96, :], ACT.Identity, (b, "bc"), bias=vec("bBC")[0:96, :])
                act.wait_ge(*after("pe", b, "de"))
                f(A(b, 7), own(b, 1), ACT.Abs, (b, "ab"), bias=vec("bd"))
                act.wait_ge(*after("act", b, "ab"))
                f(A(b, 7), A(b, 7), ACT.Exp, (b, "ex"), scale=-1.0)
                act.wait_ge(*after("act", b, "ex"))
                f(A(b, 7), A(b, 7), ACT.Ln, (b, "sp"), bias=vec("one"))
            for i in range(NS):
                for b in range(B):
                    if i == 0:
                        act.wait_ge(*after("pool", b, "dl"))
                    if i >= 2:
                        act.wait_ge(*after("dve", b, f"sc{i - 2}"))
                    f(A(b, 9 + i % 2), A(b, 8), ACT.Exp, (b, f"aa{i}"), scale=w("vec", "A", i, 1))
                    act.wait_ge(*after("pe", b, f"bn{i}"))
                    f(A(b, 4 + i % 2), own(b, 0), ACT.Copy, (b, f"bb{i}"))
            layernorm("ln4")
            for c in range(2):
                act.wait_ge(*after("pe", "w", f"kf{c}"))
                f(Kf[:, c, :, :].rearrange("p f d -> p (f d)"), bank(c), ACT.Copy, ("w", f"kf{c}"))

            for b in range(B):
                act.wait_ge(*after("dve", b, "xb.d"))
                f(A(b, 2), A(b, 2), ACT.Exp, (b, "xb.e"))
            for b in range(B):
                act.wait_ge(*after("pe", b, "xb.t"))
                f(A(b, 3), own(b, 3), ACT.Copy, (b, "xb.a"))
            act.wait_ge(*after("pool", "w", "bf1"))
            for b in range(B):
                for o, to in enumerate((4, 5, 6, 8)):
                    act.wait_ge(*after("pe", b, f"fl{o}"))
                    f(A(b, to), own(b, o), ACT.Identity, (b, f"s{o}"), bias=bfilm[:, o:o + 1])

            def affine(b, t, src, dst, g, off):
                act.wait_ge(*after("dve", b, f"{t}.x"))
                f(A(b, dst), A(b, src), ACT.Identity, (b, f"{t}.g"), scale=vec(g), bias=vec(off))

            for b in range(B):
                inverse_deviation(b, "lni", own(b, 0), own(b, 1))
            for b in range(B):
                affine(b, "lni", 9, 10, "gni", "bni")
            for b in range(B):
                act.wait_ge(*after("pe", b, "xit"))
                f(XT[:, :, b, :], own(b, 2).rearrange("p (j d) -> p j d", d=128), ACT.Copy, (b, "xit"))
            layernorm("lnf", 1)
            for b in range(B):
                affine(b, "lnf", 9, 2, "gff", "bff")
            for b in range(B):
                for k in range(4):
                    act.wait_ge(*after("pe", b, f"w1{k}"))
                    f(A(b, 6 + k), own(b, k), ACT.Gelu, (b, f"u{k}"), bias=vec("b1", k))
            layernorm("lno", 1)
            for b in range(B):
                affine(b, "lno", 9, 10, "gno", "bno")
            layernorm("ln5", 1)

            for b in range(B):
                act.wait_ge(*after("dve", b, "ms"))
                f(S(b, 288, 32), S(b, 256, 32), ACT.Exp, (b, "rt1"))
            for b in range(B):
                act.wait_ge(*after("pe", b, "wt1"))
                f(wT[b][0:3 * E1, :], own(b, 1).bitcast(BF16)[0:3 * E1, 0:T], ACT.Copy, (b, "wt1"))
            for k in range(UB1):
                for b in range(B):
                    act.wait_ge(*after("pe", b, f"eg{k}"))
                    if k >= 2:
                        act.wait_ge(*after("dve", b, f"eu{k - 2}"))
                    f(A(b, 4 + k % 2), own(b, 0), ACT.Silu, (b, f"el{k}"))
            layernorm("ln6")

        @block.vector
        def _(dve):
            def tt(out_, a, b_, op, step):
                nc.vector.tensor_tensor(out_, a, b_, op).then_inc(*done("dve", *step))

            def ts(out_, a, s1, s2, op0, op1, step):
                nc.vector.tensor_scalar(out_, a, s1, s2, op0, op1).then_inc(*done("dve", *step))

            def stt(out_, a, s1, b_, op0, op1, step):
                nc.vector.scalar_tensor_tensor(out_, a, s1, b_, op0, op1).then_inc(*done("dve", *step))

            def red(out_, a, op, step):
                nc.vector.tensor_reduce(out_, a, X, op).then_inc(*done("dve", *step))

            def inv(out_, a, step):
                nc.vector.reciprocal(out_, a).then_inc(*done("dve", *step))

            def mine(lane, name):
                dve.wait_ge(*after("dve", lane, name))

            def normed(b, t, name, i, x=None):
                dve.wait_ge(*after("act", b, f"{t}.r"))
                tt(Xin[b][:, :], own(b, i), A(b, 7), ALU.mult, (b, name))

            for n in ("km", "kr", "tm"):
                dve.wait_ge(loads[n], 16)
            nc.vector.tensor_copy(kmaskf, kmask).then_inc(*done("dve", "w", "km"))
            nc.vector.tensor_copy(krowb[:, :], krow).then_inc(*done("dve", "w", "kb0"))
            mine("w", "kb0")
            ts(krowb[:, :], krowb[:, :], -1.0, BIG, ALU.add, ALU.mult, ("w", "kb1"))
            nc.vector.tensor_copy(tmaskf[:, :], tmask).then_inc(*done("dve", "w", "tm"))
            mine("w", "km")
            dve.wait_ge(*after("pe", "w", "m0"))
            for par in range(2):
                stt(M0[:, :, :].rearrange("p b (k two j) -> p two (b k) j", two=2, j=J)[:, par],
                    bank(2 + par)[:, 0:256].rearrange("p (k j) -> p k j", j=J), 64.0 ** -0.5,
                    kmaskf.rearrange("p (k two j) -> p two k j", two=2, j=J)[:, par],
                    ALU.mult, ALU.mult, ("w", "m0" + "ab"[par]))
            dve.wait_ge(*after("pe", "w", "m1"))
            for h in range(H1):
                last = nc.vector.tensor_scalar(M1[:, :, J * h:J * h + J], grid(bank((1, 2, 3, 7)[h])[:, 0:64], J),
                                               32.0 ** -0.5, None, ALU.mult)
            last.then_inc(*done("dve", "w", "m1"))
            for b in range(B):
                dve.wait_ge(*after("pe", "w", f"f{b}"))
                ts(VF[:, b, :], bank(5 + b), vec("mg"), 1.0 / H1, ALU.mult, ALU.mult, ("w", f"VF{b}"))

            for b in range(B):
                dve.wait_ge(*after("act", b, "h1.r"))
                stt(A(b, 2), Xin[b][:, :], vec("g1"), A(b, 7), ALU.mult, ALU.mult, (b, "xn1"))
            for b in range(B):
                for tap in (2, 1, 0):
                    for k in range(2):
                        if tap == 2:
                            dve.wait_ge(*after("act", b, f"cv{k}"))
                        else:
                            mine(b, f"cw{k}.{tap + 1}")
                        n = T - (3 - tap)
                        stt(A(b, 5 + k)[:, 3 - tap:T], own(b, k)[:, 0:n], vec("cw", 4 * k + tap),
                            A(b, 5 + k)[:, 3 - tap:T], ALU.mult, ALU.add, (b, f"cw{k}.{tap}"))
            for b in range(B):
                for k in range(2):
                    dve.wait_ge(*after("act", b, f"ti{k}"))
                    stt(A(b, 9 + k), A(b, 9 + k), 1.0, A(b, 5 + k), ALU.add, ALU.mult, (b, f"in{k}"))
            for b in range(B):
                for k in range(2):
                    dve.wait_ge(*after("act", b, f"hb{k}"))
                    mine(b, f"in{k}")
                    tt(A(b, 9 + k), A(b, 9 + k), A(b, 1 + k), ALU.mult, (b, f"xs{k}"))
                for k in range(2):
                    mine(b, f"xs{k}")
                    nc.vector.tensor_tensor_scan(A(b, 9 + k), A(b, 7 + k), A(b, 9 + k), 0.0, ALU.mult, ALU.add)\
                        .then_inc(*done("dve", b, f"h{k}"))
                for k in range(2):
                    mine(b, f"h{k}")
                    tt(A(b, 3 + k), A(b, 3 + k), A(b, 9 + k), ALU.mult, (b, f"gh{k}"))
            for b in range(B):
                dve.wait_ge(*after("pe", b, "rg"))
                tt(A(b, 5), own(b, 0), Xin[b][:, :], ALU.add, (b, "x1"))
                mine(b, "x1")
                tt(A(b, 6), A(b, 5), Xin[b][:, :], ALU.add, (b, "xx"))
            for b in range(B):
                dve.wait_ge(*after("act", b, "h4.r"))
                stt(A(b, 2), A(b, 5), vec("g2"), A(b, 7), ALU.mult, ALU.mult, (b, "xn2"))
            for b in range(B):
                for k in range(2):
                    dve.wait_ge(*after("act", b, f"gm{k}"))
                    dve.wait_ge(*after("pe", b, f"gr{2 + k}"))
                    tt(A(b, 3 + k), own(b, 2 + k), A(b, 3 + k), ALU.mult, (b, f"hm{k}"))
            for b in range(B):
                dve.wait_ge(*after("pe", b, "shr"))
                tt(A(b, 0), own(b, 0), A(b, 6), ALU.add, (b, "s1"))
            for b in range(B):
                normed(b, "ln1", "X1", 1)

            for b in range(B):
                for p in range(2):
                    dve.wait_ge(*after("pe", b, f"xa.s{p}"))
                    red(S(b, 16 * p, 16), grid(own(b, p), J), ALU.max, (b, f"xa.m{p}"))
                    mine(b, f"xa.m{p}")
                    tt(grid(A(b, 2 + p), J), grid(own(b, p), J), over(S(b, 16 * p, 16), [128, 16, J], 2),
                       ALU.subtract, (b, f"xa.d{p}"))
            for b in range(B):
                for p in range(2):
                    dve.wait_ge(*after("act", b, f"xa.e{p}"))
                    red(S(b, 32 + 16 * p, 16), grid(A(b, 2 + p), J), ALU.add, (b, f"xa.u{p}"))
                    mine(b, f"xa.u{p}")
                    inv(S(b, 32 + 16 * p, 16), S(b, 32 + 16 * p, 16), (b, f"xa.i{p}"))
                    mine(b, f"xa.i{p}")
                    tt(grid(A(b, 2 + p), J), grid(A(b, 2 + p), J), over(S(b, 32 + 16 * p, 16), [128, 16, J], 2),
                       ALU.mult, (b, f"xa.p{p}"))
            for b in range(B):
                dve.wait_ge(*after("pe", b, "xa.o"))
                stt(A(b, 0), own(b, 0), vec("bo"), Xin[b][:, :], ALU.add, ALU.add, (b, "s2"))
            for b in range(B):
                normed(b, "ln2", "X2", 1)

            n = [0]

            def coef(op, *a):
                n[0] += 1
                op(*a, ("w", f"dc{n[0]}"))
                mine("w", f"dc{n[0]}")

            Are, Aim, Cre, Cim = (w("s4d", k) for k in ("Are", "Aim", "Cre", "Cim"))
            dve.wait_ge(*after("act", "w", "sy"))
            dve.wait_ge(*after("pool", "w", "kf"))
            coef(ts, dct(8), dct(3), -1.0, 1.0, ALU.mult, ALU.add)
            coef(inv, dct(8), dct(8))
            coef(stt, dct(8), dct(3), 2.0, dct(8), ALU.mult, ALU.mult)
            coef(tt, dct(9), dct(6), dct(6), ALU.mult)
            coef(ts, dct(3), dct(9), -2.0, 1.0, ALU.mult, ALU.add)
            coef(tt, dct(3), dct(3), dct(8), ALU.mult)
            coef(stt, dct(3), dct(9), -2.0, dct(3), ALU.mult, ALU.add)
            coef(stt, dct(10), dct(8), 1.0, dct(7), ALU.add, ALU.mult)
            coef(tt, dct(11), Are, Are, ALU.mult)
            coef(tt, dct(9), Aim, Aim, ALU.mult)
            coef(tt, dct(11), dct(11), dct(9), ALU.add)
            coef(inv, dct(11), dct(11))
            coef(tt, dct(6), Cre, dct(3), ALU.mult)
            coef(tt, dct(7), Cim, dct(10), ALU.mult)
            coef(tt, dct(6), dct(6), dct(7), ALU.subtract)
            coef(tt, dct(7), Cre, dct(10), ALU.mult)
            coef(tt, dct(9), Cim, dct(3), ALU.mult)
            coef(tt, dct(7), dct(7), dct(9), ALU.add)
            coef(tt, dct(8), dct(6), Are, ALU.mult)
            coef(tt, dct(9), dct(7), Aim, ALU.mult)
            coef(tt, dct(8), dct(8), dct(9), ALU.add)
            coef(tt, dct(8), dct(8), dct(11), ALU.mult)
            coef(tt, dct(5), dct(7), Are, ALU.mult)
            coef(tt, dct(9), dct(6), Aim, ALU.mult)
            coef(tt, dct(5), dct(5), dct(9), ALU.subtract)
            coef(tt, dct(5), dct(5), dct(11), ALU.mult)

            for b in range(B):
                dve.wait_ge(*after("act", b, "m1.r"))
                stt(A(b, 2), Xin[b][:, :], vec("wl1"), A(b, 7), ALU.mult, ALU.mult, (b, "xm"))
            for b in range(B):
                dve.wait_ge(*after("pe", b, "kf"))
                tt(A(b, 5), own(b, 2), w("mla", "COSk"), ALU.mult, (b, "k1"))
                tt(A(b, 6), own(b, 3), w("mla", "SINk"), ALU.mult, (b, "k2"))
                mine(b, "k2")
                tt(A(b, 5), A(b, 5), A(b, 6), ALU.add, (b, "kk"))
                dve.wait_ge(*after("act", b, "kh"))
                tt(A(b, 6), A(b, 5), KP[b][0], ALU.subtract, (b, "kr"))
                dve.wait_ge(*after("act", b, "km"))
                tt(KP[b][2], A(b, 6), KP[b][1], ALU.subtract, (b, "kl"))
                dve.wait_ge(*after("pe", b, "q1"))
                tt(A(b, 4), own(b, 0), w("mla", "COSq"), ALU.mult, (b, "q1"))
                tt(A(b, 1), own(b, 1), w("mla", "SINq"), ALU.mult, (b, "q2"))
                mine(b, "q2")
                tt(A(b, 4), A(b, 4), A(b, 1), ALU.add, (b, "qq"))
                dve.wait_ge(*after("act", b, "qh"))
                tt(A(b, 1), A(b, 4), QP[b][0], ALU.subtract, (b, "qr"))
                dve.wait_ge(*after("act", b, "qm"))
                tt(QP[b][2], A(b, 1), QP[b][1], ALU.subtract, (b, "ql"))

            def maxima(b, pair):
                h = 2 * pair
                m = S(b, 64, NT * NH).rearrange("p (t h) -> p t h", h=NH)
                for i, u in enumerate("ABCDE"):
                    ring = bank((5 * pair + i) % 2)
                    dve.wait_ge(*after("pe", b, f"mx{pair}.{u}"))
                    hh = h + (u in "CD")
                    if u in "AC":
                        red(m[:, 3, hh:hh + 1], ring, ALU.max, (b, f"mx{pair}.{u}"))
                    elif u in "BD":
                        nc.vector.tensor_reduce(m[:, 2, hh:hh + 1], ring[:, 0:384], X, ALU.max)
                        red(m[:, 0, hh:hh + 1], ring[:, 384:512], ALU.max, (b, f"mx{pair}.{u}"))
                    else:
                        red(m[:, 1, h:h + 2], grid(ring, 256), ALU.max, (b, f"mx{pair}.{u}"))

            def split_max(b):
                mine(b, f"mx{NH // 2 - 1}.E")
                m = S(b, 64, NT * NH).rearrange("p (t h) -> p t h", h=NH)
                res = S(b, 128, NT * NH).rearrange("p (t h) -> p t h", h=NH)
                hi, mid, lo = (spb[b][:, :, NH * c:NH * c + NH] for c in range(3))
                ts(hi, m, -1.0, None, ALU.mult, ALU.bypass, (b, "nh"))
                mine(b, "nh")
                stt(res, m, -1.0, hi, ALU.mult, ALU.subtract, (b, "nr"))
                mine(b, "nr")
                nc.vector.tensor_copy(mid, res).then_inc(*done("dve", b, "nm"))
                mine(b, "nm")
                tt(lo, res, mid, ALU.subtract, (b, "nl"))

            def attended(b, g):
                dve.wait_ge(*after("pe", b, f"vp{(g + 1) * GH // 2 - 1}"))
                o = bank(7)[:, 0:NT * GH * (HD + 1)].rearrange("p (k e) -> p k e", e=HD + 1)
                r_ = S(b, 192 + 32 * g, 32)
                inv(r_.unsqueeze(2), o[:, :, HD:HD + 1], (b, f"ri{g}"))
                mine(b, f"ri{g}")
                y = A(b, 4).rearrange("p (t g h d) -> p g t h d", t=NT, g=NH // GH, d=HD)[:, g]
                tt(y, o[:, :, 0:HD].rearrange("p (t h) d -> p t h d", t=NT),
                   r_.rearrange("p (t h) -> p t h", t=NT).unsqueeze(3).to_broadcast([128, NT, GH, HD]),
                   ALU.mult, (b, f"y{g}"))

            def attention_out(b):
                dve.wait_ge(*after("pe", b, "mo"))
                tt(A(b, 3), bank(1), Xin[b][:, :], ALU.add, (b, "x2a"))
                mine(b, "x2a")
                tt(A(b, 9), A(b, 3), Xin[b][:, :], ALU.add, (b, "x2x"))

            for pair in _HP:
                maxima(0, pair)
            split_max(0)
            for pair in _HP:
                maxima(1, pair)
                if 2 * pair == GH + 2:
                    attended(0, 0)
            split_max(1)
            attended(0, 1)
            attention_out(0)
            for g in range(NH // GH):
                attended(1, g)
            attention_out(1)

            def pick(b, p, e, tri, t, guard):
                n3 = [128, NT, e, e]
                p3 = p.rearrange("p (t e) -> p t e", e=e)
                pj = p3.unsqueeze(2).to_broadcast(n3)
                pe_ = p3.unsqueeze(3).to_broadcast(n3)
                gt, ge = (S(b, c, NT * e * e).rearrange("p (t e j) -> p t e j", t=NT, j=e) for c in (320, 576))
                m3 = w("vec", tri).rearrange("p (e j) -> p e j", j=e).unsqueeze(1).to_broadcast(n3)
                rk, we, ws, wi, wn, wr = (S(b, c, n_) for c, n_ in
                                          ((832, NT * e), (864, NT * e), (896, NT), (900, NT), (904, NT * e),
                                           (936, NT * e)))
                tt(gt, pj, pe_, ALU.is_gt, (b, f"gt{t}"))
                tt(ge, pj, pe_, ALU.is_ge, (b, f"ge{t}"))
                mine(b, f"ge{t}")
                tt(ge, ge, m3, ALU.mult, (b, f"gx{t}"))
                mine(b, f"gx{t}")
                tt(gt, gt, ge, ALU.max, (b, f"gm{t}"))
                mine(b, f"gm{t}")
                red(rk, S(b, 320, NT * e * e).rearrange("p (k j) -> p k j", j=e), ALU.add, (b, f"rk{t}"))
                mine(b, f"rk{t}")
                stt(we, rk, 2.0, p, ALU.is_lt, ALU.mult, (b, f"we{t}"))
                mine(b, f"we{t}")
                red(ws, grid(we, e), ALU.add, (b, f"ws{t}"))
                mine(b, f"ws{t}")
                if guard:
                    ts(ws, ws, 1e-20, None, ALU.add, ALU.bypass, (b, f"wa{t}"))
                    mine(b, f"wa{t}")
                inv(wi, ws, (b, f"wi{t}"))
                mine(b, f"wi{t}")
                tt(grid(wn, e), grid(we, e), over(wi, [128, NT, e], 2), ALU.mult, (b, f"wn{t}"))
                mine(b, f"wn{t}")
                hi, mid, lo = (spb[b][:, :, e * c:e * c + e] for c in range(3))
                nc.vector.tensor_copy(hi, grid(wn, e)).then_inc(*done("dve", b, f"wh{t}"))
                mine(b, f"wh{t}")
                tt(grid(wr, e), grid(wn, e), hi, ALU.subtract, (b, f"wr{t}"))
                mine(b, f"wr{t}")
                nc.vector.tensor_copy(mid, grid(wr, e)).then_inc(*done("dve", b, f"wm{t}"))
                mine(b, f"wm{t}")
                tt(lo, grid(wr, e), mid, ALU.subtract, (b, f"wl{t}"))

            def experts(blocks, routed, s, up, hid, wide, u):
                for k in range(blocks):
                    for b in range(B):
                        dve.wait_ge(*after("act", b, f"{s}{k}"))
                        dve.wait_ge(*after("pe", b, f"{up}{k}"))
                        if k >= 2:
                            dve.wait_ge(*after("pe", b, f"{wide[0]}d{k - 1}"))
                        tt(A(b, 6 + k % 2), own(b, 1), A(b, 4 + k % 2), ALU.mult, (b, f"{hid}{k}"))
                        if k < routed:
                            dve.wait_ge(*after("pe", b, f"{wide}{k}"))
                            mine(b, f"{hid}{k}")
                            tt(A(b, 6 + k % 2), own(b, 2), A(b, 6 + k % 2), ALU.mult, (b, f"{u}{k}"))

            for b in range(B):
                dve.wait_ge(*after("act", b, "f1.r"))
                stt(A(b, 2), A(b, 3), vec("wl2"), A(b, 7), ALU.mult, ALU.mult, (b, "xf"))
            for b in range(B):
                dve.wait_ge(*after("pe", b, "rt"))
                tt(S(b, 256, 28), own(b, 1)[:, 0:28], w("vec", "rb"), ALU.add, (b, "lg"))
            for b in range(B):
                dve.wait_ge(*after("act", b, "rt"))
                ts(S(b, 288, 28), S(b, 288, 28), 1.0, None, ALU.add, ALU.bypass, (b, "pd"))
                mine(b, "pd")
                inv(S(b, 288, 28), S(b, 288, 28), (b, "pr"))
                mine(b, "pr")
                pick(b, S(b, 288, 28), E0, "tri0", "", False)
            experts(U0, E0, "sl", "fu", "hu", "fw", "hw")
            for b in range(B):
                dve.wait_ge(*after("pe", b, f"fd{U0}"))
                tt(A(b, 0), own(b, 3), A(b, 9), ALU.add, (b, "s3"))
            for b in range(B):
                normed(b, "ln3", "X3", 0)

            for b in range(B):
                def wide(i, n_=T):
                    return A(b, i)[0:96, 0:n_]

                hi, mid, stk = (A(b, i)[:, 0:256].bitcast(BF16) for i in (4, 6, 3))
                dve.wait_ge(*after("act", b, "bc"))
                nc.vector.tensor_copy(hi[0:96, :], wide(2)).then_inc(*done("dve", b, "bh"))
                mine(b, "bh")
                tt(wide(5), wide(2), hi[0:96, :], ALU.subtract, (b, "br"))
                mine(b, "br")
                nc.vector.tensor_copy(mid[0:96, :], wide(5)).then_inc(*done("dve", b, "bm"))
                mine(b, "bm")
                nc.vector.tensor_copy(stk[0:32, :], hi[0:32, :])
                nc.vector.tensor_copy(stk[32:64, :], mid[32:64, :]).then_inc(*done("dve", b, "bs"))
                tt(stk[64:96, :], A(b, 5)[64:96, :], mid[64:96, :], ALU.subtract, (b, "bl"))
                dve.wait_ge(*after("pe", b, "de"))
                dve.wait_ge(*after("act", b, "ab"))
                ts(A(b, 8), own(b, 1), vec("bd"), 0.0, ALU.add, ALU.max, (b, "rl"))
            for i in range(NS):
                for b in range(B):
                    dve.wait_ge(*after("act", b, f"aa{i}"))
                    dve.wait_ge(*after("pool", b, f"by{i}"))
                    nc.vector.tensor_tensor_scan(A(b, 14 + i % 2), A(b, 9 + i % 2), A(b, 4 + i % 2), 0.0, ALU.mult,
                                                 ALU.add).then_inc(*done("dve", b, f"sc{i}"))
                    mine(b, f"sc{i}")
                    dve.wait_ge(*after("pe", b, f"cn{i}"))
                    if i >= 2:
                        dve.wait_ge(*after("pe", b, f"yn{i - 1}"))
                    tt(A(b, 12 + i % 2), own(b, 1), A(b, 14 + i % 2), ALU.mult, (b, f"hc{i}"))
            for b in range(B):
                dve.wait_ge(*after("pe", b, f"yn{NS}"))
                tt(A(b, 0), own(b, 2), Xin[b][:, :], ALU.add, (b, "s4"))
            for b in range(B):
                normed(b, "ln4", "X4", 0)

            for b in range(B):
                dve.wait_ge(*after("pe", b, "xb.s"))
                red(S(b, 0, 16), grid(own(b, 2), J), ALU.max, (b, "xb.m"))
                mine(b, "xb.m")
                tt(grid(A(b, 2), J), grid(own(b, 2), J), over(S(b, 0, 16), [128, 16, J], 2), ALU.subtract,
                   (b, "xb.d"))
            for b in range(B):
                dve.wait_ge(*after("act", b, "xb.e"))
                red(S(b, 32, 16), grid(A(b, 2), J), ALU.add, (b, "xb.u"))
                mine(b, "xb.u")
                inv(S(b, 32, 16), S(b, 32, 16), (b, "xb.i"))
                mine(b, "xb.i")
                tt(grid(S(b, 32, 16), H1), grid(S(b, 32, 16), H1),
                   over(tmaskf[:, NT * b:NT * b + NT], [128, NT, H1], 2), ALU.mult, (b, "xb.k"))
                mine(b, "xb.k")
                tt(grid(A(b, 2), J), grid(A(b, 2), J), over(S(b, 32, 16), [128, 16, J], 2), ALU.mult, (b, "xb.p"))
            for b in range(B):
                dve.wait_ge(*after("act", b, "lni.r"))
                tt(A(b, 9), own(b, 0), A(b, 7), ALU.mult, (b, "lni.x"))

            for h in range(2):
                Kh = [Kf[:, c, 2 * h:2 * h + 2, :].unsqueeze(2).to_broadcast([128, 2, B, 128]) for c in range(2)]
                Xh = [bank(4 * h + 2 * c).rearrange("p (f b d) -> p f b d", f=2, b=B) for c in range(2)]
                Y = [Yf[:, c, 2 * h:2 * h + 2, :] for c in range(2)]
                Y4 = [y.rearrange("p f (b d) -> p f b d", b=B) for y in Y]
                Z4 = [Zt[:, c, :].rearrange("p (f b d) -> p f b d", f=2, b=B) for c in range(2)]
                Z = [Zt[:, c, :].rearrange("p (f n) -> p f n", f=2) for c in range(2)]
                dve.wait_ge(*after("act", "w", "kf1"))
                dve.wait_ge(*after("pe", "w", f"xf{h}1"))
                if h:
                    mine("w", "yi0")
                tt(Y4[0], Xh[0], Kh[0], ALU.mult, ("w", f"rr{h}"))
                tt(Z4[0], Xh[1], Kh[1], ALU.mult, ("w", f"ii{h}"))
                tt(Y4[1], Xh[0], Kh[1], ALU.mult, ("w", f"ri{h}"))
                tt(Z4[1], Xh[1], Kh[0], ALU.mult, ("w", f"ir{h}"))
                mine("w", f"ii{h}")
                tt(Y[0], Y[0], Z[0], ALU.subtract, ("w", f"yr{h}"))
                mine("w", f"ir{h}")
                tt(Y[1], Y[1], Z[1], ALU.add, ("w", f"yi{h}"))
            for b in range(B):
                dve.wait_ge(*after("pe", b, "inv"))
                dve.wait_ge(*after("pool", b, "xin"))
                stt(A(b, 4), A(b, 2), vec("Ds"), own(b, 0), ALU.mult, ALU.add, (b, "sk"))
                mine(b, "sk")
                dve.wait_ge(*after("act", b, "s3"))
                tt(A(b, 4), A(b, 4), A(b, 6), ALU.mult, (b, "fo"))
                mine(b, "fo")
                tt(A(b, 4), A(b, 4), A(b, 8), ALU.add, (b, "fp"))
                mine(b, "fp")
                tt(A(b, 0), A(b, 4), Xin[b][:, :], ALU.add, (b, "xt"))
            for b in range(B):
                dve.wait_ge(*after("act", b, "lnf.r"))
                tt(A(b, 9), own(b, 1), A(b, 7), ALU.mult, (b, "lnf.x"))
            for b in range(B):
                dve.wait_ge(*after("pe", b, "w2"))
                stt(A(b, 0), own(b, 0), vec("b2"), A(b, 0), ALU.add, ALU.add, (b, "xt2"))
            for b in range(B):
                dve.wait_ge(*after("act", b, "lno.r"))
                tt(A(b, 9), own(b, 1), A(b, 7), ALU.mult, (b, "lno.x"))
            for b in range(B):
                dve.wait_ge(*after("act", b, "lno.g"))
                tt(A(b, 0), A(b, 10), Xin[b][:, :], ALU.add, (b, "s5"))
            for b in range(B):
                normed(b, "ln5", "X5", 1)

            for b in range(B):
                dve.wait_ge(*after("pe", b, "rt1"))
                lg = grid(own(b, 0)[:, 0:NT * E1], E1)
                red(S(b, 0, NT), lg, ALU.max, (b, "mx"))
                mine(b, "mx")
                tt(grid(S(b, 256, 32), E1), lg, over(S(b, 0, NT), [128, NT, E1], 2), ALU.subtract, (b, "ms"))
            for b in range(B):
                dve.wait_ge(*after("act", b, "rt1"))
                red(S(b, 4, NT), grid(S(b, 288, 32), E1), ALU.add, (b, "su"))
                mine(b, "su")
                inv(S(b, 4, NT), S(b, 4, NT), (b, "iv"))
                mine(b, "iv")
                tt(grid(S(b, 288, 32), E1), grid(S(b, 288, 32), E1), over(S(b, 4, NT), [128, NT, E1], 2), ALU.mult,
                   (b, "pr1"))
                mine(b, "pr1")
                pick(b, S(b, 288, 32), E1, "tri1", "1", True)
            experts(UB1, RB1, "el", "eu", "eu", "ew", "ew")
            for b in range(B):
                dve.wait_ge(*after("pe", b, f"ed{UB1}"))
                tt(A(b, 0), own(b, 3), Xin[b][:, :], ALU.add, (b, "s6"))
            for b in range(B):
                normed(b, "ln6", "X6", 0)

        @block.gpsimd
        def _(pool):
            def tt(out_, a, b_, op, step):
                nc.gpsimd.tensor_tensor(out_, a, b_, op).then_inc(*done("pool", *step))

            def ts(out_, a, s1, s2, op0, op1, step):
                nc.gpsimd.tensor_scalar(out_, a, s1, s2, op0, op1).then_inc(*done("pool", *step))

            def mine(lane, name):
                pool.wait_ge(*after("pool", lane, name))

            for b in range(B):
                nc.gpsimd.memset(Vaug[b][:, :, :, :], 1.0).then_inc(*done("pool", "w", f"va{b}"))
            pool.wait_ge(loads["vec"], 16)
            ts(fb_r, w("vec", "fb"), 0.0, None, ALU.max, ALU.bypass, ("w", "fb.r"))
            pool.wait_ge(*after("act", "w", "fb.l"))
            mine("w", "fb.r")
            tt(fb_r, fb_r, fb_l, ALU.add, ("w", "fb.s"))
            mine("w", "fb.s")
            ts(fcoef, fb_r, -4.0, None, ALU.mult, ALU.bypass, ("w", "fb.c"))
            ts(bhalf, w("vec", "bg"), 0.5, None, ALU.mult, ALU.bypass, ("w", "bh"))
            ts(bfilm, w("vec", "bfi"), vec("mg"), None, ALU.mult, ALU.bypass, ("w", "bf"))
            mine("w", "bf")
            scales = bfilm.rearrange("p (a two) -> p two a", two=2)[:, 0]
            ts(scales, scales, 1.0, None, ALU.add, ALU.bypass, ("w", "bf1"))

            pool.wait_ge(loads["s4d"], 16)
            pool.wait_ge(*after("act", "w", "dt"))
            tt(dct(1), w("s4d", "Are"), dct(0), ALU.mult, ("w", "zr"))
            tt(dct(2), w("s4d", "Aim"), dct(0), ALU.mult, ("w", "zi"))
            mine("w", "zi")
            ts(dct(4), dct(2), 1.0 / (2.0 * math.pi), None, ALU.mult, ALU.bypass, ("w", "u"))
            mine("w", "u")
            ts(dct(5), dct(4), 0.5, None, ALU.mult, ALU.bypass, ("w", "u2"))
            mine("w", "u2")
            ts(dct(6), dct(5), ROUND, None, ALU.add, ALU.bypass, ("w", "ka"))
            mine("w", "ka")
            ts(dct(6), dct(6), ROUND, None, ALU.subtract, ALU.bypass, ("w", "kb"))
            mine("w", "kb")
            tt(dct(5), dct(5), dct(6), ALU.subtract, ("w", "kc"))
            ts(dct(7), dct(4), ROUND, None, ALU.add, ALU.bypass, ("w", "kd"))
            mine("w", "kd")
            ts(dct(7), dct(7), ROUND, None, ALU.subtract, ALU.bypass, ("w", "ke"))
            mine("w", "ke")
            tt(dct(7), dct(4), dct(7), ALU.subtract, ("w", "kf"))
            for c in _HALF:
                d = slice(64 * c, 64 * c + 64)

                def spread(i, l):
                    return dct(i)[:, d].unsqueeze(2).to_broadcast([128, 64, l])

                def lags(name, l):
                    return w("s4d", name).unsqueeze(1).to_broadcast([128, 64, l])

                if c:
                    mine("w", "P0")
                tt(tb("tQ"), spread(4, PB_), lags("lb", PB_), ALU.mult, ("w", f"tQ{c}"))
                tt(tb("eQ"), spread(1, PB_), lags("lb", PB_), ALU.mult, ("w", f"aQ{c}"))
                tt(tb("tP"), spread(4, PA), lags("la", PA), ALU.mult, ("w", f"tP{c}"))
                tt(tb("eP"), spread(1, PA), lags("la", PA), ALU.mult, ("w", f"aP{c}"))
                mine("w", f"tQ{c}")
                ts(tb("tQ"), tb("tQ"), vec("phq"), None, ALU.add, ALU.bypass, ("w", f"kQ{c}"))
                mine("w", f"kQ{c}")
                ts(tb("gQ"), tb("tQ"), ROUND, ROUND, ALU.add, ALU.subtract, ("w", f"mQ{c}"))
                mine("w", f"mQ{c}")
                tt(tb("gQ"), tb("tQ"), tb("gQ"), ALU.subtract, ("w", f"gQ{c}"))
                ts(tb("g1"), tb("tP"), vec("ph1"), None, ALU.add, ALU.bypass, ("w", f"k1{c}"))
                mine("w", f"k1{c}")
                ts(tb("g2"), tb("g1"), ROUND, ROUND, ALU.add, ALU.subtract, ("w", f"n1{c}"))
                mine("w", f"n1{c}")
                tt(tb("g1"), tb("g1"), tb("g2"), ALU.subtract, ("w", f"g1{c}"))
                mine("w", f"g1{c}")
                ts(tb("g2"), tb("tP"), vec("ph2"), None, ALU.add, ALU.bypass, ("w", f"k2{c}"))
                mine("w", f"k2{c}")
                ts(tb("tP"), tb("g2"), ROUND, ROUND, ALU.add, ALU.subtract, ("w", f"n2{c}"))
                mine("w", f"n2{c}")
                tt(tb("g2"), tb("g2"), tb("tP"), ALU.subtract, ("w", f"g2{c}"))
                pool.wait_ge(*after("act", "w", f"sQ{c}"))
                tt(QT[:, d, :], tb("gQ"), tb("eQ"), ALU.mult, ("w", f"Q{c}"))
                pool.wait_ge(*after("act", "w", f"s2{c}"))
                tt(tb("g1"), tb("g1"), tb("eP"), ALU.mult, ("w", f"T1{c}"))
                tt(tb("g2"), tb("g2"), tb("eP"), ALU.mult, ("w", f"T2{c}"))
                mine("w", f"T2{c}")
                pool.wait_ge(*after("dve", "w", "dc26"))
                tt(tb("g1"), tb("g1"), spread(8, PA), ALU.mult, ("w", f"U1{c}"))
                tt(tb("g2"), tb("g2"), spread(5, PA), ALU.mult, ("w", f"U2{c}"))
                mine("w", f"U2{c}")
                tt(PT[:, d, :], tb("g1"), tb("g2"), ALU.add, ("w", f"P{c}"))

            for b in range(B):
                pool.wait_ge(*after("act", b, "sp"))
                pool.wait_ge(*after("dve", b, "rl"))
                tt(A(b, 8), A(b, 8), A(b, 7), ALU.add, (b, "dl"))
                mine(b, "dl")
                tt(A(b, 7), A(b, 8), Xin[b][:, :], ALU.mult, (b, "dx"))
            for i in range(NS):
                for b in range(B):
                    pool.wait_ge(*after("act", b, f"bb{i}"))
                    if i == 0:
                        mine(b, "dx")
                    tt(A(b, 4 + i % 2), A(b, 4 + i % 2), A(b, 7), ALU.mult, (b, f"by{i}"))

            for b in range(B):
                pool.wait_ge(*after("act", b, "lni.g"))
                tt(A(b, 10), A(b, 10), A(b, 4), ALU.mult, (b, "lni.z"))
                mine(b, "lni.z")
                tt(A(b, 2), A(b, 10), A(b, 5), ALU.add, (b, "xin"))

        for k, v in order.items():
            assert said[k] == len(v), (k, v[said[k]])


def lay_out(i):
    f4 = np.float32
    lay = layouts()
    a = {k: np.asarray(v) for k, v in i.items()}

    def bf16_words(table):
        return (np.ascontiguousarray(table, f4).view(np.uint32) >> 16).astype(np.uint16).view(f4)

    def pack(group, parts):
        d, n = lay[group]
        out = np.zeros((128, n), f4)
        assert set(parts) == set(d), (group, set(parts) ^ set(d))
        for name, v in parts.items():
            c, m = d[name]
            r0, v = v if isinstance(v, tuple) else (0, v)
            v = np.asarray(v).reshape(v.shape[0], -1)
            assert v.shape[1] == m and v.dtype == f4, (group, name, v.shape, m, v.dtype)
            out[r0:r0 + v.shape[0], c:c + m] = v
        return bf16_words(out) if group in BF_GROUPS else out

    def cols(v):
        return v.reshape(-1, 128).T

    def rows(v):
        return v.reshape(-1, 128, v.shape[1]).transpose(1, 0, 2).reshape(128, -1)

    def full(v, n=1):
        return np.broadcast_to(np.asarray(v, f4).reshape(1, -1), (128, n)).astype(f4)

    def halves(x, y):
        return np.repeat(np.array([x, y], f4), 64)[:, None]

    def tri(e):
        return full(np.tril(np.ones((e, e), f4), -1), e * e)

    bbc = np.concatenate([a["L1_attn_bb"], a["L1_attn_bc"]])
    wbc = np.concatenate([a["L1_attn_Wb"], a["L1_attn_Wc"]]).T
    out = {"x": a["x"].reshape(B * T, D).T}
    out["vec"] = pack("vec", {
        "g1": cols(a["L0_attn_gamma1"]), "g2": cols(a["L0_attn_gamma2"]),
        "cw": a["L0_attn_conv_w"].reshape(2, 128, 4).transpose(1, 0, 2), "cb": cols(a["L0_attn_conv_b"]),
        "bg": cols(a["L0_attn_b_gates"]), "fb": cols(a["L0_attn_forget_base"]), "bo": cols(a["L0_xattn_b_o"]),
        "wl1": cols(a["L0_ffn_w_ln1"]), "wl2": cols(a["L0_ffn_w_ln2"]), "A": a["L1_attn_A"],
        "bd": cols(a["L1_attn_bd"]), "bBC": np.tile(bbc, 3)[:, None], "gni": cols(a["L1_xattn_g_norm_in"]),
        "bni": cols(a["L1_xattn_b_norm_in"]), "gff": cols(a["L1_xattn_g_ffn"]), "bff": cols(a["L1_xattn_b_ffn"]),
        "gno": cols(a["L1_xattn_g_norm_out"]), "bno": cols(a["L1_xattn_b_norm_out"]), "b1": cols(a["L1_xattn_b1"]),
        "b2": cols(a["L1_xattn_b2"]),
        "bfi": cols(np.concatenate([a["L1_xattn_b_film_in"], a["L1_xattn_b_film_out"]])),
        "Ds": cols(a["L1_xattn_D_skip"]), "mg": full(a["L1_xattn_mod_gate"]), "eps": full(1e-5),
        "q25": full(0.25 * (1.0 + 1e-6)), "one": full(1.0), "phq": halves(0.25, 0.0), "ph1": halves(0.25, 0.5),
        "ph2": halves(0.5, 0.75),
        "rb": full(np.tile(a["L0_ffn_routing_bias"], NT), NT * E0), "tri0": tri(E0), "tri1": tri(E1)})
    out["hawk"] = pack("hawk", {
        "Win": a["L0_attn_W_in"].T, "Wga": rows(a["L0_attn_W_gates"].T), "Wou": rows(a["L0_attn_W_out"].T),
        "Wgr": a["L0_attn_W_grow"].T, "Wsh": rows(a["L0_attn_W_shrink"].T)})
    out["xa0"] = pack("xa0", {
        "Wk": a["L0_xattn_W_k"], "Wv": a["L0_xattn_W_v"], "WqT": rows(a["L0_xattn_W_q"].T),
        "Wo": rows(a["L0_xattn_W_o"]), "ctx": a["ctx_768"].reshape(B * J, CD).T})
    eye = np.eye(128, dtype=f4)
    out["sq"] = pack("sq", {"Cm": eye - f4(1 / 128), "ones": np.ones((128, 128), f4), "id": eye})

    half = HD // 2
    kv, q, kx, kr, ks = (np.zeros((r_, 128), f4) for r_ in (32, 32, 32, 128, 128))
    qs = np.zeros((32, 128), f4)
    turned = [(d + half // 2) % half for d in range(half)]
    for d in range(half):
        plain, rope, swap = (np.arange(NH) * half + e for e in (d, d, turned[d]))
        kx[:, NH * d:NH * d + NH] = a["L0_ffn_W_ku"][:, plain]
        q[:, NH * d:NH * d + NH] = a["L0_ffn_W_qu"][:, plain]
        r0 = NH * (half + d)
        kr[:, r0:r0 + NH] = a["L0_ffn_W_ropek"][:, rope]
        ks[:, r0:r0 + NH] = a["L0_ffn_W_ropek"][:, swap]
        q[:, r0:r0 + NH] = a["L0_ffn_W_ropeq"][:, rope]
        qs[:, r0:r0 + NH] = a["L0_ffn_W_ropeq"][:, swap]
    freq = (1.0 / 10000.0 ** (np.arange(0, half, 2, dtype=f4) / half)).astype(f4)
    angle = (np.arange(T, dtype=f4)[:, None] * freq[None, :]).astype(f4).astype(np.float64)
    cos, sin = np.ones((128, T)), np.zeros((128, T))
    for d in range(half):
        r0 = NH * (half + d)
        cos[r0:r0 + NH] = np.cos(angle[:, d % 2])
        sin[r0:r0 + NH] = np.sin(angle[:, d % 2]) * (-1 if d < half // 2 else 1)
    sc = HD ** -0.5
    out["mla"] = pack("mla", {
        "lat": np.concatenate([a["L0_ffn_W_kvd"], a["L0_ffn_W_qd"]], 1), "kx": kx, "kr": kr, "ks": ks,
        "q": (32, q), "qs": (32, qs), "v": a["L0_ffn_W_vu"], "o": a["L0_ffn_W_o"],
        "COSk": cos.astype(f4), "SINk": sin.astype(f4), "COSq": (cos * sc).astype(f4),
        "SINq": (sin * sc).astype(f4)})

    def experts(shared, routed):
        return np.concatenate([routed.transpose(1, 0, 2).reshape(128, -1), shared], 1)

    out["moe0"] = pack("moe0", {
        "g": experts(a["L0_ffn_Wg_s"], a["L0_ffn_Wg_r"]), "u": experts(a["L0_ffn_Wu_s"], a["L0_ffn_Wu_r"]),
        "d": rows(np.concatenate([a["L0_ffn_Wd_r"].reshape(-1, 128), a["L0_ffn_Wd_s"]])),
        "r": a["L0_ffn_W_router"]})
    out["late"] = pack("late", {
        "Wd": a["L1_attn_Wd"].T, "WBC": np.tile(wbc, (1, 3)), "WqT": a["L1_xattn_Wq"].T, "Wk": a["L1_xattn_Wk"],
        "Wv": a["L1_xattn_Wv"], "film": np.concatenate([a["L1_xattn_W_film_in"], a["L1_xattn_W_film_out"]], 1),
        "W1": a["L1_xattn_W1"], "W2": rows(a["L1_xattn_W2"]), "gate": a["L1_ffn_gate_w"].T})
    twice = {k: np.tile(a[f"L1_xattn_{v}"].T, (2, 1)) for k, v in
             (("Are", "A_re"), ("Aim", "A_im"), ("Cre", "C_re"), ("Cim", "C_im"))}
    out["s4d"] = pack("s4d", {**twice, "ldt": full(a["L1_xattn_log_dt"], 128), "lb": full(np.arange(PB_), PB_),
                              "la": full(np.arange(PA) * PB_, PA)})
    theta = 2 * np.pi * np.outer(np.arange(T), np.arange(NF) + 0.5) / (2 * T)
    F = np.concatenate([np.cos(theta), -np.sin(theta)], 1).astype(f4)
    G = (np.concatenate([np.cos(theta.T), -np.sin(theta.T)]) * (2 * 2 / (2 * T))).astype(f4)
    out["dft"] = pack("dft", {"F": rows(F), "G": rows(G)})

    def padded(v, axis):
        z = np.zeros([128 * UB1 - N1 if k == axis else n for k, n in enumerate(v.shape)], f4)
        return np.concatenate([v, z], axis)

    out["ffn1"] = pack("ffn1", {
        "g": padded(experts(a["L1_ffn_swg"], a["L1_ffn_wg"]), 1), "u": padded(experts(a["L1_ffn_swu"], a["L1_ffn_wu"]), 1),
        "d": rows(padded(np.concatenate([a["L1_ffn_wd"].reshape(-1, 128), a["L1_ffn_swd"]]), 0))})
    k = np.arange(128)
    low = np.where(k[:, None] < k[None, :], -BIG, 0.0).astype(f4)
    out["bf"] = pack("bf", {"id": eye, "mS": low, "mT": low.T,
                            "one": np.ones((128, 128), f4)})
    out["sel0"] = pack("sel0", {"s": np.tile(np.repeat(np.eye(E0, dtype=f4), 128, 1), (3, 1))})
    out["selA"] = pack("selA", {"s": np.tile(np.repeat(np.eye(2 * NS, dtype=f4), 128, 1), (3, 1))})
    out["sel1"] = pack("sel1", {"s": np.tile(np.repeat(np.eye(E1, dtype=f4), I1, 1), (3, 1))})
    out["ones"] = bf16_words(np.ones((KROWS - C6 * HD, NH * T)))

    def heads(m, h):
        return np.repeat(m.reshape(B, 1, J), h, 1).reshape(1, -1)

    m0, m1 = (a[f"mask_BxS2_{s}"].view(np.uint8) for s in ("bk0", "bf1"))
    out["km"] = np.repeat(heads(m0, H0), 128, 0)
    out["kr"] = np.concatenate([heads(m0, H0), heads(m1, H1)], 1)
    out["tm"] = a["mask_BxS_bf1"].view(np.uint8).reshape(B * NT, 128).T
    out = {k: np.ascontiguousarray(v) for k, v in out.items()}
    for k in ("km", "kr", "tm"):
        out[k] = out[k].view(np.uint32)
    return out


def kernel(**inputs):
    import concourse.bacc as bacc
    from concourse.bass_utils import run_bass_kernel_spmd as run

    arrays = lay_out(inputs)
    nc = bacc.Bacc("TRN2", target_bir_lowering=False, num_devices=1)
    dram = {n: nc.dram_tensor(f"in_{n}", v.shape, mybir.dt.from_np(v.dtype), kind="ExternalInput").ap()
            for n, v in arrays.items()}
    out = nc.dram_tensor("out", (D, B * T), F32, kind="ExternalOutput").ap()
    build(nc, dram, out)
    r = run(nc, [{f"in_{n}": v for n, v in arrays.items()}], core_ids=[0])
    return np.ascontiguousarray(r.results[0]["out"].T).reshape(B, T, D)
```

```python
import math
from contextlib import ExitStack

import concourse.bass as bass
import numpy as np
from concourse import mybir

F32 = mybir.dt.float32
BF16 = mybir.dt.bfloat16
U8 = mybir.dt.uint8
U32 = mybir.dt.uint32
ALU = mybir.AluOpType
ACT = mybir.ActivationFunctionType
X = mybir.AxisListType.X

B, T, D = 2, 512, 128
NT = T // 128
J = 32
CD = 96
H0, H1 = 8, 4
NH, HD = 16, 8
GH = 8
E0, E1 = 7, 8
U0 = E0 + 1
I1 = 176
R1 = E1 * I1
N1 = R1 + 2 * I1
UB1 = -(-N1 // 128)
RB1 = R1 // 128
NS = 16
PA, PB_ = 16, 32
NF = 512
NFB = NF // 128
BIG = 2.0 ** 100
TWO_PI = 6.283184
ROUND = 1.5 * 2.0 ** 23
C6 = 6
KROWS = C6 * HD + 3


def _ln(t):
    return [f"{t}.sq", f"{t}.l", f"{t}.r"]


_U = list(range(U0))
_N = list(range(NS))
_K = list(range(UB1))
_HP = list(range(NH // 2))
_ATT_PE = [x for h in range(NH // 2) for x in
           [f"st{h}.X", f"st{h}.Y", f"st{h}.Z"] + ([f"vp{h - 1}"] if h else [])] + [f"vp{NH // 2 - 1}"]
STEPS = {
    "pe": [
        "h1.ss", "z0", "z1", "z2", "z3", "g0", "g1", "g2", "g3", "rg", "h4.ss", "gr0", "gr1", "gr2", "gr3", "shr",
        "ln1.c", "ln1.v", "xa.s0", "xa.s1", "xa.t0", "xa.t1", "xa.o", "ln2.c", "ln2.v",
        "m1.ss", "lat", "kf", "q0", "q1", "v",
        *[f"mx{h}.{u}" for h in _HP for u in "ABCDE"], "nmt",
        *_ATT_PE, "yt", "mo",
        "f1.ss", "rt", "wt", *[f"{n}{u}" for u in range(U0 + 1) for n in ("fg", "fu", "fw", "fd")
                               if not (u == 0 and n == "fd") and not (u == U0 and n != "fd")
                               and not (u == U0 - 1 and n == "fw")],
        "ln3.c", "ln3.v", "bc", "de", *[f"{n}{i}" for i in range(NS + 1) for n in ("bn", "cn", "yn")
                                        if not (i == 0 and n == "yn") and not (i == NS and n != "yn")],
        "ln4.c", "ln4.v", "xb.s", "xb.t", "fl0", "fl1", "fl2", "fl3", "lni.c", "lni.v", "xit",
        "inv", "lnf.c", "lnf.v", "w10", "w11", "w12", "w13", "w2", "lno.c", "lno.v", "ln5.c", "ln5.v",
        "rt1", "wt1", *[f"{n}{k}" for k in range(UB1 + 1) for n in ("eg", "eu", "ew", "ed")
                        if not (k == 0 and n == "ed") and not (k == UB1 and n != "ed")
                        and not (k >= RB1 and n == "ew")],
        "ln6.c", "ln6.v"],
    "act": [
        "h1.sq", "h1.l", "h1.r", "cv0", "cv1", "gg0", "gg1", "tf0", "tf1", "ti0", "ti1",
        "al0", "al1", "sa0", "sa1", "lb0", "lb1", "hb0", "hb1", "h4.sq", "h4.l", "h4.r", "gm0", "gm1", *_ln("ln1"),
        "xa.e0", "xa.e1", "xa.a0", "xa.a1", *_ln("ln2"), "m1.sq", "m1.l", "m1.n", "m1.m", "m1.r", "lat",
        "kh", "km", "qh", "qm", "v", "nmt", *[f"st{h}.{u}" for h in _HP for u in "XYZ"], "yt",
        "f1.sq", "f1.l", "f1.n", "f1.m", "f1.r", "rt", "wt", *[f"sl{u}" for u in _U], *_ln("ln3"),
        "bc", "ab", "ex", "sp", *[f"{n}{i}" for i in _N for n in ("aa", "bb")], *_ln("ln4"),
        "xb.e", "xb.a", "s0", "s1", "s2", "s3", *_ln("lni"), "lni.g", "xit", *_ln("lnf"), "lnf.g",
        "u0", "u1", "u2", "u3", *_ln("lno"), "lno.g", *_ln("ln5"), "rt1", "wt1", *[f"el{k}" for k in _K],
        *_ln("ln6")],
    "dve": [
        "xn1", "cw0.2", "cw1.2", "cw0.1", "cw1.1", "cw0.0", "cw1.0", "in0", "in1", "xs0", "xs1", "h0", "h1",
        "gh0", "gh1", "x1", "xx", "xn2", "hm0", "hm1", "s1", "X1",
        "xa.m0", "xa.d0", "xa.m1", "xa.d1", "xa.u0", "xa.i0", "xa.p0", "xa.u1", "xa.i1", "xa.p1", "s2", "X2",
        "xm", "k1", "k2", "kk", "kr", "kl", "q1", "q2", "qq", "qr", "ql",
        *[f"mx{h}.{u}" for h in _HP for u in "ABCDE"], "nh", "nr", "nm", "nl",
        *[f"{n}{g}" for g in range(NH // GH) for n in ("ri", "y")], "x2a", "x2x",
        "xf", "lg", "pd", "pr", "gt", "ge", "gx", "gm", "rk", "we", "ws", "wi", "wn", "wh", "wr", "wm", "wl",
        *[f"{n}{u}" for u in _U for n in ("hu", "hw") if not (u == U0 - 1 and n == "hw")], "s3", "X3",
        "bh", "br", "bm", "bs", "bl", "rl", *[f"{n}{i}" for i in _N for n in ("sc", "hc")], "s4", "X4",
        "xb.m", "xb.d", "xb.u", "xb.i", "xb.k", "xb.p", "lni.x", "sk", "fo", "fp", "xt",
        "lnf.x", "xt2", "lno.x", "s5", "X5",
        "mx", "ms", "su", "iv", "pr1", "gt1", "ge1", "gx1", "gm1", "rk1", "we1", "ws1", "wa1", "wi1", "wn1",
        "wh1", "wr1", "wm1", "wl1",
        *[f"{n}{k}" for k in _K for n in ("eu", "ew") if not (k >= RB1 and n == "ew")], "s6", "X6"],
    "pool": ["dl", "dx", *[f"by{i}" for i in _N], "lni.z", "xin"],
}
_HALF = (0, 1)
STEPS_W = {
    "pe": ["kv", "m0", "v0", "k1", "m1", "f0", "f1", "kp0", "kp1", "kp2", "kp3", "kt", "kf0", "kf1",
           *[f"xf{c}{i}" for c in _HALF for i in _HALF]],
    "act": ["fb.a", "fb.e", "fb.l", "dt", "kv0", "kv", "th", "sh", "sy", "s1", "s2", "v0", "k1", "vr", "eP", "eQ",
            "sQ", "kp0", "kp1", "kp2", "kp3", "kl", "kf0", "kf1"],
    "dve": ["km", "kb0", "kb1", "tm", *[f"z{i}" for i in range(1, 10)], "tP", "r1", "q1", "r2", "q2", "aP",
            "m0a", "m0b", *[f"dc{i}" for i in range(1, 27)], "U1", "U2", "V", "P", "m1", "VF0", "VF1",
            *[f"{n}{c}" for c in _HALF for n in ("rr", "ii", "ri", "ir", "yr", "yi")]],
    "pool": ["va0", "va1", "fb.r", "fb.s", "fb.c", "bh", "bf", "bf1", "aQ", "tQ",
             *[f"{n}{c}" for c in _HALF for n in ("rQ", "sQ", "qQ")], "Q"],
}


def layouts():
    groups = {
        "vec": [("g1", 1), ("g2", 1), ("cw", 8), ("cb", 2), ("bg", 4), ("fb", 2), ("bo", 1), ("wl1", 1), ("wl2", 1),
                ("A", NS), ("bd", 1), ("bBC", 1), ("gni", 1), ("bni", 1), ("gff", 1), ("bff", 1), ("gno", 1),
                ("bno", 1), ("b1", 4), ("b2", 1), ("bfi", 4), ("Ds", 1), ("mg", 1), ("eps", 1), ("q25", 1),
                ("one", 1), ("phq", 1), ("ph1", 1), ("ph2", 1), ("raq", 1), ("ra1", 1), ("ra2", 1), ("rb", NT * E0), ("tri0", E0 * E0),
                ("tri1", E1 * E1)],
        "hawk": [("Wga", 1024), ("Wou", 256), ("Wgr", 512), ("Wsh", 256)],
        "win": [("Win", 512)],
        "xa0": [("Wk", 512), ("Wv", 512), ("WqT", 512), ("Wo", 512), ("ctx", B * J)],
        "sq": [("Cm", 128), ("ones", 128), ("id", 128)],
        "mla": [("lat", 64), ("kx", 128), ("kr", 128), ("ks", 128), ("q", 128), ("qs", 128), ("v", 128), ("o", 128),
                ("COSk", T), ("SINk", T), ("COSq", T), ("SINq", T)],
        "moe0": [("g", 128 * U0), ("u", 128 * U0), ("d", 128 * U0), ("r", E0)],
        "late": [("Wd", 128), ("WBC", 96), ("WqT", 128), ("Wk", 128), ("Wv", 128), ("film", 512), ("W1", 512),
                 ("W2", 512), ("gate", E1)],
        "s4d": [("Are", 128), ("Aim", 128), ("Cre", 128), ("Cim", 128), ("ldt", 128), ("lb", PB_), ("la", PA)],
        "dft": [("F", NT * 2 * NF), ("G", 2 * NF // 128 * T)],
        "ffn1": [("g", 128 * UB1), ("u", 128 * UB1), ("d", 128 * UB1)],
        "bf": [("id", 128), ("mS", 128), ("mT", 128), ("one", 128)],
        "sel0": [("s", 128 * E0)],
        "selA": [("s", 128 * 2 * NS)],
        "sel1": [("s", 128 * RB1)],
    }
    out = {}
    for g, items in groups.items():
        at, d = 0, {}
        for name, n in items:
            d[name] = (at, n)
            at += n
        out[g] = (d, at)
    return out


BF_GROUPS = ("bf", "sel0", "selA", "sel1")


def build(nc, dram, out):
    lay = layouts()
    with ExitStack() as ctx:
        def sb(name, shape, dt=F32):
            return ctx.enter_context(nc.sbuf_tensor(name, shape, dt))

        lanes = (0, 1, "w")
        sems = {(e, l): ctx.enter_context(nc.semaphore(f"{e}_steps_{l}")) for e in STEPS for l in lanes}
        order = {(e, l): (STEPS_W if l == "w" else STEPS)[e] for e in STEPS for l in lanes}
        place = {k: {n: i + 1 for i, n in enumerate(v)} for k, v in order.items()}
        for k, v in order.items():
            assert len(place[k]) == len(v), k
        said = {k: 0 for k in order}

        def done(engine, lane, name):
            k = (engine, lane)
            assert place[k][name] == said[k] + 1, (k, name, "expected", order[k][said[k]])
            said[k] += 1
            return sems[k], 1

        def after(engine, lane, name):
            return sems[engine, lane], place[engine, lane][name]

        loads = {n: ctx.enter_context(nc.semaphore(f"load_{n}")) for n in
                 ["x0", "x1", "vec", "win", "hawk", "xa0", "sq", "mla", "moe0", "late", "s4d", "dft", "ffn1", "bf", "sel0",
                  "selA", "sel1", "km", "kr", "tm"]}
        stack = {(w, b): ctx.enter_context(nc.semaphore(f"stack_{w}{b}")) for w in "kqm" for b in range(B)}
        kshuf = ctx.enter_context(nc.semaphore("kernel_rows_moved"))
        stored = ctx.enter_context(nc.semaphore("stored"))

        PS = ctx.enter_context(nc.psum_tensor("PS", [128, 8, T], F32))
        RA = sb("RA", [128, lay["win"][1] + lay["hawk"][1] + lay["xa0"][1]])
        RR = sb("RR", [128, 16384])
        SL = 16
        AR = [sb(f"AR{b}", [128, SL, T]) for b in range(B)]

        def flat(b, i, j):
            return AR[b][:, i:j, :].rearrange("p a t -> p (a t)")

        tiles = {}
        for g, (d, n) in lay.items():
            if g == "hawk":
                tiles[g] = RA[:, 0:n]
            elif g == "xa0":
                tiles[g] = RA[:, lay["hawk"][1]:lay["hawk"][1] + n]
            elif g == "win":
                at = lay["hawk"][1] + lay["xa0"][1]
                tiles[g] = RA[:, at:at + n]
            elif g == "moe0":
                tiles[g] = RA[:, 0:n]
            elif g == "sel0":
                at = lay["moe0"][1] + 1
                tiles[g] = RA[:, at:at + n // 2]
            elif g == "dft":
                tiles[g] = RR[:, 0:n]
            elif g == "ffn1":
                tiles[g] = RR[:, 8192:8192 + n]
            elif g == "selA":
                tiles[g] = RR[:, 13600:13600 + n // 2]
            elif g == "sel1":
                tiles[g] = RR[:, 15648:15648 + n // 2]
            elif g == "s4d":
                tiles[g] = flat(1, 14, 16)[:, 0:n]
            else:
                tiles[g] = sb(f"W_{g}", [128, n // (2 if g in BF_GROUPS else 1)])[:, :]

        def w(group, name, a=0, n=None):
            c, full = lay[group][0][name]
            t = tiles[group].bitcast(BF16) if group in BF_GROUPS else tiles[group]
            return t[:, c + a:c + a + (full if n is None else n)]

        def vec(name, i=0):
            return w("vec", name, i, 1)

        Xin = [sb(f"x_in{b}", [128, T]) for b in range(B)]
        kmask_w, krow_w, tmask_w = (sb("kmask", [128, B * H0 * J // 4], U32), sb("krow", [1, B * (H0 + H1) * J // 4], U32),
                                    sb("tmask", [128, B * NT // 4], U32))
        kmask, krow, tmask = (m[:, :].bitcast(U8) for m in (kmask_w, krow_w, tmask_w))
        tmaskf = sb("tmaskf", [128, B * NT])
        krowb = sb("krowb", [1, B * (H0 + H1) * J], BF16)
        pre = flat(0, 11, 14)
        kmaskf, KTs, VTs, K1s, Vrep = (pre[:, 0:512], pre[:, 512:768], pre[:, 768:1024], pre[:, 1024:1088],
                                       pre[:, 1088:1344])
        M0 = sb("M0", [128, B, H0 * J])
        V0 = sb("V0", [128, B, 2, 128])
        M1 = sb("M1", [128, B, H1 * J])
        VF = sb("VF", [128, B, 512])
        small = sb("small", [128, 64])
        fcoef, bhalf, bfilm = small[:, 0:2], small[:, 2:6], small[:, 6:10]
        fb_r, fb_a, fb_e, fb_l = small[:, 10:12], small[:, 12:14], small[:, 14:16], small[:, 16:18]
        st = [sb(f"stats{b}", [128, 1024]) for b in range(B)]
        spb = [sb(f"parts{b}", [128, NT, 48], BF16) for b in range(B)]
        wT = [sb(f"wT{b}", [48, T], BF16) for b in range(B)]
        Vaug = [sb(f"Vaug{b}", [128, NT, NH, HD + 1]) for b in range(B)]
        KL = sb("KL", [128, NT, 128])
        Kf = sb("Kf", [128, 2, NFB, 128])

        QT = RR[:, 0:4096].rearrange("p (d l) -> p d l", l=PB_)
        PT = RR[:, 4096:6144].rearrange("p (d l) -> p d l", l=PA)
        Ksb = RR[:, 6144:7168]
        Kdl = RR[:, 7168:7680]

        KV = [[RR[:, (2 * b + i) * 4096:(2 * b + i + 1) * 4096].bitcast(BF16).rearrange("p (h t) -> p h t", h=NH)
               for b in range(B)] for i in range(2)]
        Kst, Qst = KV
        P = [flat(s_, 11, 16) for s_ in range(2)]
        XT = flat(0, 11, 13).rearrange("p (j b d) -> p j b d", j=NT, b=B)
        Yf = flat(1, 11, 15).rearrange("p (c f n) -> p c f n", c=2, f=NFB)
        Zt = flat(0, 13, 15).rearrange("p (c n) -> p c n", c=2)

        def A(b, i):
            return AR[b][:, i, :]

        def S(b, c, n):
            return st[b][:, c:c + n]

        def dct(i):
            return flat(1, 11, 14)[:, 128 * i:128 * i + 128]

        def tb(name):
            at, l = {"tQ": (6144, PB_), "rQ": (10240, PB_), "p1": (12288, PA), "p2": (14336, PA)}[name]
            n = 64 if name == "rQ" else 128
            return RR[:, at:at + n * l].rearrange("p (d l) -> p d l", l=l)

        def bank(i):
            return PS[:, i, :]

        def own(b, i):
            return PS[:, 4 * b + i, :]

        def grid(ap, k):
            return ap.rearrange("p (a k) -> p a k", k=k)

        def over(ap, shape, at):
            return ap.unsqueeze(at).to_broadcast(shape)

        half = [[flat(b, 8, 11)[:, 256 * i:256 * i + 256].bitcast(BF16) for i in range(6)] for b in range(B)]
        KP = [half[b][0:3] for b in range(B)]
        QP = [half[b][3:6] for b in range(B)]

        M1_BANKS = (3, 6, 7, 1)

        block = ctx.enter_context(nc.Block())

        @block.sync
        def _(sp):
            def load(name, dst, src=None):
                sp.dma_start(dst, dram[name] if src is None else src).then_inc(loads[name], 16)

            load("x0", Xin[0][:, :], dram["x"][:, 0:T])
            load("sq", tiles["sq"])
            load("vec", tiles["vec"])
            load("win", tiles["win"])
            load("x1", Xin[1][:, :], dram["x"][:, T:2 * T])
            load("s4d", tiles["s4d"])
            load("km", kmask_w[:, :])
            load("kr", krow_w[:, :])
            load("tm", tmask_w[:, :])
            load("xa0", tiles["xa0"])
            load("hawk", tiles["hawk"])
            load("late", tiles["late"])
            load("bf", tiles["bf"])
            load("mla", tiles["mla"])

            def parts(which, b):
                dst, hi, mid, lo, rows = {
                    "k": (Kst[b], KP[b][0], KP[b][1], KP[b][2], "hmhlhm"),
                    "q": (Qst[b], QP[b][0], QP[b][1], QP[b][2], "hhmhlm")}[which]
                for c, part in enumerate(rows):
                    src = {"h": hi, "m": mid, "l": lo}[part]
                    sp.dma_start(dst[c * HD:(c + 1) * HD, :, :], src).then_inc(stack[which, b], 16)

            sp.wait_ge(*after("act", "w", "kp3"))
            for a in range(PA):
                sp.dma_start(Kdl[:, PB_ * a:PB_ * a + PB_],
                             Ksb[a:128:32, :].rearrange("p (d l) -> p d l", l=PB_)).then_inc(kshuf, 16)
            for b in range(B):
                sp.wait_ge(*after("pe", "w", "kt"))
                if b == 0:
                    for q in range(B):
                        sp.dma_start(RR[C6 * HD:KROWS, 8192 * q:8192 * q + 4096], dram["ones"])\
                            .then_inc(stack["k", q], 16)
                sp.wait_ge(*after("dve", b, "kl"))
                parts("k", b)
                sp.wait_ge(*after("dve", b, "ql"))
                parts("q", b)
            for b in range(B):
                sp.wait_ge(*after("pe", b, "xa.o"))
            load("moe0", tiles["moe0"])
            load("sel0", tiles["sel0"])
            for b in range(B):
                sp.wait_ge(*after("act", b, "nmt"))
                sp.dma_start(Qst[b][C6 * HD:KROWS, :, :], wT[b][:, :]).then_inc(stack["m", b], 16)
            for b in range(B):
                sp.wait_ge(*after("pe", b, f"st{NH // 2 - 1}.Z"))
            load("selA", tiles["selA"])
            load("dft", tiles["dft"])
            load("ffn1", tiles["ffn1"])
            load("sel1", tiles["sel1"])
            for b in range(B):
                sp.wait_ge(*after("dve", b, "X6"))
                sp.dma_start(out[:, b * T:(b + 1) * T], Xin[b][:, :]).then_inc(stored, 16)
            sp.wait_ge(stored, 16 * B)

        @block.tensor
        def _(pe):
            mm, tr = nc.tensor.matmul, nc.tensor.transpose

            def layernorm(b, t, ready, i=0):
                pe.wait_ge(*ready)
                mm(own(b, i), w("sq", "Cm"), A(b, 0), start=True, stop=True).then_inc(*done("pe", b, f"{t}.c"))
                pe.wait_ge(*after("act", b, f"{t}.sq"))
                mm(own(b, i + 1), w("sq", "ones"), A(b, 1), start=True, stop=True).then_inc(*done("pe", b, f"{t}.v"))

            def squares(b, t, i):
                pe.wait_ge(*after("act", b, f"{t}.sq"))
                mm(own(b, i), w("sq", "ones"), A(b, 1), start=True, stop=True).then_inc(*done("pe", b, f"{t}.ss"))

            def kernel_products(q, first):
                pe.wait_ge(*after("dve", "w", "P"))
                pe.wait_ge(*after("pool", "w", "Q"))
                for i in range(32):
                    d = 32 * q + i
                    last = mm(bank(first + i // 16)[32 * q:32 * q + PA, PB_ * (i % 16):PB_ * (i % 16) + PB_],
                              PT[:, d, :], QT[:, d, :], start=True, stop=True)
                last.then_inc(*done("pe", "w", f"kp{q}"))

            ctxT = w("xa0", "ctx")
            pe.wait_ge(loads["sq"], 16)
            for b in range(B):
                squares(b, "h1", 0)
            pe.wait_ge(loads["win"], 16)
            for b in range(B):
                pe.wait_ge(*after("dve", b, "xn1"))
                for i, blk in enumerate((2, 3, 0, 1)):
                    mm(own(b, i), w("win", "Win", 128 * blk, 128), A(b, 2), start=True, stop=True)\
                        .then_inc(*done("pe", b, f"z{i}"))
            pe.wait_ge(loads["xa0"], 16)
            pe.wait_ge(*after("act", 0, "gg1"))
            for i, name in enumerate(("Wk", "Wv")):
                for blk in range(4):
                    last = mm(bank(2 + i)[:, blk * 64:blk * 64 + 64], w("xa0", name, 128 * blk, 128)[0:CD, :],
                              ctxT[0:CD, :], start=True, stop=True)
            last.then_inc(*done("pe", "w", "kv"))
            pe.wait_ge(*after("act", "w", "kv"))
            pe.wait_ge(*after("act", 1, "gg1"))
            for par in range(2):
                p0 = 64 * par
                for blk in range(4):
                    last = mm(bank(6 + par)[:, blk * 64:blk * 64 + 64], w("xa0", "WqT", 128 * blk, 128)[p0:p0 + 64, :],
                              KTs[p0:p0 + 64, blk * 64:blk * 64 + 64], start=True, stop=True)
            last.then_inc(*done("pe", "w", "m0"))
            pe.wait_ge(loads["hawk"], 16)
            for b in range(B):
                pe.wait_ge(*after("dve", b, "cw1.0"))
                for o in range(4):
                    if o == 2 and b:
                        pe.wait_ge(*after("dve", "w", "m0b"))
                    for k in range(2):
                        last = mm(own(b, o), w("hawk", "Wga", 512 * k + 128 * o, 128), A(b, 5 + k),
                                  start=(k == 0), stop=(k == 1))
                    last.then_inc(*done("pe", b, f"g{o}"))
            for b in range(B):
                pe.wait_ge(*after("act", b, "ti1"))
            for par in range(2):
                p0 = 64 * par
                for b in range(B):
                    for blk in range(4):
                        q = 32 * ((2 * blk + par) % 4)
                        c = (b * 2 + blk // 2) * 128
                        last = mm(bank((1, 5)[par])[q:q + 32, c:c + 128],
                                  grid(VTs, 64)[p0:p0 + 64, blk, b * J:b * J + J],
                                  w("xa0", "Wo", 128 * blk, 128)[p0:p0 + 64, :], start=True, stop=True)
            last.then_inc(*done("pe", "w", "v0"))
            pe.wait_ge(loads["late"], 16)
            mm(bank(2)[:, 0:64], w("late", "Wk")[0:CD, :], ctxT[0:CD, :], start=True, stop=True)
            mm(bank(2)[:, 64:128], w("late", "Wv")[0:CD, :], ctxT[0:CD, :], start=True, stop=True)\
                .then_inc(*done("pe", "w", "k1"))
            pe.wait_ge(*after("act", "w", "v0"))
            pe.wait_ge(*after("act", "w", "k1"))
            for h in range(H1):
                p0 = 32 * h
                last = mm(bank(M1_BANKS[h])[:, 0:64], w("late", "WqT")[p0:p0 + 32, :], K1s[p0:p0 + 32, :], start=True,
                          stop=True)
            last.then_inc(*done("pe", "w", "m1"))
            pe.wait_ge(*after("act", "w", "vr"))
            for b in range(B):
                mm(bank((2, 5)[b]), Vrep[:, 128 * b:128 * b + 128], w("late", "film"), start=True, stop=True)\
                    .then_inc(*done("pe", "w", f"f{b}"))
            for b in range(B):
                for k in range(2):
                    pe.wait_ge(*after("dve", b, f"gh{k}"))
                    last = mm(own(b, 0), w("hawk", "Wou", 128 * k, 128), A(b, 3 + k), start=(k == 0), stop=(k == 1))
                last.then_inc(*done("pe", b, "rg"))
            pe.wait_ge(*after("dve", "w", "m1"))
            pe.wait_ge(*after("dve", "w", "VF1"))
            for b in range(B):
                squares(b, "h4", 1)
            kernel_products(0, 2)
            kernel_products(1, 6)
            for b in range(B):
                pe.wait_ge(*after("dve", b, "xn2"))
                pe.wait_ge(*after("act", "w", f"kp{b}"))
                for i, blk in enumerate((0, 1, 2, 3)):
                    mm(own(b, i), w("hawk", "Wgr", 128 * blk, 128), A(b, 2), start=True, stop=True)\
                        .then_inc(*done("pe", b, f"gr{i}"))
            for b in range(B):
                for k in range(2):
                    pe.wait_ge(*after("dve", b, f"hm{k}"))
                    last = mm(own(b, 0), w("hawk", "Wsh", 128 * k, 128), A(b, 3 + k), start=(k == 0), stop=(k == 1))
                last.then_inc(*done("pe", b, "shr"))
            for b in range(B):
                layernorm(b, "ln1", after("dve", b, "s1"), 1)

            pe.wait_ge(loads["bf"], 16)
            pe.wait_ge(*after("dve", "w", "kb1"))
            for b in range(B):
                pe.wait_ge(*after("dve", b, "X1"))
                for p in range(2):
                    for i in range(2):
                        c = own(b, p)[:, 256 * i:256 * i + 256]
                        mm(c, Xin[b][:, 128 * (2 * p + i):128 * (2 * p + i) + 128], M0[:, b, :], start=True, stop=False)
                        last = mm(c, w("bf", "one")[0:1, :], krowb[:, 256 * b:256 * b + 256], start=False, stop=True)
                    last.then_inc(*done("pe", b, f"xa.s{p}"))
            kernel_products(2, 2)
            kernel_products(3, 6)
            for b in range(B):
                pe.wait_ge(*after("act", "w", f"kp{2 + b}"))
                for p in range(2):
                    pe.wait_ge(*after("dve", b, f"xa.p{p}"))
                    for g in range(2):
                        for i in range(2):
                            tt = 128 * (2 * p + i)
                            last = tr(own(b, 2 + g)[:, tt:tt + 128],
                                      A(b, 2 + p)[:, 256 * i + 128 * g:256 * i + 128 * g + 128], w("sq", "id"))
                    last.then_inc(*done("pe", b, f"xa.t{p}"))
            for b in range(B):
                for g in range(2):
                    pe.wait_ge(*after("act", b, f"xa.a{g}"))
                    last = mm(own(b, 0), V0[:, b, g, :], A(b, 4 + g), start=(g == 0), stop=(g == 1))
                last.then_inc(*done("pe", b, "xa.o"))
            for b in range(B):
                layernorm(b, "ln2", after("dve", b, "s2"), 1)

            pe.wait_ge(kshuf, 16 * PA)
            pe.wait_ge(*after("act", 0, "xa.a1"))
            for j in range(NT):
                last = tr(bank(3)[:, 128 * j:128 * j + 128], Kdl[:, 128 * j:128 * j + 128], w("sq", "id"))
            last.then_inc(*done("pe", "w", "kt"))

            pe.wait_ge(loads["mla"], 16)
            for b in range(B):
                squares(b, "m1", 0)
            pe.wait_ge(*after("act", "w", "kl"))
            for b in range(B):
                pe.wait_ge(*after("dve", b, "xm"))
                mm(own(b, 1)[0:64, :], w("mla", "lat"), A(b, 2), start=True, stop=True).then_inc(*done("pe", b, "lat"))
                mm(own(b, 2), w("mla", "kr"), A(b, 2), start=True, stop=False)
                mm(own(b, 3), w("mla", "ks"), A(b, 2), start=True, stop=True)
                pe.wait_ge(*after("act", b, "lat"))
                mm(own(b, 2), w("mla", "kx")[0:32, :], A(b, 3)[0:32, :], start=False, stop=True)\
                    .then_inc(*done("pe", b, "kf"))
                mm(own(b, 0), w("mla", "q")[32:64, :], A(b, 3)[32:64, :], start=True, stop=True)\
                    .then_inc(*done("pe", b, "q0"))
                mm(own(b, 1), w("mla", "qs")[32:64, :], A(b, 3)[32:64, :], start=True, stop=True)\
                    .then_inc(*done("pe", b, "q1"))
                pe.wait_ge(*after("dve", b, "k2"))
                for i in range(NT):
                    last = mm(own(b, 3)[:, 128 * i:128 * i + 128], A(b, 3)[0:32, 128 * i:128 * i + 128],
                              w("mla", "v")[0:32, :], start=True, stop=True)
                last.then_inc(*done("pe", b, "v"))

            def max_unit(b, pair, u):
                hs = (2 * pair, 2 * pair + 1)
                n = 5 * pair + "ABCDE".index(u)
                ring = bank(n % 2)
                if n >= 2:
                    pe.wait_ge(*after("dve", b, f"mx{(n - 2) // 5}.{'ABCDE'[(n - 2) % 5]}"))
                segs = {"A": [(hs[0], 3, 0)], "B": [(hs[0], 2, 0), (hs[0], 0, 384)],
                        "C": [(hs[1], 3, 0)], "D": [(hs[1], 2, 0), (hs[1], 0, 384)],
                        "E": [(hs[0], 1, 0), (hs[1], 1, 256)]}[u]
                rows = C6 * HD
                for h, qt, c in segs:
                    n_ = 128 * (qt + 1)
                    mm(ring[:, c:c + n_], Qst[b][0:rows, h, 128 * qt:128 * qt + 128], Kst[b][0:rows, h, 0:n_],
                       start=True, stop=False)
                    last = mm(ring[:, c + n_ - 128:c + n_], w("bf", "id"), w("bf", "mS"), start=False, stop=True)
                last.then_inc(*done("pe", b, f"mx{pair}.{u}"))

            def score_unit(b, pair, u):
                hs = (2 * pair, 2 * pair + 1)
                first = {"X": 2, "Y": 4, "Z": 6}[u]
                if pair:
                    pe.wait_ge(*after("act", b, f"st{pair - 1}.{u}"))
                segs = {"X": [(hs[0], 0, 0), (hs[0], 1, 512), (hs[0], 3, 896)],
                        "Y": [(hs[1], 0, 0), (hs[1], 1, 512), (hs[1], 3, 896)],
                        "Z": [(hs[0], 2, 0), (hs[1], 2, 256)]}[u]
                for h, kb, c in segs:
                    n_ = T - 128 * kb
                    o = bank(first + c // T)[:, c % T:c % T + n_]
                    mm(o, Kst[b][0:KROWS, h, 128 * kb:128 * kb + 128], Qst[b][0:KROWS, h, 128 * kb:T],
                       start=True, stop=False)
                    last = mm(o[:, 0:128], w("bf", "id"), w("bf", "mT"), start=False, stop=True)
                last.then_inc(*done("pe", b, f"st{pair}.{u}"))

            def values(b, pair):
                g = 2 * pair // GH
                if 2 * pair % GH == 0:
                    if g:
                        pe.wait_ge(*after("dve", b, f"y{g - 1}"))
                    elif b:
                        pe.wait_ge(*after("dve", 0, f"y{NH // GH - 1}"))
                pe.wait_ge(*after("act", b, f"st{pair}.Z"))
                base = {0: (0, 0), 1: (512, 0), 3: (896, 0)}
                for i in range(2):
                    h = 2 * pair + i
                    for qt in range(NT):
                        for kb in range(qt + 1):
                            col = (2048 + 256 * i if kb == 2 else 1024 * i + base[kb][0]) + 128 * (qt - kb)
                            c = (qt * GH + h % GH) * (HD + 1)
                            last = mm(bank(7)[:, c:c + HD + 1], P[pair % 2][:, col:col + 128], Vaug[b][:, kb, h, :],
                                      start=(kb == 0), stop=(kb == qt))
                last.then_inc(*done("pe", b, f"vp{pair}"))

            def minus_max(b):
                pe.wait_ge(*after("dve", b, "nl"))
                for i in range(NT):
                    last = tr(bank(0).bitcast(BF16)[0:48, 128 * i:128 * i + 128], spb[b][:, i, :], w("bf", "id"))
                last.then_inc(*done("pe", b, "nmt"))

            def attention_out(b):
                for g in range(NH // GH):
                    pe.wait_ge(*after("dve", b, f"y{g}"))
                for i in range(NT):
                    last = tr(bank(0)[:, 128 * i:128 * i + 128], A(b, 4)[:, 128 * i:128 * i + 128], w("sq", "id"))
                last.then_inc(*done("pe", b, "yt"))
                pe.wait_ge(*after("act", b, "yt"))
                mm(bank(1), w("mla", "o"), A(b, 5), start=True, stop=True).then_inc(*done("pe", b, "mo"))

            for b in range(B):
                pe.wait_ge(*after("act", b, "v"))
                pe.wait_ge(*after("dve", b, "q2"))
            pe.wait_ge(stack["k", 0], 16 * 7)
            pe.wait_ge(stack["q", 0], 16 * 6)
            for pair in _HP:
                for u in "ABCDE":
                    max_unit(0, pair, u)
            minus_max(0)
            pe.wait_ge(stack["k", 1], 16 * 7)
            pe.wait_ge(stack["q", 1], 16 * 6)
            pe.wait_ge(*after("act", 0, "nmt"))
            for pair in _HP:
                if pair == 1:
                    pe.wait_ge(stack["m", 0], 16)
                for u in "ABCDE":
                    max_unit(1, pair, u)
                if pair >= 1:
                    for u in "XYZ":
                        score_unit(0, pair - 1, u)
                if pair >= 2:
                    values(0, pair - 2)
            minus_max(1)
            for u in "XYZ":
                score_unit(0, NH // 2 - 1, u)
            values(0, NH // 2 - 2)
            values(0, NH // 2 - 1)
            pe.wait_ge(*after("act", 1, "nmt"))
            attention_out(0)
            pe.wait_ge(stack["m", 1], 16)
            for u in "XYZ":
                pe.wait_ge(*after("act", 0, f"st{NH // 2 - 1}.{u}"))
            for pair in _HP:
                for u in "XYZ":
                    score_unit(1, pair, u)
                if pair >= 1:
                    values(1, pair - 1)
            values(1, NH // 2 - 1)
            pe.wait_ge(*after("dve", 0, "x2a"))
            attention_out(1)

            def route(b, r, group, name, n, i):
                for t in range(NT):
                    last = mm(own(b, i)[:, n * t:n * t + n], A(b, 2)[:, 128 * t:128 * t + 128], w(group, name),
                              start=True, stop=True)
                last.then_inc(*done("pe", b, r))

            def turn_weights(b, name, ready, n, i):
                pe.wait_ge(*ready)
                for t in range(NT):
                    last = tr(own(b, i).bitcast(BF16)[0:n, 128 * t:128 * t + 128], spb[b][:, t, 0:n], w("bf", "id"))
                last.then_inc(*done("pe", b, name))

            pe.wait_ge(loads["moe0"], 16)
            pe.wait_ge(loads["sel0"], 16)
            pe.wait_ge(*after("dve", 1, "x2a"))
            for b in range(B):
                squares(b, "f1", 0)
            for b in range(B):
                pe.wait_ge(*after("dve", b, "xf"))
                route(b, "rt", "moe0", "r", E0, 1)
            for b in range(B):
                turn_weights(b, "wt", after("dve", b, "wl"), 3 * E0, 2)

            def unit(b, k, last_k, routed, group, sel, rows, x, n):
                g, u, ww, d = n
                if k <= last_k:
                    if k:
                        pe.wait_ge(*after("act", b, f"{ {'fg': 'sl', 'eg': 'el'}[g] }{k - 1}"))
                    mm(own(b, 0), w(group, "g", 128 * k, 128), x, start=True, stop=True)\
                        .then_inc(*done("pe", b, f"{g}{k}"))
                    if k:
                        pe.wait_ge(*after("dve", b, f"{ {'fu': 'hu', 'eu': 'eu'}[u] }{k - 1}"))
                    mm(own(b, 1), w(group, "u", 128 * k, 128), x, start=True, stop=True)\
                        .then_inc(*done("pe", b, f"{u}{k}"))
                    if k < routed:
                        if k:
                            pe.wait_ge(*after("dve", b, f"{ {'fw': 'hw', 'ew': 'ew'}[ww] }{k - 1}"))
                        mm(own(b, 2), w(sel, "s", 128 * k, 128)[0:rows, :], wT[b][0:rows, :], start=True, stop=True)\
                            .then_inc(*done("pe", b, f"{ww}{k}"))
                if k:
                    j = k - 1
                    h = ({'fd': 'hw', 'ed': 'ew'} if j < routed else {'fd': 'hu', 'ed': 'eu'})[d]
                    pe.wait_ge(*after("dve", b, f"{h}{j}"))
                    mm(own(b, 3), w(group, "d", 128 * j, 128), A(b, 6 + j % 2), start=(j == 0), stop=(j == last_k))\
                        .then_inc(*done("pe", b, f"{d}{k}"))

            for b in range(B):
                pe.wait_ge(*after("act", b, "wt"))
            for k in range(U0 + 1):
                for b in range(B):
                    unit(b, k, U0 - 1, E0, "moe0", "sel0", 3 * E0, A(b, 2), ("fg", "fu", "fw", "fd"))
            for b in range(B):
                layernorm(b, "ln3", after("dve", b, "s3"), 0)

            pe.wait_ge(loads["selA"], 16)
            for b in range(B):
                pe.wait_ge(*after("dve", b, "X3"))
                mm(own(b, 0)[0:96, :], w("late", "WBC"), Xin[b][:, :], start=True, stop=True)\
                    .then_inc(*done("pe", b, "bc"))
                mm(own(b, 1), w("late", "Wd"), Xin[b][:, :], start=True, stop=True).then_inc(*done("pe", b, "de"))
            for b in range(B):
                pe.wait_ge(*after("dve", b, "bl"))
                pe.wait_ge(*after("dve", b, "rl"))
            for i in range(NS + 1):
                for b in range(B):
                    parts_bc = A(b, 3)[:, 0:256].bitcast(BF16)
                    if i < NS:
                        if i:
                            pe.wait_ge(*after("act", b, f"bb{i - 1}"))
                        mm(own(b, 0), w("selA", "s", 128 * i, 128)[0:96, :], parts_bc[0:96, :], start=True, stop=True)\
                            .then_inc(*done("pe", b, f"bn{i}"))
                        if i:
                            pe.wait_ge(*after("dve", b, f"hc{i - 1}"))
                        mm(own(b, 1), w("selA", "s", 128 * (NS + i), 128)[0:96, :], parts_bc[0:96, :], start=True,
                           stop=True).then_inc(*done("pe", b, f"cn{i}"))
                    if i:
                        pe.wait_ge(*after("dve", b, f"hc{i - 1}"))
                        mm(own(b, 2), w("sq", "id"), A(b, 12 + (i - 1) % 2), start=(i == 1), stop=(i == NS))\
                            .then_inc(*done("pe", b, f"yn{i}"))
            for b in range(B):
                layernorm(b, "ln4", after("dve", b, "s4"), 0)

            for b in range(B):
                pe.wait_ge(*after("dve", b, "X4"))
            pe.wait_ge(loads["dft"], 16)

            def forward(o, c, f, rhs):
                for j in range(NT):
                    last = mm(o, w("dft", "F", 1024 * j + 512 * c + 128 * f, 128), rhs(j), start=(j == 0),
                              stop=(j == NT - 1))
                return last

            for c in range(2):
                for f in range(NFB):
                    last = forward(bank(c)[:, 128 * f:128 * f + 128], c, f, lambda j: KL[:, j, :])
                last.then_inc(*done("pe", "w", f"kf{c}"))

            for b in range(B):
                for i in range(NT):
                    c = own(b, 2)[:, 128 * i:128 * i + 128]
                    mm(c, Xin[b][:, 128 * i:128 * i + 128], M1[:, b, :], start=True, stop=False)
                    last = mm(c, w("bf", "one")[0:1, :], krowb[:, 512 + 128 * b:640 + 128 * b], start=False, stop=True)
                last.then_inc(*done("pe", b, "xb.s"))
            for b in range(B):
                pe.wait_ge(*after("dve", b, "xb.p"))
                for i in range(NT):
                    last = tr(own(b, 3)[:, 128 * i:128 * i + 128], A(b, 2)[:, 128 * i:128 * i + 128], w("sq", "id"))
                last.then_inc(*done("pe", b, "xb.t"))
            pe.wait_ge(*after("act", "w", "kf1"))
            for b in range(B):
                pe.wait_ge(*after("act", b, "xb.a"))
                for o in range(4):
                    mm(own(b, o), VF[:, b, 128 * o:128 * o + 128], A(b, 3), start=True, stop=True)\
                        .then_inc(*done("pe", b, f"fl{o}"))
            for b in range(B):
                pe.wait_ge(*after("act", b, "s1"))
                mm(own(b, 0), w("sq", "Cm"), Xin[b][:, :], start=True, stop=True).then_inc(*done("pe", b, "lni.c"))
                pe.wait_ge(*after("act", b, "lni.sq"))
                mm(own(b, 1), w("sq", "ones"), A(b, 1), start=True, stop=True).then_inc(*done("pe", b, "lni.v"))
            for b in range(B):
                pe.wait_ge(*after("pool", b, "xin"))
                pe.wait_ge(*after("act", b, "s3"))
                for j in range(NT):
                    last = tr(own(b, 2)[:, 128 * j:128 * j + 128], A(b, 2)[:, 128 * j:128 * j + 128], w("sq", "id"))
                last.then_inc(*done("pe", b, "xit"))

            for b in range(B):
                pe.wait_ge(*after("act", b, "xit"))
                pe.wait_ge(*after("dve", b, "lni.x"))
            for h in range(2):
                for c in range(2):
                    for f in range(2):
                        last = forward(bank(4 * h + 2 * c)[:, 256 * f:256 * f + 256], c, 2 * h + f,
                                       lambda j: XT[:, j, :, :].rearrange("p b d -> p (b d)"))
                    last.then_inc(*done("pe", "w", f"xf{h}{c}"))
            pe.wait_ge(*after("dve", "w", "yi1"))
            for b in range(B):
                n = 0
                for c in range(2):
                    for f in range(NFB):
                        last = mm(own(b, 0), Yf[:, c, f, 128 * b:128 * b + 128],
                                  w("dft", "G", (NFB * c + f) * T, T), start=(n == 0), stop=(n == 2 * NFB - 1))
                        n += 1
                last.then_inc(*done("pe", b, "inv"))
            for b in range(B):
                layernorm(b, "lnf", after("dve", b, "xt"), 1)
            for b in range(B):
                pe.wait_ge(*after("act", b, "lnf.g"))
                for o in range(4):
                    mm(own(b, o), w("late", "W1", 128 * o, 128), A(b, 2), start=True, stop=True)\
                        .then_inc(*done("pe", b, f"w1{o}"))
            for b in range(B):
                for k in range(4):
                    pe.wait_ge(*after("act", b, f"u{k}"))
                    last = mm(own(b, 0), w("late", "W2", 128 * k, 128), A(b, 6 + k), start=(k == 0), stop=(k == 3))
                last.then_inc(*done("pe", b, "w2"))
            for b in range(B):
                layernorm(b, "lno", after("dve", b, "xt2"), 1)
            for b in range(B):
                layernorm(b, "ln5", after("dve", b, "s5"), 1)

            for b in range(B):
                pe.wait_ge(*after("dve", b, "X5"))
                for t in range(NT):
                    last = mm(own(b, 0)[:, E1 * t:E1 * t + E1], Xin[b][:, 128 * t:128 * t + 128], w("late", "gate"),
                              start=True, stop=True)
                last.then_inc(*done("pe", b, "rt1"))
            for b in range(B):
                turn_weights(b, "wt1", after("dve", b, "wl1"), 3 * E1, 1)
            pe.wait_ge(loads["ffn1"], 16)
            pe.wait_ge(loads["sel1"], 16)
            for b in range(B):
                pe.wait_ge(*after("act", b, "wt1"))
            for k in range(UB1 + 1):
                for b in range(B):
                    unit(b, k, UB1 - 1, RB1, "ffn1", "sel1", 3 * E1, Xin[b][:, :], ("eg", "eu", "ew", "ed"))
            for b in range(B):
                layernorm(b, "ln6", after("dve", b, "s6"), 0)

        @block.scalar
        def _(act):
            def f(out_, in_, func, step, bias=0.0, scale=1.0):
                nc.scalar.activation(out_, in_, func, bias=bias, scale=scale).then_inc(*done("act", *step))

            def inverse_deviation(b, t, src, stat):
                act.wait_ge(*after("pe", b, f"{t}.c"))
                f(A(b, 1), src, ACT.Square, (b, f"{t}.sq"))
                act.wait_ge(*after("pe", b, f"{t}.v"))
                f(A(b, 7), stat, ACT.Ln, (b, f"{t}.l"), scale=1.0 / D, bias=vec("eps"))
                act.wait_ge(*after("act", b, f"{t}.l"))
                f(A(b, 7), A(b, 7), ACT.Exp, (b, f"{t}.r"), scale=-0.5)

            def layernorm(t, i=0):
                for b in range(B):
                    inverse_deviation(b, t, own(b, i), own(b, i + 1))

            def root_mean_square(t, i, bias=None):
                for b in range(B):
                    act.wait_ge(*after("pe", b, f"{t}.ss"))
                    f(A(b, 7), own(b, i), ACT.Ln, (b, f"{t}.l"), scale=1.0 / D)
                    act.wait_ge(*after("act", b, f"{t}.l"))
                    if bias is None:
                        f(A(b, 7), A(b, 7), ACT.Exp, (b, f"{t}.r"), scale=-0.5)
                    else:
                        f(A(b, 7), A(b, 7), ACT.Exp, (b, f"{t}.n"), scale=0.5)
                        act.wait_ge(*after("act", b, f"{t}.n"))
                        f(A(b, 7), A(b, 7), ACT.Ln, (b, f"{t}.m"), bias=bias)
                        act.wait_ge(*after("act", b, f"{t}.m"))
                        f(A(b, 7), A(b, 7), ACT.Exp, (b, f"{t}.r"), scale=-1.0)

            def table(name):
                nc.scalar.preload_act_table_set(
                    {"exp": "natural_log_exp_and_others", "gelu": "gelu_and_others", "silu": "silu_and_others"}[name])

            table("exp")
            for b in range(B):
                act.wait_ge(loads[f"x{b}"], 16)
                f(A(b, 1), Xin[b][:, :], ACT.Square, (b, "h1.sq"))
            act.wait_ge(loads["vec"], 16)
            f(fb_a, w("vec", "fb"), ACT.Abs, ("w", "fb.a"))
            act.wait_ge(*after("act", "w", "fb.a"))
            f(fb_e, fb_a, ACT.Exp, ("w", "fb.e"), scale=-1.0)
            act.wait_ge(*after("act", "w", "fb.e"))
            f(fb_l, fb_e, ACT.Ln, ("w", "fb.l"), bias=vec("one"))
            act.wait_ge(loads["s4d"], 16)
            f(dct(0), w("s4d", "ldt"), ACT.Exp, ("w", "dt"))
            root_mean_square("h1", 0)

            table("gelu")
            for b in range(B):
                for k in range(2):
                    act.wait_ge(*after("pe", b, f"z{k}"))
                    f(A(b, 5 + k), own(b, k), ACT.Identity, (b, f"cv{k}"), scale=vec("cw", 4 * k + 3), bias=vec("cb", k))
                for k in range(2):
                    act.wait_ge(*after("pe", b, f"z{2 + k}"))
                    f(A(b, 3 + k), own(b, 2 + k), ACT.Gelu, (b, f"gg{k}"))
            act.wait_ge(*after("pe", "w", "kv"))
            f(KTs, bank(2)[:, 0:256], ACT.Copy, ("w", "kv0"))
            f(VTs, bank(3)[:, 0:256], ACT.Copy, ("w", "kv"))
            table("silu")
            act.wait_ge(*after("dve", "w", "z9"))
            f(dct(3), dct(1), ACT.Tanh, ("w", "th"), scale=0.5)
            f(dct(6), dct(5), ACT.Sin, ("w", "sh"), scale=TWO_PI)
            f(dct(7), dct(7), ACT.Sin, ("w", "sy"), scale=TWO_PI)
            act.wait_ge(*after("dve", "w", "q2"))
            f(tb("p1"), tb("p1"), ACT.Sin, ("w", "s1"), scale=-TWO_PI, bias=vec("ra1"))
            f(tb("p2"), tb("p2"), ACT.Sin, ("w", "s2"), scale=-TWO_PI, bias=vec("ra2"))
            act.wait_ge(*after("pool", "w", "bh"))
            act.wait_ge(*after("pool", "w", "fb.c"))
            for b in range(B):
                for o, name in enumerate(("tf0", "tf1", "ti0", "ti1")):
                    act.wait_ge(*after("pe", b, f"g{o}"))
                    f(A(b, 7 + o), own(b, o), ACT.Tanh, (b, name), scale=0.5, bias=bhalf[:, o:o + 1])
            table("exp")
            for b in range(B):
                for k in range(2):
                    act.wait_ge(*after("act", b, f"tf{k}"))
                    f(A(b, 7 + k), A(b, 7 + k), ACT.Exp, (b, f"al{k}"), scale=fcoef[:, k:k + 1], bias=fcoef[:, k:k + 1])
                for k in range(2):
                    act.wait_ge(*after("act", b, f"al{k}"))
                    f(A(b, 1 + k), A(b, 7 + k), ACT.Square, (b, f"sa{k}"))
                for k in range(2):
                    act.wait_ge(*after("act", b, f"sa{k}"))
                    f(A(b, 1 + k), A(b, 1 + k), ACT.Ln, (b, f"lb{k}"), scale=-0.25, bias=vec("q25"))
                for k in range(2):
                    act.wait_ge(*after("act", b, f"lb{k}"))
                    f(A(b, 1 + k), A(b, 1 + k), ACT.Exp, (b, f"hb{k}"), scale=0.5)
                if b == 0:
                    act.wait_ge(*after("pe", "w", "v0"))
                    for q in range(4):
                        last = nc.scalar.activation(V0[32 * q:32 * q + 32, :, :, :].rearrange("p b g n -> p (b g n)"),
                                                    bank((1, 5)[q % 2])[32 * q:32 * q + 32, :], ACT.Copy)
                    last.then_inc(*done("act", "w", "v0"))
                    act.wait_ge(*after("pe", "w", "k1"))
                    f(K1s, bank(2)[:, 0:64], ACT.Copy, ("w", "k1"))
                    for c in range(B):
                        last = nc.scalar.activation(Vrep[:, 128 * c:128 * c + 128].rearrange("p (h g) -> p h g", g=J),
                                                    over(bank(2)[:, 64 + J * c:64 + J * c + J], [128, H1, J], 1),
                                                    ACT.Copy)
                    last.then_inc(*done("act", "w", "vr"))
            act.wait_ge(*after("dve", "w", "aP"))
            f(PT, PT, ACT.Exp, ("w", "eP"))
            act.wait_ge(*after("pool", "w", "aQ"))
            f(QT, QT, ACT.Exp, ("w", "eQ"))
            table("silu")
            act.wait_ge(*after("pool", "w", "qQ1"))
            f(tb("tQ"), tb("tQ"), ACT.Sin, ("w", "sQ"), scale=-TWO_PI, bias=vec("raq"))
            table("exp")
            for b in range(B):
                act.wait_ge(*after("dve", b, "x1"))
                f(A(b, 1), A(b, 5), ACT.Square, (b, "h4.sq"))
            root_mean_square("h4", 1)
            table("gelu")

            def kernel_rows(q, first):
                act.wait_ge(*after("pe", "w", f"kp{q}"))
                f(Ksb[32 * q:32 * q + PA, :], PS[32 * q:32 * q + PA, first:first + 2, :].rearrange("p a t -> p (a t)"),
                  ACT.Copy, ("w", f"kp{q}"))

            kernel_rows(0, 2)
            kernel_rows(1, 6)
            for b in range(B):
                for k in range(2):
                    act.wait_ge(*after("pe", b, f"gr{k}"))
                    f(A(b, 3 + k), own(b, k), ACT.Gelu, (b, f"gm{k}"))
            table("exp")
            layernorm("ln1", 1)

            kernel_rows(2, 2)
            kernel_rows(3, 6)
            for b in range(B):
                for p in range(2):
                    act.wait_ge(*after("dve", b, f"xa.d{p}"))
                    f(A(b, 2 + p), A(b, 2 + p), ACT.Exp, (b, f"xa.e{p}"))
            for b in range(B):
                act.wait_ge(*after("pe", b, "xa.t1"))
                for g in range(2):
                    f(A(b, 4 + g), own(b, 2 + g), ACT.Copy, (b, f"xa.a{g}"))
            layernorm("ln2", 1)

            for b in range(B):
                act.wait_ge(*after("dve", b, "X2"))
                f(A(b, 1), Xin[b][:, :], ACT.Square, (b, "m1.sq"))
            act.wait_ge(*after("pe", "w", "kt"))
            f(KL[:, :, :].rearrange("p j d -> p (j d)"), bank(3), ACT.Copy, ("w", "kl"))
            root_mean_square("m1", 0, vec("eps"))
            for b in range(B):
                act.wait_ge(*after("pe", b, "lat"))
                f(A(b, 3)[0:64, :], own(b, 1)[0:64, :], ACT.Copy, (b, "lat"))
            for b in range(B):
                act.wait_ge(*after("dve", b, "kk"))
                f(KP[b][0], A(b, 5), ACT.Copy, (b, "kh"))
                act.wait_ge(*after("dve", b, "kr"))
                f(KP[b][1], A(b, 6), ACT.Copy, (b, "km"))
                act.wait_ge(*after("dve", b, "qq"))
                f(QP[b][0], A(b, 4), ACT.Copy, (b, "qh"))
                act.wait_ge(*after("dve", b, "qr"))
                f(QP[b][1], A(b, 1), ACT.Copy, (b, "qm"))
                act.wait_ge(*after("pe", b, "v"))
                act.wait_ge(*after("pool", "w", f"va{b}"))
                f(Vaug[b][:, :, :, 0:HD], own(b, 3).rearrange("p (i h d) -> p i h d", i=NT, d=HD), ACT.Copy, (b, "v"))

            def parts_of_max(b):
                act.wait_ge(*after("pe", b, "nmt"))
                f(wT[b][0:48, :], bank(0).bitcast(BF16)[0:48, 0:T], ACT.Copy, (b, "nmt"))

            def probabilities(b, pair):
                s_ = pair % 2
                for u, (b0, n, c) in {"X": (2, 2, 0), "Y": (4, 2, 1024), "Z": (6, 1, 2048)}.items():
                    act.wait_ge(*after("pe", b, f"st{pair}.{u}"))
                    if u == "X":
                        if pair >= 2:
                            act.wait_ge(*after("pe", b, f"vp{pair - 2}"))
                        elif b:
                            act.wait_ge(*after("pe", 0, f"vp{NH // 2 - 2 + pair}"))
                    f(P[s_][:, c:c + n * T], PS[:, b0:b0 + n, :].rearrange("p a t -> p (a t)"), ACT.Exp,
                      (b, f"st{pair}.{u}"))

            parts_of_max(0)
            for pair in range(NH // 2 - 1):
                probabilities(0, pair)
            parts_of_max(1)
            probabilities(0, NH // 2 - 1)

            def attention_out(b):
                act.wait_ge(*after("pe", b, "yt"))
                f(A(b, 5), bank(0), ACT.Copy, (b, "yt"))

            attention_out(0)
            for pair in _HP:
                probabilities(1, pair)
            attention_out(1)

            for b in range(B):
                act.wait_ge(*after("dve", b, "x2a"))
                f(A(b, 1), A(b, 3), ACT.Square, (b, "f1.sq"))
            root_mean_square("f1", 0, vec("eps"))
            for b in range(B):
                act.wait_ge(*after("dve", b, "lg"))
                f(S(b, 288, 28), S(b, 256, 28), ACT.Exp, (b, "rt"), scale=-1.0)
            for b in range(B):
                act.wait_ge(*after("pe", b, "wt"))
                f(wT[b][0:3 * E0, :], own(b, 2).bitcast(BF16)[0:3 * E0, 0:T], ACT.Copy, (b, "wt"))
            table("silu")
            for k in range(U0):
                for b in range(B):
                    act.wait_ge(*after("pe", b, f"fg{k}"))
                    if k >= 2:
                        act.wait_ge(*after("dve", b, f"hu{k - 2}"))
                    f(A(b, 4 + k % 2), own(b, 0), ACT.Silu, (b, f"sl{k}"))
            table("exp")
            layernorm("ln3")

            for b in range(B):
                act.wait_ge(*after("pe", b, "bc"))
                f(A(b, 2)[0:96, :], own(b, 0)[0:96, :], ACT.Identity, (b, "bc"), bias=vec("bBC")[0:96, :])
                act.wait_ge(*after("pe", b, "de"))
                f(A(b, 7), own(b, 1), ACT.Abs, (b, "ab"), bias=vec("bd"))
                act.wait_ge(*after("act", b, "ab"))
                f(A(b, 7), A(b, 7), ACT.Exp, (b, "ex"), scale=-1.0)
                act.wait_ge(*after("act", b, "ex"))
                f(A(b, 7), A(b, 7), ACT.Ln, (b, "sp"), bias=vec("one"))
            for i in range(NS):
                for b in range(B):
                    if i == 0:
                        act.wait_ge(*after("pool", b, "dl"))
                    if i >= 2:
                        act.wait_ge(*after("dve", b, f"sc{i - 2}"))
                    f(A(b, 9 + i % 2), A(b, 8), ACT.Exp, (b, f"aa{i}"), scale=w("vec", "A", i, 1))
                    act.wait_ge(*after("pe", b, f"bn{i}"))
                    f(A(b, 4 + i % 2), own(b, 0), ACT.Copy, (b, f"bb{i}"))
            layernorm("ln4")
            for c in range(2):
                act.wait_ge(*after("pe", "w", f"kf{c}"))
                f(Kf[:, c, :, :].rearrange("p f d -> p (f d)"), bank(c), ACT.Copy, ("w", f"kf{c}"))

            for b in range(B):
                act.wait_ge(*after("dve", b, "xb.d"))
                f(A(b, 2), A(b, 2), ACT.Exp, (b, "xb.e"))
            for b in range(B):
                act.wait_ge(*after("pe", b, "xb.t"))
                f(A(b, 3), own(b, 3), ACT.Copy, (b, "xb.a"))
            act.wait_ge(*after("pool", "w", "bf1"))
            for b in range(B):
                for o, to in enumerate((4, 5, 6, 8)):
                    act.wait_ge(*after("pe", b, f"fl{o}"))
                    f(A(b, to), own(b, o), ACT.Identity, (b, f"s{o}"), bias=bfilm[:, o:o + 1])

            def affine(b, t, src, dst, g, off):
                act.wait_ge(*after("dve", b, f"{t}.x"))
                f(A(b, dst), A(b, src), ACT.Identity, (b, f"{t}.g"), scale=vec(g), bias=vec(off))

            for b in range(B):
                inverse_deviation(b, "lni", own(b, 0), own(b, 1))
            for b in range(B):
                affine(b, "lni", 9, 10, "gni", "bni")
            for b in range(B):
                act.wait_ge(*after("pe", b, "xit"))
                f(XT[:, :, b, :], own(b, 2).rearrange("p (j d) -> p j d", d=128), ACT.Copy, (b, "xit"))
            layernorm("lnf", 1)
            for b in range(B):
                affine(b, "lnf", 9, 2, "gff", "bff")
            table("gelu")
            for b in range(B):
                for k in range(4):
                    act.wait_ge(*after("pe", b, f"w1{k}"))
                    f(A(b, 6 + k), own(b, k), ACT.Gelu, (b, f"u{k}"), bias=vec("b1", k))
            table("exp")
            layernorm("lno", 1)
            for b in range(B):
                affine(b, "lno", 9, 10, "gno", "bno")
            layernorm("ln5", 1)

            for b in range(B):
                act.wait_ge(*after("dve", b, "ms"))
                f(S(b, 288, 32), S(b, 256, 32), ACT.Exp, (b, "rt1"))
            for b in range(B):
                act.wait_ge(*after("pe", b, "wt1"))
                f(wT[b][0:3 * E1, :], own(b, 1).bitcast(BF16)[0:3 * E1, 0:T], ACT.Copy, (b, "wt1"))
            table("silu")
            for k in range(UB1):
                for b in range(B):
                    act.wait_ge(*after("pe", b, f"eg{k}"))
                    if k >= 2:
                        act.wait_ge(*after("dve", b, f"eu{k - 2}"))
                    f(A(b, 4 + k % 2), own(b, 0), ACT.Silu, (b, f"el{k}"))
            table("exp")
            layernorm("ln6")

        @block.vector
        def _(dve):
            def tt(out_, a, b_, op, step):
                nc.vector.tensor_tensor(out_, a, b_, op).then_inc(*done("dve", *step))

            def ts(out_, a, s1, s2, op0, op1, step):
                nc.vector.tensor_scalar(out_, a, s1, s2, op0, op1).then_inc(*done("dve", *step))

            def stt(out_, a, s1, b_, op0, op1, step):
                nc.vector.scalar_tensor_tensor(out_, a, s1, b_, op0, op1).then_inc(*done("dve", *step))

            def red(out_, a, op, step):
                nc.vector.tensor_reduce(out_, a, X, op).then_inc(*done("dve", *step))

            def inv(out_, a, step):
                nc.vector.reciprocal(out_, a).then_inc(*done("dve", *step))

            def mine(lane, name):
                dve.wait_ge(*after("dve", lane, name))

            def normed(b, t, name, i, x=None):
                dve.wait_ge(*after("act", b, f"{t}.r"))
                tt(Xin[b][:, :], own(b, i), A(b, 7), ALU.mult, (b, name))

            for n in ("km", "kr", "tm"):
                dve.wait_ge(loads[n], 16)
            nc.vector.tensor_copy(kmaskf, kmask).then_inc(*done("dve", "w", "km"))
            nc.vector.tensor_copy(krowb[:, :], krow).then_inc(*done("dve", "w", "kb0"))
            mine("w", "kb0")
            ts(krowb[:, :], krowb[:, :], -1.0, BIG, ALU.add, ALU.mult, ("w", "kb1"))
            nc.vector.tensor_copy(tmaskf[:, :], tmask).then_inc(*done("dve", "w", "tm"))

            link = [0]

            def chain(prefix, op, *a):
                link[0] += 1
                op(*a, ("w", f"{prefix}{link[0]}"))
                mine("w", f"{prefix}{link[0]}")

            for b in range(B):
                dve.wait_ge(*after("act", b, "h1.r"))
                stt(A(b, 2), Xin[b][:, :], vec("g1"), A(b, 7), ALU.mult, ALU.mult, (b, "xn1"))
            dve.wait_ge(*after("act", "w", "dt"))
            chain("z", tt, dct(1), w("s4d", "Are"), dct(0), ALU.mult)
            chain("z", tt, dct(2), w("s4d", "Aim"), dct(0), ALU.mult)
            chain("z", ts, dct(4), dct(2), 1.0 / (2.0 * math.pi), None, ALU.mult, ALU.bypass)
            chain("z", ts, dct(5), dct(4), 0.5, None, ALU.mult, ALU.bypass)
            chain("z", ts, dct(6), dct(5), ROUND, None, ALU.add, ALU.bypass)
            chain("z", stt, dct(6), dct(6), ROUND, dct(5), ALU.subtract, ALU.subtract)
            chain("z", ts, dct(5), dct(6), -1.0, None, ALU.mult, ALU.bypass)
            chain("z", ts, dct(7), dct(4), ROUND, ROUND, ALU.add, ALU.subtract)
            chain("z", tt, dct(7), dct(4), dct(7), ALU.subtract)

            def spread(i, l):
                return dct(i).unsqueeze(2).to_broadcast([128, 128, l])

            lags = w("s4d", "la").unsqueeze(1).to_broadcast([128, 128, PA])

            def turns(to, ph, r_, q_):
                mine("w", "tP")
                ts(PT, tb("p2"), vec(ph), ROUND, ALU.add, ALU.add, ("w", r_))
                mine("w", r_)
                stt(tb(to), PT, ROUND, tb("p2"), ALU.subtract, ALU.subtract, ("w", q_))

            tt(tb("p2"), spread(4, PA), lags, ALU.mult, ("w", "tP"))
            turns("p1", "ph1", "r1", "q1")
            for b in range(B):
                for tap in (2, 1, 0):
                    for k in range(2):
                        if tap == 2:
                            dve.wait_ge(*after("act", b, f"cv{k}"))
                        else:
                            mine(b, f"cw{k}.{tap + 1}")
                        n = T - (3 - tap)
                        stt(A(b, 5 + k)[:, 3 - tap:T], own(b, k)[:, 0:n], vec("cw", 4 * k + tap),
                            A(b, 5 + k)[:, 3 - tap:T], ALU.mult, ALU.add, (b, f"cw{k}.{tap}"))
            mine("w", "q1")
            turns("p2", "ph2", "r2", "q2")
            mine("w", "q2")
            tt(PT, spread(1, PA), lags, ALU.mult, ("w", "aP"))
            mine("w", "km")
            dve.wait_ge(*after("pe", "w", "m0"))
            for par in range(2):
                for b in range(B):
                    last = nc.vector.scalar_tensor_tensor(
                        M0[:, b, :].rearrange("p (k two j) -> p two k j", two=2, j=J)[:, par],
                        bank(6 + par)[:, 0:256].rearrange("p (k b j) -> p b k j", b=B, j=J)[:, b], 64.0 ** -0.5,
                        kmaskf.rearrange("p (b k two j) -> p b two k j", b=B, two=2, j=J)[:, b, par],
                        ALU.mult, ALU.mult)
                last.then_inc(*done("dve", "w", "m0" + "ab"[par]))
            Are, Aim, Cre, Cim = (w("s4d", k) for k in ("Are", "Aim", "Cre", "Cim"))
            dve.wait_ge(*after("act", "w", "sy"))
            link[0] = 0
            chain("dc", ts, dct(8), dct(3), -1.0, 1.0, ALU.mult, ALU.add)
            chain("dc", inv, dct(8), dct(8))
            chain("dc", stt, dct(8), dct(3), 2.0, dct(8), ALU.mult, ALU.mult)
            chain("dc", tt, dct(9), dct(6), dct(6), ALU.mult)
            chain("dc", ts, dct(3), dct(9), -2.0, 1.0, ALU.mult, ALU.add)
            chain("dc", tt, dct(3), dct(3), dct(8), ALU.mult)
            chain("dc", stt, dct(3), dct(9), -2.0, dct(3), ALU.mult, ALU.add)
            chain("dc", stt, dct(10), dct(8), 1.0, dct(7), ALU.add, ALU.mult)
            chain("dc", tt, dct(11), Are, Are, ALU.mult)
            chain("dc", tt, dct(9), Aim, Aim, ALU.mult)
            chain("dc", tt, dct(11), dct(11), dct(9), ALU.add)
            chain("dc", inv, dct(11), dct(11))
            chain("dc", tt, dct(6), Cre, dct(3), ALU.mult)
            chain("dc", tt, dct(7), Cim, dct(10), ALU.mult)
            chain("dc", tt, dct(6), dct(6), dct(7), ALU.subtract)
            chain("dc", tt, dct(7), Cre, dct(10), ALU.mult)
            chain("dc", tt, dct(9), Cim, dct(3), ALU.mult)
            chain("dc", tt, dct(7), dct(7), dct(9), ALU.add)
            chain("dc", tt, dct(8), dct(6), Are, ALU.mult)
            chain("dc", tt, dct(9), dct(7), Aim, ALU.mult)
            chain("dc", tt, dct(8), dct(8), dct(9), ALU.add)
            chain("dc", tt, dct(8), dct(8), dct(11), ALU.mult)
            chain("dc", tt, dct(5), dct(7), Are, ALU.mult)
            chain("dc", tt, dct(9), dct(6), Aim, ALU.mult)
            chain("dc", tt, dct(5), dct(5), dct(9), ALU.subtract)
            chain("dc", tt, dct(5), dct(5), dct(11), ALU.mult)
            dve.wait_ge(*after("act", "w", "s2"))
            tt(tb("p1"), tb("p1"), spread(8, PA), ALU.mult, ("w", "U1"))
            tt(tb("p2"), tb("p2"), spread(5, PA), ALU.mult, ("w", "U2"))
            mine("w", "U2")
            tt(tb("p1"), tb("p1"), tb("p2"), ALU.add, ("w", "V"))
            for b in range(B):
                for k in range(2):
                    dve.wait_ge(*after("act", b, f"ti{k}"))
                    stt(A(b, 9 + k), A(b, 9 + k), 1.0, A(b, 5 + k), ALU.add, ALU.mult, (b, f"in{k}"))
            for b in range(B):
                for k in range(2):
                    dve.wait_ge(*after("act", b, f"hb{k}"))
                    mine(b, f"in{k}")
                    tt(A(b, 9 + k), A(b, 9 + k), A(b, 1 + k), ALU.mult, (b, f"xs{k}"))
                for k in range(2):
                    mine(b, f"xs{k}")
                    nc.vector.tensor_tensor_scan(A(b, 9 + k), A(b, 7 + k), A(b, 9 + k), 0.0, ALU.mult, ALU.add)\
                        .then_inc(*done("dve", b, f"h{k}"))
                for k in range(2):
                    mine(b, f"h{k}")
                    tt(A(b, 3 + k), A(b, 3 + k), A(b, 9 + k), ALU.mult, (b, f"gh{k}"))
            dve.wait_ge(*after("act", "w", "eP"))
            tt(PT, PT, tb("p1"), ALU.mult, ("w", "P"))
            dve.wait_ge(*after("pe", "w", "m1"))
            for h in range(H1):
                last = nc.vector.tensor_scalar(M1[:, :, J * h:J * h + J], grid(bank(M1_BANKS[h])[:, 0:64], J),
                                               32.0 ** -0.5, None, ALU.mult)
            last.then_inc(*done("dve", "w", "m1"))
            for b in range(B):
                dve.wait_ge(*after("pe", "w", f"f{b}"))
                ts(VF[:, b, :], bank((2, 5)[b]), vec("mg"), 1.0 / H1, ALU.mult, ALU.mult, ("w", f"VF{b}"))
            for b in range(B):
                dve.wait_ge(*after("pe", b, "rg"))
                tt(A(b, 5), own(b, 0), Xin[b][:, :], ALU.add, (b, "x1"))
                mine(b, "x1")
                tt(A(b, 6), A(b, 5), Xin[b][:, :], ALU.add, (b, "xx"))
            for b in range(B):
                dve.wait_ge(*after("act", b, "h4.r"))
                stt(A(b, 2), A(b, 5), vec("g2"), A(b, 7), ALU.mult, ALU.mult, (b, "xn2"))
            for b in range(B):
                for k in range(2):
                    dve.wait_ge(*after("act", b, f"gm{k}"))
                    dve.wait_ge(*after("pe", b, f"gr{2 + k}"))
                    tt(A(b, 3 + k), own(b, 2 + k), A(b, 3 + k), ALU.mult, (b, f"hm{k}"))
            for b in range(B):
                dve.wait_ge(*after("pe", b, "shr"))
                tt(A(b, 0), own(b, 0), A(b, 6), ALU.add, (b, "s1"))
            for b in range(B):
                normed(b, "ln1", "X1", 1)

            for b in range(B):
                for p in range(2):
                    dve.wait_ge(*after("pe", b, f"xa.s{p}"))
                    red(S(b, 16 * p, 16), grid(own(b, p), J), ALU.max, (b, f"xa.m{p}"))
                    mine(b, f"xa.m{p}")
                    tt(grid(A(b, 2 + p), J), grid(own(b, p), J), over(S(b, 16 * p, 16), [128, 16, J], 2),
                       ALU.subtract, (b, f"xa.d{p}"))
            for b in range(B):
                for p in range(2):
                    dve.wait_ge(*after("act", b, f"xa.e{p}"))
                    red(S(b, 32 + 16 * p, 16), grid(A(b, 2 + p), J), ALU.add, (b, f"xa.u{p}"))
                    mine(b, f"xa.u{p}")
                    inv(S(b, 32 + 16 * p, 16), S(b, 32 + 16 * p, 16), (b, f"xa.i{p}"))
                    mine(b, f"xa.i{p}")
                    tt(grid(A(b, 2 + p), J), grid(A(b, 2 + p), J), over(S(b, 32 + 16 * p, 16), [128, 16, J], 2),
                       ALU.mult, (b, f"xa.p{p}"))
            for b in range(B):
                dve.wait_ge(*after("pe", b, "xa.o"))
                stt(A(b, 0), own(b, 0), vec("bo"), Xin[b][:, :], ALU.add, ALU.add, (b, "s2"))
            for b in range(B):
                normed(b, "ln2", "X2", 1)

            for b in range(B):
                dve.wait_ge(*after("act", b, "m1.r"))
                stt(A(b, 2), Xin[b][:, :], vec("wl1"), A(b, 7), ALU.mult, ALU.mult, (b, "xm"))
            for b in range(B):
                dve.wait_ge(*after("pe", b, "kf"))
                tt(A(b, 5), own(b, 2), w("mla", "COSk"), ALU.mult, (b, "k1"))
                tt(A(b, 6), own(b, 3), w("mla", "SINk"), ALU.mult, (b, "k2"))
                mine(b, "k2")
                tt(A(b, 5), A(b, 5), A(b, 6), ALU.add, (b, "kk"))
                dve.wait_ge(*after("act", b, "kh"))
                tt(A(b, 6), A(b, 5), KP[b][0], ALU.subtract, (b, "kr"))
                dve.wait_ge(*after("act", b, "km"))
                tt(KP[b][2], A(b, 6), KP[b][1], ALU.subtract, (b, "kl"))
                dve.wait_ge(*after("pe", b, "q1"))
                tt(A(b, 4), own(b, 0), w("mla", "COSq"), ALU.mult, (b, "q1"))
                tt(A(b, 1), own(b, 1), w("mla", "SINq"), ALU.mult, (b, "q2"))
                mine(b, "q2")
                tt(A(b, 4), A(b, 4), A(b, 1), ALU.add, (b, "qq"))
                dve.wait_ge(*after("act", b, "qh"))
                tt(A(b, 1), A(b, 4), QP[b][0], ALU.subtract, (b, "qr"))
                dve.wait_ge(*after("act", b, "qm"))
                tt(QP[b][2], A(b, 1), QP[b][1], ALU.subtract, (b, "ql"))

            def maxima(b, pair):
                h = 2 * pair
                m = S(b, 64, NT * NH).rearrange("p (t h) -> p t h", h=NH)
                for i, u in enumerate("ABCDE"):
                    ring = bank((5 * pair + i) % 2)
                    dve.wait_ge(*after("pe", b, f"mx{pair}.{u}"))
                    hh = h + (u in "CD")
                    if u in "AC":
                        red(m[:, 3, hh:hh + 1], ring, ALU.max, (b, f"mx{pair}.{u}"))
                    elif u in "BD":
                        nc.vector.tensor_reduce(m[:, 2, hh:hh + 1], ring[:, 0:384], X, ALU.max)
                        red(m[:, 0, hh:hh + 1], ring[:, 384:512], ALU.max, (b, f"mx{pair}.{u}"))
                    else:
                        red(m[:, 1, h:h + 2], grid(ring, 256), ALU.max, (b, f"mx{pair}.{u}"))

            def split_max(b):
                mine(b, f"mx{NH // 2 - 1}.E")
                m = S(b, 64, NT * NH).rearrange("p (t h) -> p t h", h=NH)
                res = S(b, 128, NT * NH).rearrange("p (t h) -> p t h", h=NH)
                hi, mid, lo = (spb[b][:, :, NH * c:NH * c + NH] for c in range(3))
                ts(hi, m, -1.0, None, ALU.mult, ALU.bypass, (b, "nh"))
                mine(b, "nh")
                stt(res, m, -1.0, hi, ALU.mult, ALU.subtract, (b, "nr"))
                mine(b, "nr")
                nc.vector.tensor_copy(mid, res).then_inc(*done("dve", b, "nm"))
                mine(b, "nm")
                tt(lo, res, mid, ALU.subtract, (b, "nl"))

            def attended(b, g):
                dve.wait_ge(*after("pe", b, f"vp{(g + 1) * GH // 2 - 1}"))
                o = bank(7)[:, 0:NT * GH * (HD + 1)].rearrange("p (k e) -> p k e", e=HD + 1)
                r_ = S(b, 192 + 32 * g, 32)
                inv(r_.unsqueeze(2), o[:, :, HD:HD + 1], (b, f"ri{g}"))
                mine(b, f"ri{g}")
                y = A(b, 4).rearrange("p (t g h d) -> p g t h d", t=NT, g=NH // GH, d=HD)[:, g]
                tt(y, o[:, :, 0:HD].rearrange("p (t h) d -> p t h d", t=NT),
                   r_.rearrange("p (t h) -> p t h", t=NT).unsqueeze(3).to_broadcast([128, NT, GH, HD]),
                   ALU.mult, (b, f"y{g}"))

            def attention_out(b):
                dve.wait_ge(*after("pe", b, "mo"))
                tt(A(b, 3), bank(1), Xin[b][:, :], ALU.add, (b, "x2a"))
                mine(b, "x2a")
                tt(A(b, 9), A(b, 3), Xin[b][:, :], ALU.add, (b, "x2x"))

            for pair in _HP:
                maxima(0, pair)
            split_max(0)
            for pair in _HP:
                maxima(1, pair)
                if 2 * pair == GH + 2:
                    attended(0, 0)
            split_max(1)
            attended(0, 1)
            attention_out(0)
            for g in range(NH // GH):
                attended(1, g)
            attention_out(1)

            def pick(b, p, e, tri, t, guard):
                n3 = [128, NT, e, e]
                p3 = p.rearrange("p (t e) -> p t e", e=e)
                pj = p3.unsqueeze(2).to_broadcast(n3)
                pe_ = p3.unsqueeze(3).to_broadcast(n3)
                gt, ge = (S(b, c, NT * e * e).rearrange("p (t e j) -> p t e j", t=NT, j=e) for c in (320, 576))
                m3 = w("vec", tri).rearrange("p (e j) -> p e j", j=e).unsqueeze(1).to_broadcast(n3)
                rk, we, ws, wi, wn, wr = (S(b, c, n_) for c, n_ in
                                          ((832, NT * e), (864, NT * e), (896, NT), (900, NT), (904, NT * e),
                                           (936, NT * e)))
                tt(gt, pj, pe_, ALU.is_gt, (b, f"gt{t}"))
                tt(ge, pj, pe_, ALU.is_ge, (b, f"ge{t}"))
                mine(b, f"ge{t}")
                tt(ge, ge, m3, ALU.mult, (b, f"gx{t}"))
                mine(b, f"gx{t}")
                tt(gt, gt, ge, ALU.max, (b, f"gm{t}"))
                mine(b, f"gm{t}")
                red(rk, S(b, 320, NT * e * e).rearrange("p (k j) -> p k j", j=e), ALU.add, (b, f"rk{t}"))
                mine(b, f"rk{t}")
                stt(we, rk, 2.0, p, ALU.is_lt, ALU.mult, (b, f"we{t}"))
                mine(b, f"we{t}")
                red(ws, grid(we, e), ALU.add, (b, f"ws{t}"))
                mine(b, f"ws{t}")
                if guard:
                    ts(ws, ws, 1e-20, None, ALU.add, ALU.bypass, (b, f"wa{t}"))
                    mine(b, f"wa{t}")
                inv(wi, ws, (b, f"wi{t}"))
                mine(b, f"wi{t}")
                tt(grid(wn, e), grid(we, e), over(wi, [128, NT, e], 2), ALU.mult, (b, f"wn{t}"))
                mine(b, f"wn{t}")
                hi, mid, lo = (spb[b][:, :, e * c:e * c + e] for c in range(3))
                nc.vector.tensor_copy(hi, grid(wn, e)).then_inc(*done("dve", b, f"wh{t}"))
                mine(b, f"wh{t}")
                tt(grid(wr, e), grid(wn, e), hi, ALU.subtract, (b, f"wr{t}"))
                mine(b, f"wr{t}")
                nc.vector.tensor_copy(mid, grid(wr, e)).then_inc(*done("dve", b, f"wm{t}"))
                mine(b, f"wm{t}")
                tt(lo, grid(wr, e), mid, ALU.subtract, (b, f"wl{t}"))

            def experts(blocks, routed, s, up, hid, wide, u):
                for k in range(blocks):
                    for b in range(B):
                        dve.wait_ge(*after("act", b, f"{s}{k}"))
                        dve.wait_ge(*after("pe", b, f"{up}{k}"))
                        if k >= 2:
                            dve.wait_ge(*after("pe", b, f"{wide[0]}d{k - 1}"))
                        tt(A(b, 6 + k % 2), own(b, 1), A(b, 4 + k % 2), ALU.mult, (b, f"{hid}{k}"))
                        if k < routed:
                            dve.wait_ge(*after("pe", b, f"{wide}{k}"))
                            mine(b, f"{hid}{k}")
                            tt(A(b, 6 + k % 2), own(b, 2), A(b, 6 + k % 2), ALU.mult, (b, f"{u}{k}"))

            for b in range(B):
                dve.wait_ge(*after("act", b, "f1.r"))
                stt(A(b, 2), A(b, 3), vec("wl2"), A(b, 7), ALU.mult, ALU.mult, (b, "xf"))
            for b in range(B):
                dve.wait_ge(*after("pe", b, "rt"))
                tt(S(b, 256, 28), own(b, 1)[:, 0:28], w("vec", "rb"), ALU.add, (b, "lg"))
            for b in range(B):
                dve.wait_ge(*after("act", b, "rt"))
                ts(S(b, 288, 28), S(b, 288, 28), 1.0, None, ALU.add, ALU.bypass, (b, "pd"))
                mine(b, "pd")
                inv(S(b, 288, 28), S(b, 288, 28), (b, "pr"))
                mine(b, "pr")
                pick(b, S(b, 288, 28), E0, "tri0", "", False)
            experts(U0, E0, "sl", "fu", "hu", "fw", "hw")
            for b in range(B):
                dve.wait_ge(*after("pe", b, f"fd{U0}"))
                tt(A(b, 0), own(b, 3), A(b, 9), ALU.add, (b, "s3"))
            for b in range(B):
                normed(b, "ln3", "X3", 0)

            for b in range(B):
                def wide(i, n_=T):
                    return A(b, i)[0:96, 0:n_]

                hi, mid, stk = (A(b, i)[:, 0:256].bitcast(BF16) for i in (4, 6, 3))
                dve.wait_ge(*after("act", b, "bc"))
                nc.vector.tensor_copy(hi[0:96, :], wide(2)).then_inc(*done("dve", b, "bh"))
                mine(b, "bh")
                tt(wide(5), wide(2), hi[0:96, :], ALU.subtract, (b, "br"))
                mine(b, "br")
                nc.vector.tensor_copy(mid[0:96, :], wide(5)).then_inc(*done("dve", b, "bm"))
                mine(b, "bm")
                nc.vector.tensor_copy(stk[0:32, :], hi[0:32, :])
                nc.vector.tensor_copy(stk[32:64, :], mid[32:64, :]).then_inc(*done("dve", b, "bs"))
                tt(stk[64:96, :], A(b, 5)[64:96, :], mid[64:96, :], ALU.subtract, (b, "bl"))
                dve.wait_ge(*after("pe", b, "de"))
                dve.wait_ge(*after("act", b, "ab"))
                ts(A(b, 8), own(b, 1), vec("bd"), 0.0, ALU.add, ALU.max, (b, "rl"))
            for i in range(NS):
                for b in range(B):
                    dve.wait_ge(*after("act", b, f"aa{i}"))
                    dve.wait_ge(*after("pool", b, f"by{i}"))
                    nc.vector.tensor_tensor_scan(A(b, 14 + i % 2), A(b, 9 + i % 2), A(b, 4 + i % 2), 0.0, ALU.mult,
                                                 ALU.add).then_inc(*done("dve", b, f"sc{i}"))
                    mine(b, f"sc{i}")
                    dve.wait_ge(*after("pe", b, f"cn{i}"))
                    if i >= 2:
                        dve.wait_ge(*after("pe", b, f"yn{i - 1}"))
                    tt(A(b, 12 + i % 2), own(b, 1), A(b, 14 + i % 2), ALU.mult, (b, f"hc{i}"))
            for b in range(B):
                dve.wait_ge(*after("pe", b, f"yn{NS}"))
                tt(A(b, 0), own(b, 2), Xin[b][:, :], ALU.add, (b, "s4"))
            for b in range(B):
                normed(b, "ln4", "X4", 0)

            for b in range(B):
                dve.wait_ge(*after("pe", b, "xb.s"))
                red(S(b, 0, 16), grid(own(b, 2), J), ALU.max, (b, "xb.m"))
                mine(b, "xb.m")
                tt(grid(A(b, 2), J), grid(own(b, 2), J), over(S(b, 0, 16), [128, 16, J], 2), ALU.subtract,
                   (b, "xb.d"))
            for b in range(B):
                dve.wait_ge(*after("act", b, "xb.e"))
                red(S(b, 32, 16), grid(A(b, 2), J), ALU.add, (b, "xb.u"))
                mine(b, "xb.u")
                inv(S(b, 32, 16), S(b, 32, 16), (b, "xb.i"))
                mine(b, "xb.i")
                tt(grid(S(b, 32, 16), H1), grid(S(b, 32, 16), H1),
                   over(tmaskf[:, NT * b:NT * b + NT], [128, NT, H1], 2), ALU.mult, (b, "xb.k"))
                mine(b, "xb.k")
                tt(grid(A(b, 2), J), grid(A(b, 2), J), over(S(b, 32, 16), [128, 16, J], 2), ALU.mult, (b, "xb.p"))
            for b in range(B):
                dve.wait_ge(*after("act", b, "lni.r"))
                tt(A(b, 9), own(b, 0), A(b, 7), ALU.mult, (b, "lni.x"))

            for h in range(2):
                Kh = [Kf[:, c, 2 * h:2 * h + 2, :].unsqueeze(2).to_broadcast([128, 2, B, 128]) for c in range(2)]
                Xh = [bank(4 * h + 2 * c).rearrange("p (f b d) -> p f b d", f=2, b=B) for c in range(2)]
                Y = [Yf[:, c, 2 * h:2 * h + 2, :] for c in range(2)]
                Y4 = [y.rearrange("p f (b d) -> p f b d", b=B) for y in Y]
                Z4 = [Zt[:, c, :].rearrange("p (f b d) -> p f b d", f=2, b=B) for c in range(2)]
                Z = [Zt[:, c, :].rearrange("p (f n) -> p f n", f=2) for c in range(2)]
                dve.wait_ge(*after("act", "w", "kf1"))
                dve.wait_ge(*after("pe", "w", f"xf{h}1"))
                if h:
                    mine("w", "yi0")
                tt(Y4[0], Xh[0], Kh[0], ALU.mult, ("w", f"rr{h}"))
                tt(Z4[0], Xh[1], Kh[1], ALU.mult, ("w", f"ii{h}"))
                tt(Y4[1], Xh[0], Kh[1], ALU.mult, ("w", f"ri{h}"))
                tt(Z4[1], Xh[1], Kh[0], ALU.mult, ("w", f"ir{h}"))
                mine("w", f"ii{h}")
                tt(Y[0], Y[0], Z[0], ALU.subtract, ("w", f"yr{h}"))
                mine("w", f"ir{h}")
                tt(Y[1], Y[1], Z[1], ALU.add, ("w", f"yi{h}"))
            for b in range(B):
                dve.wait_ge(*after("pe", b, "inv"))
                dve.wait_ge(*after("pool", b, "xin"))
                stt(A(b, 4), A(b, 2), vec("Ds"), own(b, 0), ALU.mult, ALU.add, (b, "sk"))
                mine(b, "sk")
                dve.wait_ge(*after("act", b, "s3"))
                tt(A(b, 4), A(b, 4), A(b, 6), ALU.mult, (b, "fo"))
                mine(b, "fo")
                tt(A(b, 4), A(b, 4), A(b, 8), ALU.add, (b, "fp"))
                mine(b, "fp")
                tt(A(b, 0), A(b, 4), Xin[b][:, :], ALU.add, (b, "xt"))
            for b in range(B):
                dve.wait_ge(*after("act", b, "lnf.r"))
                tt(A(b, 9), own(b, 1), A(b, 7), ALU.mult, (b, "lnf.x"))
            for b in range(B):
                dve.wait_ge(*after("pe", b, "w2"))
                stt(A(b, 0), own(b, 0), vec("b2"), A(b, 0), ALU.add, ALU.add, (b, "xt2"))
            for b in range(B):
                dve.wait_ge(*after("act", b, "lno.r"))
                tt(A(b, 9), own(b, 1), A(b, 7), ALU.mult, (b, "lno.x"))
            for b in range(B):
                dve.wait_ge(*after("act", b, "lno.g"))
                tt(A(b, 0), A(b, 10), Xin[b][:, :], ALU.add, (b, "s5"))
            for b in range(B):
                normed(b, "ln5", "X5", 1)

            for b in range(B):
                dve.wait_ge(*after("pe", b, "rt1"))
                lg = grid(own(b, 0)[:, 0:NT * E1], E1)
                red(S(b, 0, NT), lg, ALU.max, (b, "mx"))
                mine(b, "mx")
                tt(grid(S(b, 256, 32), E1), lg, over(S(b, 0, NT), [128, NT, E1], 2), ALU.subtract, (b, "ms"))
            for b in range(B):
                dve.wait_ge(*after("act", b, "rt1"))
                red(S(b, 4, NT), grid(S(b, 288, 32), E1), ALU.add, (b, "su"))
                mine(b, "su")
                inv(S(b, 4, NT), S(b, 4, NT), (b, "iv"))
                mine(b, "iv")
                tt(grid(S(b, 288, 32), E1), grid(S(b, 288, 32), E1), over(S(b, 4, NT), [128, NT, E1], 2), ALU.mult,
                   (b, "pr1"))
                mine(b, "pr1")
                pick(b, S(b, 288, 32), E1, "tri1", "1", True)
            experts(UB1, RB1, "el", "eu", "eu", "ew", "ew")
            for b in range(B):
                dve.wait_ge(*after("pe", b, f"ed{UB1}"))
                tt(A(b, 0), own(b, 3), Xin[b][:, :], ALU.add, (b, "s6"))
            for b in range(B):
                normed(b, "ln6", "X6", 0)

        @block.gpsimd
        def _(pool):
            def tt(out_, a, b_, op, step):
                nc.gpsimd.tensor_tensor(out_, a, b_, op).then_inc(*done("pool", *step))

            def ts(out_, a, s1, s2, op0, op1, step):
                nc.gpsimd.tensor_scalar(out_, a, s1, s2, op0, op1).then_inc(*done("pool", *step))

            def mine(lane, name):
                pool.wait_ge(*after("pool", lane, name))

            for b in range(B):
                nc.gpsimd.memset(Vaug[b][:, :, :, :], 1.0).then_inc(*done("pool", "w", f"va{b}"))
            pool.wait_ge(loads["vec"], 16)
            ts(fb_r, w("vec", "fb"), 0.0, None, ALU.max, ALU.bypass, ("w", "fb.r"))
            pool.wait_ge(*after("act", "w", "fb.l"))
            mine("w", "fb.r")
            tt(fb_r, fb_r, fb_l, ALU.add, ("w", "fb.s"))
            mine("w", "fb.s")
            ts(fcoef, fb_r, -4.0, None, ALU.mult, ALU.bypass, ("w", "fb.c"))
            ts(bhalf, w("vec", "bg"), 0.5, None, ALU.mult, ALU.bypass, ("w", "bh"))
            ts(bfilm, w("vec", "bfi"), vec("mg"), None, ALU.mult, ALU.bypass, ("w", "bf"))
            mine("w", "bf")
            scales = bfilm.rearrange("p (a two) -> p two a", two=2)[:, 0]
            ts(scales, scales, 1.0, None, ALU.add, ALU.bypass, ("w", "bf1"))

            pool.wait_ge(*after("dve", "w", "z3"))
            for name, i, to in (("aQ", 1, QT), ("tQ", 4, tb("tQ"))):
                tt(to, dct(i).unsqueeze(2).to_broadcast([128, 128, PB_]),
                   w("s4d", "lb").unsqueeze(1).to_broadcast([128, 128, PB_]), ALU.mult, ("w", name))
            mine("w", "tQ")
            for c in _HALF:
                d = slice(64 * c, 64 * c + 64)
                if c:
                    mine("w", "qQ0")
                ts(tb("rQ"), tb("tQ")[:, d, :], vec("phq"), ROUND, ALU.add, ALU.add, ("w", f"rQ{c}"))
                mine("w", f"rQ{c}")
                ts(tb("rQ"), tb("rQ"), ROUND, None, ALU.subtract, ALU.bypass, ("w", f"sQ{c}"))
                mine("w", f"sQ{c}")
                tt(tb("tQ")[:, d, :], tb("rQ"), tb("tQ")[:, d, :], ALU.subtract, ("w", f"qQ{c}"))
            pool.wait_ge(*after("act", "w", "sQ"))
            tt(QT, QT, tb("tQ"), ALU.mult, ("w", "Q"))

            for b in range(B):
                pool.wait_ge(*after("act", b, "sp"))
                pool.wait_ge(*after("dve", b, "rl"))
                tt(A(b, 8), A(b, 8), A(b, 7), ALU.add, (b, "dl"))
                mine(b, "dl")
                tt(A(b, 7), A(b, 8), Xin[b][:, :], ALU.mult, (b, "dx"))
            for i in range(NS):
                for b in range(B):
                    pool.wait_ge(*after("act", b, f"bb{i}"))
                    if i == 0:
                        mine(b, "dx")
                    tt(A(b, 4 + i % 2), A(b, 4 + i % 2), A(b, 7), ALU.mult, (b, f"by{i}"))

            for b in range(B):
                pool.wait_ge(*after("act", b, "lni.g"))
                tt(A(b, 10), A(b, 10), A(b, 4), ALU.mult, (b, "lni.z"))
                mine(b, "lni.z")
                tt(A(b, 2), A(b, 10), A(b, 5), ALU.add, (b, "xin"))

        for k, v in order.items():
            assert said[k] == len(v), (k, v[said[k]])


def lay_out(i):
    f4 = np.float32
    lay = layouts()
    a = {k: np.asarray(v) for k, v in i.items()}

    def bf16_words(table):
        return (np.ascontiguousarray(table, f4).view(np.uint32) >> 16).astype(np.uint16).view(f4)

    def pack(group, parts):
        d, n = lay[group]
        out = np.zeros((128, n), f4)
        assert set(parts) == set(d), (group, set(parts) ^ set(d))
        for name, v in parts.items():
            c, m = d[name]
            r0, v = v if isinstance(v, tuple) else (0, v)
            v = np.asarray(v).reshape(v.shape[0], -1)
            assert v.shape[1] == m and v.dtype == f4, (group, name, v.shape, m, v.dtype)
            out[r0:r0 + v.shape[0], c:c + m] = v
        return bf16_words(out) if group in BF_GROUPS else out

    def cols(v):
        return v.reshape(-1, 128).T

    def rows(v):
        return v.reshape(-1, 128, v.shape[1]).transpose(1, 0, 2).reshape(128, -1)

    def full(v, n=1):
        return np.broadcast_to(np.asarray(v, f4).reshape(1, -1), (128, n)).astype(f4)

    def halves(x, y):
        return np.repeat(np.array([x, y], f4), 64)[:, None]

    def tri(e):
        return full(np.tril(np.ones((e, e), f4), -1), e * e)

    bbc = np.concatenate([a["L1_attn_bb"], a["L1_attn_bc"]])
    wbc = np.concatenate([a["L1_attn_Wb"], a["L1_attn_Wc"]]).T
    out = {"x": a["x"].reshape(B * T, D).T}
    out["vec"] = pack("vec", {
        "g1": cols(a["L0_attn_gamma1"]), "g2": cols(a["L0_attn_gamma2"]),
        "cw": a["L0_attn_conv_w"].reshape(2, 128, 4).transpose(1, 0, 2), "cb": cols(a["L0_attn_conv_b"]),
        "bg": cols(a["L0_attn_b_gates"]), "fb": cols(a["L0_attn_forget_base"]), "bo": cols(a["L0_xattn_b_o"]),
        "wl1": cols(a["L0_ffn_w_ln1"]), "wl2": cols(a["L0_ffn_w_ln2"]), "A": a["L1_attn_A"],
        "bd": cols(a["L1_attn_bd"]), "bBC": np.tile(bbc, 3)[:, None], "gni": cols(a["L1_xattn_g_norm_in"]),
        "bni": cols(a["L1_xattn_b_norm_in"]), "gff": cols(a["L1_xattn_g_ffn"]), "bff": cols(a["L1_xattn_b_ffn"]),
        "gno": cols(a["L1_xattn_g_norm_out"]), "bno": cols(a["L1_xattn_b_norm_out"]), "b1": cols(a["L1_xattn_b1"]),
        "b2": cols(a["L1_xattn_b2"]),
        "bfi": cols(np.concatenate([a["L1_xattn_b_film_in"], a["L1_xattn_b_film_out"]])),
        "Ds": cols(a["L1_xattn_D_skip"]), "mg": full(a["L1_xattn_mod_gate"]), "eps": full(1e-5),
        "q25": full(0.25 * (1.0 + 1e-6)), "one": full(1.0), "phq": halves(0.25, 0.0), "ph1": halves(0.25, 0.5),
        "ph2": halves(0.5, 0.75), "raq": halves(0.25 * TWO_PI, 0.0), "ra1": halves(0.25 * TWO_PI, 0.5 * TWO_PI),
        "ra2": halves(0.5 * TWO_PI, 0.75 * TWO_PI),
        "rb": full(np.tile(a["L0_ffn_routing_bias"], NT), NT * E0), "tri0": tri(E0), "tri1": tri(E1)})
    out["hawk"] = pack("hawk", {
        "Wga": rows(a["L0_attn_W_gates"].T), "Wou": rows(a["L0_attn_W_out"].T),
        "Wgr": a["L0_attn_W_grow"].T, "Wsh": rows(a["L0_attn_W_shrink"].T)})
    out["win"] = pack("win", {"Win": a["L0_attn_W_in"].T})
    out["xa0"] = pack("xa0", {
        "Wk": a["L0_xattn_W_k"], "Wv": a["L0_xattn_W_v"], "WqT": rows(a["L0_xattn_W_q"].T),
        "Wo": rows(a["L0_xattn_W_o"]), "ctx": a["ctx_768"].reshape(B * J, CD).T})
    eye = np.eye(128, dtype=f4)
    out["sq"] = pack("sq", {"Cm": eye - f4(1 / 128), "ones": np.ones((128, 128), f4), "id": eye})

    half = HD // 2
    kv, q, kx, kr, ks = (np.zeros((r_, 128), f4) for r_ in (32, 32, 32, 128, 128))
    qs = np.zeros((32, 128), f4)
    turned = [(d + half // 2) % half for d in range(half)]
    for d in range(half):
        plain, rope, swap = (np.arange(NH) * half + e for e in (d, d, turned[d]))
        kx[:, NH * d:NH * d + NH] = a["L0_ffn_W_ku"][:, plain]
        q[:, NH * d:NH * d + NH] = a["L0_ffn_W_qu"][:, plain]
        r0 = NH * (half + d)
        kr[:, r0:r0 + NH] = a["L0_ffn_W_ropek"][:, rope]
        ks[:, r0:r0 + NH] = a["L0_ffn_W_ropek"][:, swap]
        q[:, r0:r0 + NH] = a["L0_ffn_W_ropeq"][:, rope]
        qs[:, r0:r0 + NH] = a["L0_ffn_W_ropeq"][:, swap]
    freq = (1.0 / 10000.0 ** (np.arange(0, half, 2, dtype=f4) / half)).astype(f4)
    angle = (np.arange(T, dtype=f4)[:, None] * freq[None, :]).astype(f4).astype(np.float64)
    cos, sin = np.ones((128, T)), np.zeros((128, T))
    for d in range(half):
        r0 = NH * (half + d)
        cos[r0:r0 + NH] = np.cos(angle[:, d % 2])
        sin[r0:r0 + NH] = np.sin(angle[:, d % 2]) * (-1 if d < half // 2 else 1)
    sc = HD ** -0.5
    out["mla"] = pack("mla", {
        "lat": np.concatenate([a["L0_ffn_W_kvd"], a["L0_ffn_W_qd"]], 1), "kx": kx, "kr": kr, "ks": ks,
        "q": (32, q), "qs": (32, qs), "v": a["L0_ffn_W_vu"], "o": a["L0_ffn_W_o"],
        "COSk": cos.astype(f4), "SINk": sin.astype(f4), "COSq": (cos * sc).astype(f4),
        "SINq": (sin * sc).astype(f4)})

    def experts(shared, routed):
        return np.concatenate([routed.transpose(1, 0, 2).reshape(128, -1), shared], 1)

    out["moe0"] = pack("moe0", {
        "g": experts(a["L0_ffn_Wg_s"], a["L0_ffn_Wg_r"]), "u": experts(a["L0_ffn_Wu_s"], a["L0_ffn_Wu_r"]),
        "d": rows(np.concatenate([a["L0_ffn_Wd_r"].reshape(-1, 128), a["L0_ffn_Wd_s"]])),
        "r": a["L0_ffn_W_router"]})
    out["late"] = pack("late", {
        "Wd": a["L1_attn_Wd"].T, "WBC": np.tile(wbc, (1, 3)), "WqT": a["L1_xattn_Wq"].T, "Wk": a["L1_xattn_Wk"],
        "Wv": a["L1_xattn_Wv"], "film": np.concatenate([a["L1_xattn_W_film_in"], a["L1_xattn_W_film_out"]], 1),
        "W1": a["L1_xattn_W1"], "W2": rows(a["L1_xattn_W2"]), "gate": a["L1_ffn_gate_w"].T})
    twice = {k: np.tile(a[f"L1_xattn_{v}"].T, (2, 1)) for k, v in
             (("Are", "A_re"), ("Aim", "A_im"), ("Cre", "C_re"), ("Cim", "C_im"))}
    out["s4d"] = pack("s4d", {**twice, "ldt": full(a["L1_xattn_log_dt"], 128), "lb": full(np.arange(PB_), PB_),
                              "la": full(np.arange(PA) * PB_, PA)})
    theta = 2 * np.pi * np.outer(np.arange(T), np.arange(NF) + 0.5) / (2 * T)
    F = np.concatenate([np.cos(theta), -np.sin(theta)], 1).astype(f4)
    G = (np.concatenate([np.cos(theta.T), -np.sin(theta.T)]) * (2 * 2 / (2 * T))).astype(f4)
    out["dft"] = pack("dft", {"F": rows(F), "G": rows(G)})

    def padded(v, axis):
        z = np.zeros([128 * UB1 - N1 if k == axis else n for k, n in enumerate(v.shape)], f4)
        return np.concatenate([v, z], axis)

    out["ffn1"] = pack("ffn1", {
        "g": padded(experts(a["L1_ffn_swg"], a["L1_ffn_wg"]), 1), "u": padded(experts(a["L1_ffn_swu"], a["L1_ffn_wu"]), 1),
        "d": rows(padded(np.concatenate([a["L1_ffn_wd"].reshape(-1, 128), a["L1_ffn_swd"]]), 0))})
    k = np.arange(128)
    low = np.where(k[:, None] < k[None, :], -BIG, 0.0).astype(f4)
    out["bf"] = pack("bf", {"id": eye, "mS": low, "mT": low.T,
                            "one": np.ones((128, 128), f4)})
    out["sel0"] = pack("sel0", {"s": np.tile(np.repeat(np.eye(E0, dtype=f4), 128, 1), (3, 1))})
    out["selA"] = pack("selA", {"s": np.tile(np.repeat(np.eye(2 * NS, dtype=f4), 128, 1), (3, 1))})
    out["sel1"] = pack("sel1", {"s": np.tile(np.repeat(np.eye(E1, dtype=f4), I1, 1), (3, 1))})
    out["ones"] = bf16_words(np.ones((KROWS - C6 * HD, NH * T)))

    def heads(m, h):
        return np.repeat(m.reshape(B, 1, J), h, 1).reshape(1, -1)

    m0, m1 = (a[f"mask_BxS2_{s}"].view(np.uint8) for s in ("bk0", "bf1"))
    out["km"] = np.repeat(heads(m0, H0), 128, 0)
    out["kr"] = np.concatenate([heads(m0, H0), heads(m1, H1)], 1)
    out["tm"] = a["mask_BxS_bf1"].view(np.uint8).reshape(B * NT, 128).T
    out = {k: np.ascontiguousarray(v) for k, v in out.items()}
    for k in ("km", "kr", "tm"):
        out[k] = out[k].view(np.uint32)
    return out


def kernel(**inputs):
    import concourse.bacc as bacc
    from concourse.bass_utils import run_bass_kernel_spmd as run

    arrays = lay_out(inputs)
    nc = bacc.Bacc("TRN2", target_bir_lowering=False, num_devices=1)
    dram = {n: nc.dram_tensor(f"in_{n}", v.shape, mybir.dt.from_np(v.dtype), kind="ExternalInput").ap()
            for n, v in arrays.items()}
    out = nc.dram_tensor("out", (D, B * T), F32, kind="ExternalOutput").ap()
    build(nc, dram, out)
    r = run(nc, [{f"in_{n}": v for n, v in arrays.items()}], core_ids=[0])
    return np.ascontiguousarray(r.results[0]["out"].T).reshape(B, T, D)
```

```python
import math
from contextlib import ExitStack

import concourse.bass as bass
import numpy as np
from concourse import mybir

F32 = mybir.dt.float32
BF16 = mybir.dt.bfloat16
U8 = mybir.dt.uint8
U32 = mybir.dt.uint32
ALU = mybir.AluOpType
ACT = mybir.ActivationFunctionType
X = mybir.AxisListType.X

B, T, D = 2, 512, 128
NT = T // 128
J = 32
CD = 96
H0, H1 = 8, 4
NH, HD = 16, 8
E0, E1 = 7, 8
U0 = E0 + 1
SH0 = 1
I1 = 176
SH1 = -(-2 * I1 // 128)
RB1 = E1 * I1 // 128
UB1 = SH1 + RB1
NS = 16
PA, PB_ = 16, 32
NF = 512
NFB = NF // 128
BIG = 2.0 ** 100
TWO_PI = 6.283184
ROUND = 1.5 * 2.0 ** 23
PRODUCTS = 6
ZROWS = 21
MROWS = PRODUCTS * HD + ZROWS
KROWS = MROWS + 3


def _ln(t):
    return [f"{t}.sq", f"{t}.l", f"{t}.r"]


_U = list(range(U0))
_N = list(range(NS))
_K = list(range(UB1))
PAIRS = range(NH // 2)
GROUPS, UNITS = NH // 4, 10
STAGE_ENDS = {3: 0, 7: 1, 9: 2}
PV_LAG, YC_LAG, YT_LAG = 2, 12, 14


def attention_events(n):
    out = []
    g, r = divmod(n - PV_LAG, UNITS)
    if g >= 0 and r in STAGE_ENDS:
        out.append(("pv", g, STAGE_ENDS[r]))
    g, r = divmod(n - YT_LAG, UNITS)
    if 0 <= g < GROUPS and r == 0:
        out.append(("yT", g, 0))
    return out


def unit_steps(k, units, shared, p):
    out = []
    if k < units:
        out += [f"{p}g{k}", f"{p}u{k}"]
        if k == shared:
            out += [f"{p}wt"]
        if k >= shared:
            out += [f"{p}w{k}"]
    return out + ([f"{p}d{k}"] if k else [])


LAG = YT_LAG - UNITS + 1
_ATT_PE = [x for n in range(GROUPS * UNITS + LAG)
           for x in ([f"su{n}"] if n < GROUPS * UNITS else [])
           + [f"pv{g}.{i}" if kind == "pv" else f"yT{g}" for kind, g, i in attention_events(n)]]
_ATT_ACT = [x for n in range(GROUPS * UNITS + LAG)
            for x in ([f"su{n}"] if n < GROUPS * UNITS else []) + ([f"yc{(n - YC_LAG) // UNITS}"]
                                                                   if n >= YC_LAG and (n - YC_LAG) % UNITS == 0 else [])]
SPLIT = ["kk", "qq", "kr", "qr", "kl", "ql"]
STEPS = {
    "pe": [
        "h1.ss", "z0", "z1", "z2", "z3", "g0", "g1", "g2", "g3", "rg", "h4.ss", "gr0", "gr1", "gr2", "gr3", "shr",
        "ln1.c", "ln1.v", "xa.s0", "xa.s1", "xa.t0", "xa.t1", "xa.o", "ln2.c", "ln2.v",
        "m1.ss", "lat", "kf", "q0", "q1", "v",
        *[f"mx{h}.{u}" for h in PAIRS for u in "ABCDE"], "nmt",
        *_ATT_PE, "yt", "mo",
        "f1.ss", "rt", *[x for k in range(U0 + 1) for x in unit_steps(k, U0, SH0, "f")],
        "ln3.c", "ln3.v", "bc", "de", *[f"{n}{i + (n == 'bn')}" for i in range(-1, NS + 1) for n in ("bn", "cn", "yn")
                                        if {"bn": i + 1 < NS, "cn": 0 <= i < NS, "yn": i > 0}[n]],
        "ln4.c", "ln4.v", "lni.c", "xb.s", "lni.v", "xb.t", "fl0", "fl1", "fl2", "fl3", "xit",
        "inv", "lnf.c", "lnf.v", "w10", "w11", "w12", "w13", "w2", "lno.c", "lno.v", "ln5.c", "ln5.v",
        "rt1", *[x for k in range(UB1 + 1) for x in unit_steps(k, UB1, SH1, "e")],
        "ln6.c", "ln6.v"],
    "act": [
        "h1.sq", "h1.l", "h1.r", "cv0", "cv1", "gg0", "gg1", "tf0", "tf1", "ti0", "ti1",
        "al0", "al1", "sa0", "sa1", "lb0", "lb1", "hb0", "hb1", "h4.sq", "h4.l", "h4.r", "gm0", "gm1", *_ln("ln1"),
        "xa.e0", "xa.e1", "xa.a0", "xa.a1", *_ln("ln2"), "m1.sq", "m1.l", "m1.n", "m1.m", "m1.r", "lat",
        "kh", "qh", "km", "qm", "v", "nmt", *_ATT_ACT, "yt",
        "f1.sq", "f1.l", "f1.n", "f1.m", "f1.r", *[x for u in _U for x in [f"sl{u}"] + ["wt"] * (u == SH0)], *_ln("ln3"),
        "bc", "ab", "ex", "sp", *[f"{n}{i}" for i in _N for n in ("aa", "bb")], *_ln("ln4"),
        *_ln("lni"), "xb.e", "lni.g", "xb.a", "s0", "s1", "s2", "s3", "xit", *_ln("lnf"), "lnf.g",
        "u0", "u1", "u2", "u3", *_ln("lno"), "lno.g", *_ln("ln5"), *[x for k in _K for x in [f"el{k}"] + ["wt1"] * (k == SH1)],
        *_ln("ln6")],
    "dve": [
        "xn1", "cw0.2", "cw1.2", "cw0.1", "cw1.1", "cw0.0", "cw1.0", "in0", "in1", "xs0", "xs1", "h0", "h1",
        "gh0", "gh1", "x1", "xx", "xn2", "hm0", "hm1", "s1", "X1",
        "xa.m0", "xa.d0", "xa.m1", "xa.d1", "xa.u0", "xa.i0", "xa.p0", "xa.u1", "xa.i1", "xa.p1", "s2", "X2",
        "xm", "k1", "k2", "q1", "q2", *SPLIT,
        *[f"mx{h}.{u}" for h in PAIRS for u in "ABCDE"], "nh", "nr", "nm", "nl",
        *[f"{n}{g}" for g in range(GROUPS) for n in ("ri", "y")], "x2a", "x2x",
        "xf", "lg",
        *[f"{n}{u}" for u in _U for n in ("hu", "hw") if not (u < SH0 and n == "hw")], "s3", "X3",
        "bh", "br", "rl", "bm", "bl", "dl", *[f"{n}{i}" for i in _N for n in ("sc", "hc")], "s4", "X4",
        "xb.m", "xb.d", "lni.x", "xb.u", "xb.i", "xb.k", "xb.p", "lni.z", "xin", "sk", "fo", "fp", "xt",
        "lnf.x", "xt2", "lno.x", "s5", "X5",
        "mx", "ms",
        *[f"{n}{k}" for k in _K for n in ("eu", "ew") if not (k < SH1 and n == "ew")], "s6", "X6"],
    "pool": [*SPLIT, "dx", *[f"by{i}" for i in _N]],
}
_HALF = (0, 1)
STEPS_W = {
    "pe": ["kv", "m0", "v0", "k1", "m1", "f0", "f1", "kp", "kt", "kf0", "kf1",
           *[f"xf{c}{i}" for c in _HALF for i in _HALF]],
    "act": ["fb.a", "fb.e", "fb.l", "dt", "th", "sh", "sy", "kv0", "kv", "s1", "s2", "eP",
            "eQ", "sQ", "kp", "kl", "rt", "kf0", "kf1", "rt1"],
    "dve": ["km", "kb0", "kb1", "tm", *[f"z{i}" for i in range(1, 10)], *[f"a{i}" for i in range(1, 7)],
            "r1", "q1", "r2", "q2", "rQ0", "qQ0", "m0a", "m0b", "rQ1", "qQ1", "v0", "k1", "vr",
            "m1", "VF0", "VF1", "P",
            "pd", "pr", "gt", "ge", "gx", "gm", "rk", "we", "ws", "wi", "wn", "wh", "wr", "wm", "wl",
            *[f"{n}{c}" for c in _HALF for n in ("rr", "ii", "ri", "ir", "yr", "yi")],
            "su", "iv", "pr1", "gt1", "ge1", "gx1", "gm1", "rk1", "we1", "ws1", "wa1", "wi1", "wn1", "wh1", "wr1",
            "wm1", "wl1"],
    "pool": ["va0", "va1", "fb.r", "fb.s", "fb.c", "bh", "bf", "bf1", "tP", "tQ", "aP", "aQ",
             *[f"dc{i}" for i in range(1, 24)], "U1", "U2", "V", "Q"],
}


def steps_of(engine, lane):
    if lane == "w":
        return STEPS_W[engine]
    left_out = SPLIT if (engine, lane) in (("dve", 1), ("pool", 0)) else ()
    return [n for n in STEPS[engine] if n not in left_out]


def layouts():
    groups = {
        "vec": [("g1", 1), ("g2", 1), ("cw", 8), ("cb", 2), ("bg", 4), ("fb", 2), ("bo", 1), ("wl1", 1), ("wl2", 1),
                ("A", NS), ("bd", 1), ("bBC", 1), ("gni", 1), ("bni", 1), ("gff", 1), ("bff", 1), ("gno", 1),
                ("bno", 1), ("b1", 4), ("b2", 1), ("bfi", 4), ("Ds", 1), ("mg", 1), ("eps", 1), ("q25", 1),
                ("one", 1), ("phq", 1), ("ph1", 1), ("ph2", 1), ("raq", 1), ("ra1", 1), ("ra2", 1), ("rb", NT * E0), ("tri0", E0 * E0),
                ("tri1", E1 * E1)],
        "hawk": [("Wga", 1024), ("Wou", 256), ("Wgr", 512), ("Wsh", 256)],
        "win": [("Win", 512)],
        "xa0": [("Wk", 512), ("Wv", 512), ("WqT", 512), ("Wo", 512), ("ctx", B * J)],
        "sq": [("Cm", 128), ("ones", 128), ("id", 128)],
        "mla": [("lat", 64), ("kx", 128), ("kr", 128), ("ks", 128), ("q", 128), ("qs", 128), ("v", 128), ("o", 128),
                ("COSk", T), ("SINk", T), ("COSq", T), ("SINq", T)],
        "moe0": [("g", 128 * U0), ("u", 128 * U0), ("d", 128 * U0), ("r", E0)],
        "late": [("Wd", 128), ("WBC", 96), ("WqT", 128), ("Wk", 128), ("Wv", 128), ("film", 512), ("W1", 512),
                 ("W2", 512), ("gate", E1)],
        "s4d": [("Are", 128), ("Aim", 128), ("Cre", 128), ("Cim", 128), ("ldt", 128), ("lb", PB_), ("la", PA)],
        "dft": [("F", NT * 2 * NF), ("G", 2 * NF // 128 * T)],
        "ffn1": [("g", 128 * UB1), ("u", 128 * UB1), ("d", 128 * UB1)],
        "bf": [("id", 128), ("mS", 128), ("mT", 128), ("one", 128)],
        "sel0": [("s", 128 * E0)],
        "selA": [("s", 128 * 2 * NS)],
        "sel1": [("s", 128 * RB1)],
    }
    out = {}
    for g, items in groups.items():
        at, d = 0, {}
        for name, n in items:
            d[name] = (at, n)
            at += n
        out[g] = (d, at)
    return out


BF_GROUPS = ("bf", "sel0", "selA", "sel1")


def build(nc, dram, out):
    lay = layouts()
    with ExitStack() as ctx:
        def sb(name, shape, dt=F32):
            return ctx.enter_context(nc.sbuf_tensor(name, shape, dt))

        lanes = (0, 1, "w")
        sems = {(e, l): ctx.enter_context(nc.semaphore(f"{e}_steps_{l}")) for e in STEPS for l in lanes}
        order = {(e, l): steps_of(e, l) for e in STEPS for l in lanes}
        place = {k: {n: i + 1 for i, n in enumerate(v)} for k, v in order.items()}
        for k, v in order.items():
            assert len(place[k]) == len(v), k
        said = {k: 0 for k in order}

        def done(engine, lane, name):
            k = (engine, lane)
            assert place[k][name] == said[k] + 1, (k, name, "expected", order[k][said[k]])
            said[k] += 1
            return sems[k], 1

        def after(engine, lane, name):
            return sems[engine, lane], place[engine, lane][name]

        def splitter(b):
            return ("dve", "pool")[b]

        loads = {n: ctx.enter_context(nc.semaphore(f"load_{n}")) for n in
                 ["x0", "x1", "vec", "win", "hawk", "xa0", "sq", "mla", "moe0", "late", "s4d", "dft", "ffn1", "bf", "sel0",
                  "selA", "sel1", "km", "kr", "tm"]}
        stack = {(w, b): ctx.enter_context(nc.semaphore(f"stack_{w}{b}")) for w in "kqm" for b in range(B)}
        kshuf = ctx.enter_context(nc.semaphore("kernel_rows_moved"))
        stored = ctx.enter_context(nc.semaphore("stored"))

        PS = ctx.enter_context(nc.psum_tensor("PS", [128, 8, T], F32))
        RA = sb("RA", [128, lay["win"][1] + lay["hawk"][1] + lay["xa0"][1]])
        RR = sb("RR", [128, 16384])
        AR = [sb(f"AR{b}", [128, 16, T]) for b in range(B)]

        def flat(b, i, j):
            return AR[b][:, i:j, :].rearrange("p a t -> p (a t)")

        tiles = {}
        for g, (d, n) in lay.items():
            if g == "hawk":
                tiles[g] = RA[:, 0:n]
            elif g == "xa0":
                tiles[g] = RA[:, lay["hawk"][1]:lay["hawk"][1] + n]
            elif g == "win":
                at = lay["hawk"][1] + lay["xa0"][1]
                tiles[g] = RA[:, at:at + n]
            elif g == "moe0":
                tiles[g] = RA[:, 0:n]
            elif g == "sel0":
                at = lay["moe0"][1] + 1
                tiles[g] = RA[:, at:at + n // 2]
            elif g == "dft":
                tiles[g] = RR[:, 0:n]
            elif g == "ffn1":
                tiles[g] = RR[:, 8192:8192 + n]
            elif g == "selA":
                tiles[g] = RR[:, 13600:13600 + n // 2]
            elif g == "sel1":
                tiles[g] = RR[:, 15648:15648 + n // 2]
            elif g == "s4d":
                tiles[g] = flat(1, 14, 16)[:, 0:n]
            else:
                tiles[g] = sb(f"W_{g}", [128, n // (2 if g in BF_GROUPS else 1)])[:, :]

        def w(group, name, a=0, n=None):
            c, full = lay[group][0][name]
            t = tiles[group].bitcast(BF16) if group in BF_GROUPS else tiles[group]
            return t[:, c + a:c + a + (full if n is None else n)]

        def vec(name, i=0):
            return w("vec", name, i, 1)

        Xin = [sb(f"x_in{b}", [128, T]) for b in range(B)]
        kmask_w, krow_w, tmask_w = (sb("kmask", [128, B * H0 * J // 4], U32), sb("krow", [1, B * (H0 + H1) * J // 4], U32),
                                    sb("tmask", [128, B * NT // 4], U32))
        kmask, krow, tmask = (m[:, :].bitcast(U8) for m in (kmask_w, krow_w, tmask_w))
        tmaskf = sb("tmaskf", [128, B * NT])
        krowb = sb("krowb", [1, B * (H0 + H1) * J], BF16)
        pre = flat(0, 11, 14)
        kmaskf, KTs, VTs, K1s, Vrep = (pre[:, 0:512], pre[:, 512:768], pre[:, 768:1024], pre[:, 1024:1088],
                                       pre[:, 1088:1344])
        M0 = sb("M0", [128, B, H0 * J])
        V0 = sb("V0", [128, B, 2, 128])
        M1 = sb("M1", [128, B, H1 * J])
        VF = sb("VF", [128, B, 512])
        small = sb("small", [128, 64])
        fcoef, bhalf, bfilm = small[:, 0:2], small[:, 2:6], small[:, 6:10]
        fb_r, fb_a, fb_e, fb_l = small[:, 10:12], small[:, 12:14], small[:, 14:16], small[:, 16:18]
        stats = sb("stats", [128, B * 1024])
        parts48 = sb("parts", [128, B, NT, 48], BF16)
        spb = [parts48[:, b] for b in range(B)]
        wT = [sb(f"wT{b}", [48, T], BF16) for b in range(B)]
        Vaug = [sb(f"Vaug{b}", [128, NT, NH, HD + 1]) for b in range(B)]
        KL = sb("KL", [128, NT, 128])
        Kf = sb("Kf", [128, 2, NFB, 128])

        QT = RR[:, 0:4096].rearrange("p (d l) -> p d l", l=PB_)
        PT = RR[:, 4096:6144].rearrange("p (d l) -> p d l", l=PA)
        Ksb = RR[:, 6144:7168]
        Kdl = RR[:, 7168:7680]

        KV = [[RR[:, (2 * b + i) * 4096:(2 * b + i + 1) * 4096].bitcast(BF16).rearrange("p (h t) -> p h t", h=NH)
               for b in range(B)] for i in range(2)]
        Kst, Qst = KV
        P = [AR[s_][:, 11 + i, :] for s_ in range(2) for i in range(5)]
        XT = flat(0, 11, 13).rearrange("p (j b d) -> p j b d", j=NT, b=B)
        Yf = flat(1, 11, 15).rearrange("p (c f n) -> p c f n", c=2, f=NFB)
        Zt = flat(0, 13, 15).rearrange("p (c n) -> p c n", c=2)

        def A(b, i):
            return AR[b][:, i, :]

        def S(b, c, n):
            return stats[:, 1024 * b + c:1024 * b + c + n]

        def routing(c, n):
            return stats[:, c:c + n]

        def dct(i):
            return flat(1, 11, 14)[:, 128 * i:128 * i + 128]

        def tb(name):
            at, l = {"tQ": (6144, PB_), "rQ": (10240, PB_), "p1": (12288, PA), "p2": (14336, PA)}[name]
            n = 64 if name == "rQ" else 128
            return RR[:, at:at + n * l].rearrange("p (d l) -> p d l", l=l)

        def bank(i):
            return PS[:, i, :]

        def own(b, i):
            return PS[:, 4 * b + i, :]

        def grid(ap, k):
            return ap.rearrange("p (a k) -> p a k", k=k)

        def over(ap, shape, at):
            return ap.unsqueeze(at).to_broadcast(shape)

        half = [[flat(b, 8, 11)[:, 256 * i:256 * i + 256].bitcast(BF16) for i in range(6)] for b in range(B)]
        KP = [half[b][0:3] for b in range(B)]
        QP = [half[b][3:6] for b in range(B)]

        def split(engine, tt, b):
            engine.wait_ge(*after("dve", b, "q2"))
            tt(A(b, 5), A(b, 5), A(b, 6), ALU.add, (b, "kk"))
            tt(A(b, 4), A(b, 4), A(b, 1), ALU.add, (b, "qq"))
            engine.wait_ge(*after("act", b, "kh"))
            tt(A(b, 6), A(b, 5), KP[b][0], ALU.subtract, (b, "kr"))
            engine.wait_ge(*after("act", b, "qh"))
            tt(A(b, 1), A(b, 4), QP[b][0], ALU.subtract, (b, "qr"))
            engine.wait_ge(*after("act", b, "km"))
            tt(KP[b][2], A(b, 6), KP[b][1], ALU.subtract, (b, "kl"))
            engine.wait_ge(*after("act", b, "qm"))
            tt(QP[b][2], A(b, 1), QP[b][1], ALU.subtract, (b, "ql"))

        M1_BANKS = (3, 6, 7, 1)

        block = ctx.enter_context(nc.Block())

        @block.sync
        def _(sp):
            def load(name, dst, src=None):
                sp.dma_start(dst, dram[name] if src is None else src).then_inc(loads[name], 16)

            load("x0", Xin[0][:, :], dram["x"][:, 0:T])
            load("sq", tiles["sq"])
            load("vec", tiles["vec"])
            load("win", tiles["win"])
            load("x1", Xin[1][:, :], dram["x"][:, T:2 * T])
            load("s4d", tiles["s4d"])
            load("km", kmask_w[:, :])
            load("kr", krow_w[:, :])
            load("tm", tmask_w[:, :])
            load("xa0", tiles["xa0"])
            load("hawk", tiles["hawk"])
            load("late", tiles["late"])
            load("bf", tiles["bf"])
            load("mla", tiles["mla"])

            def parts(b, part):
                for which, dst, src, rows in (("k", Kst[b], KP[b], "hmhlhm"), ("q", Qst[b], QP[b], "hhmhlm")):
                    sp.wait_ge(*(after(splitter(b), b, f"{which}l") if part == "l"
                                 else after("act", b, f"{which}{part}")))
                    for c in range(PRODUCTS):
                        if rows[c] == part:
                            sp.dma_start(dst[c * HD:(c + 1) * HD, :, :], src["hml".index(part)])\
                                .then_inc(stack[which, b], 16)

            sp.wait_ge(*after("act", "w", "kp"))
            for a in range(PA):
                sp.dma_start(Kdl[:, PB_ * a:PB_ * a + PB_],
                             Ksb[a:128:32, :].rearrange("p (d l) -> p d l", l=PB_)).then_inc(kshuf, 16)
            for b in range(B):
                sp.wait_ge(*after("pe", "w", "kt"))
                if b == 0:
                    for q in range(B):
                        sp.dma_start(RR[PRODUCTS * HD:KROWS, 8192 * q:8192 * q + 4096], dram["ones"])\
                            .then_inc(stack["k", q], 16)
                        sp.dma_start(RR[PRODUCTS * HD:MROWS, 8192 * q + 4096:8192 * q + 8192],
                                     dram["ones"][0:ZROWS, :]).then_inc(stack["q", q], 16)
                for part in "hml":
                    parts(b, part)
            for b in range(B):
                sp.wait_ge(*after("pe", b, "xa.o"))
            load("moe0", tiles["moe0"])
            load("sel0", tiles["sel0"])
            for b in range(B):
                sp.wait_ge(*after("act", b, "nmt"))
                sp.dma_start(Qst[b][MROWS:KROWS, :, :], wT[b][:, :]).then_inc(stack["m", b], 16)
            for b in range(B):
                sp.wait_ge(*after("pe", b, f"su{GROUPS * UNITS - 1}"))
            load("selA", tiles["selA"])
            load("dft", tiles["dft"])
            load("ffn1", tiles["ffn1"])
            load("sel1", tiles["sel1"])
            for b in range(B):
                sp.wait_ge(*after("dve", b, "X6"))
                sp.dma_start(out[:, b * T:(b + 1) * T], Xin[b][:, :]).then_inc(stored, 16)
            sp.wait_ge(stored, 16 * B)

        @block.tensor
        def _(pe):
            mm, tr = nc.tensor.matmul, nc.tensor.transpose

            def layernorm(t, ready, i=0):
                for b in range(B):
                    pe.wait_ge(*after("dve", b, ready))
                    mm(own(b, i), w("sq", "Cm"), A(b, 0), start=True, stop=True).then_inc(*done("pe", b, f"{t}.c"))
                mean_squares(t, i + 1)

            def mean_squares(t, i):
                for b in range(B):
                    pe.wait_ge(*after("act", b, f"{t}.sq"))
                    mm(own(b, i), w("sq", "ones"), A(b, 1), start=True, stop=True).then_inc(*done("pe", b, f"{t}.v"))

            def squares(b, t, i):
                pe.wait_ge(*after("act", b, f"{t}.sq"))
                mm(own(b, i), w("sq", "ones"), A(b, 1), start=True, stop=True).then_inc(*done("pe", b, f"{t}.ss"))

            def kernel_products():
                pe.wait_ge(*after("dve", "w", "P"))
                pe.wait_ge(*after("pool", "w", "Q"))
                for i in range(32):
                    for q in range(4):
                        d = 32 * q + i
                        last = mm(bank(2 + i // 16)[32 * q:32 * q + PA, PB_ * (i % 16):PB_ * (i % 16) + PB_],
                                  PT[:, d, :], QT[:, d, :], start=True, stop=True)
                last.then_inc(*done("pe", "w", "kp"))

            ctxT = w("xa0", "ctx")
            pe.wait_ge(loads["sq"], 16)
            for b in range(B):
                squares(b, "h1", 0)
            pe.wait_ge(loads["win"], 16)
            for b in range(B):
                pe.wait_ge(*after("dve", b, "xn1"))
                for i, blk in enumerate((2, 3, 0, 1)):
                    mm(own(b, i), w("win", "Win", 128 * blk, 128), A(b, 2), start=True, stop=True)\
                        .then_inc(*done("pe", b, f"z{i}"))
            pe.wait_ge(loads["xa0"], 16)
            pe.wait_ge(*after("act", 0, "gg1"))
            for i, name in enumerate(("Wk", "Wv")):
                for blk in range(4):
                    last = mm(bank(2 + i)[:, blk * 64:blk * 64 + 64], w("xa0", name, 128 * blk, 128)[0:CD, :],
                              ctxT[0:CD, :], start=True, stop=True)
            last.then_inc(*done("pe", "w", "kv"))
            pe.wait_ge(*after("act", "w", "kv"))
            pe.wait_ge(*after("act", 1, "gg1"))
            for par in range(2):
                p0 = 64 * par
                for blk in range(4):
                    last = mm(bank(6 + par)[:, blk * 64:blk * 64 + 64], w("xa0", "WqT", 128 * blk, 128)[p0:p0 + 64, :],
                              KTs[p0:p0 + 64, blk * 64:blk * 64 + 64], start=True, stop=True)
            last.then_inc(*done("pe", "w", "m0"))
            pe.wait_ge(loads["hawk"], 16)
            for b in range(B):
                pe.wait_ge(*after("dve", b, "cw1.0"))
                for o in range(4):
                    if o == 2 and b:
                        pe.wait_ge(*after("dve", "w", "m0b"))
                    for k in range(2):
                        last = mm(own(b, o), w("hawk", "Wga", 512 * k + 128 * o, 128), A(b, 5 + k),
                                  start=(k == 0), stop=(k == 1))
                    last.then_inc(*done("pe", b, f"g{o}"))
            for b in range(B):
                pe.wait_ge(*after("act", b, "ti1"))
            for par in range(2):
                p0 = 64 * par
                for b in range(B):
                    for blk in range(4):
                        q = 32 * ((2 * blk + par) % 4)
                        c = (b * 2 + blk // 2) * 128
                        last = mm(bank((1, 5)[par])[q:q + 32, c:c + 128],
                                  grid(VTs, 64)[p0:p0 + 64, blk, b * J:b * J + J],
                                  w("xa0", "Wo", 128 * blk, 128)[p0:p0 + 64, :], start=True, stop=True)
            last.then_inc(*done("pe", "w", "v0"))
            pe.wait_ge(loads["late"], 16)
            mm(bank(2)[:, 0:64], w("late", "Wk")[0:CD, :], ctxT[0:CD, :], start=True, stop=True)
            mm(bank(2)[:, 64:128], w("late", "Wv")[0:CD, :], ctxT[0:CD, :], start=True, stop=True)\
                .then_inc(*done("pe", "w", "k1"))
            pe.wait_ge(*after("dve", "w", "v0"))
            pe.wait_ge(*after("dve", "w", "k1"))
            for h in range(H1):
                p0 = 32 * h
                last = mm(bank(M1_BANKS[h])[:, 0:64], w("late", "WqT")[p0:p0 + 32, :], K1s[p0:p0 + 32, :], start=True,
                          stop=True)
            last.then_inc(*done("pe", "w", "m1"))
            pe.wait_ge(*after("dve", "w", "vr"))
            for b in range(B):
                mm(bank((2, 5)[b]), Vrep[:, 128 * b:128 * b + 128], w("late", "film"), start=True, stop=True)\
                    .then_inc(*done("pe", "w", f"f{b}"))
            for b in range(B):
                for k in range(2):
                    pe.wait_ge(*after("dve", b, f"gh{k}"))
                    last = mm(own(b, 0), w("hawk", "Wou", 128 * k, 128), A(b, 3 + k), start=(k == 0), stop=(k == 1))
                last.then_inc(*done("pe", b, "rg"))
            pe.wait_ge(*after("dve", "w", "m1"))
            pe.wait_ge(*after("dve", "w", "VF1"))
            for b in range(B):
                squares(b, "h4", 1)
            for b in range(B):
                pe.wait_ge(*after("dve", b, "xn2"))
                for i, blk in enumerate((0, 1, 2, 3)):
                    mm(own(b, i), w("hawk", "Wgr", 128 * blk, 128), A(b, 2), start=True, stop=True)\
                        .then_inc(*done("pe", b, f"gr{i}"))
            for b in range(B):
                for k in range(2):
                    pe.wait_ge(*after("dve", b, f"hm{k}"))
                    last = mm(own(b, 0), w("hawk", "Wsh", 128 * k, 128), A(b, 3 + k), start=(k == 0), stop=(k == 1))
                last.then_inc(*done("pe", b, "shr"))
            layernorm("ln1", "s1", 1)

            pe.wait_ge(loads["bf"], 16)
            pe.wait_ge(*after("dve", "w", "kb1"))
            for b in range(B):
                pe.wait_ge(*after("dve", b, "X1"))
                for p in range(2):
                    for i in range(2):
                        c = own(b, p)[:, 256 * i:256 * i + 256]
                        mm(c, Xin[b][:, 128 * (2 * p + i):128 * (2 * p + i) + 128], M0[:, b, :], start=True, stop=False)
                        last = mm(c, w("bf", "one")[0:1, :], krowb[:, 256 * b:256 * b + 256], start=False, stop=True)
                    last.then_inc(*done("pe", b, f"xa.s{p}"))
            kernel_products()
            pe.wait_ge(*after("act", "w", "kp"))
            for b in range(B):
                for p in range(2):
                    pe.wait_ge(*after("dve", b, f"xa.p{p}"))
                    for g in range(2):
                        for i in range(2):
                            tt = 128 * (2 * p + i)
                            last = tr(own(b, 2 + g)[:, tt:tt + 128],
                                      A(b, 2 + p)[:, 256 * i + 128 * g:256 * i + 128 * g + 128], w("sq", "id"))
                    last.then_inc(*done("pe", b, f"xa.t{p}"))
            for b in range(B):
                for g in range(2):
                    pe.wait_ge(*after("act", b, f"xa.a{g}"))
                    last = mm(own(b, 0), V0[:, b, g, :], A(b, 4 + g), start=(g == 0), stop=(g == 1))
                last.then_inc(*done("pe", b, "xa.o"))
            layernorm("ln2", "s2", 1)

            pe.wait_ge(kshuf, 16 * PA)
            pe.wait_ge(*after("act", 0, "xa.a1"))
            for j in range(NT):
                last = tr(bank(3)[:, 128 * j:128 * j + 128], Kdl[:, 128 * j:128 * j + 128], w("sq", "id"))
            last.then_inc(*done("pe", "w", "kt"))

            pe.wait_ge(loads["mla"], 16)
            for b in range(B):
                squares(b, "m1", 0)
            pe.wait_ge(*after("act", "w", "kl"))
            for b in range(B):
                pe.wait_ge(*after("dve", b, "xm"))
                mm(own(b, 1)[0:64, :], w("mla", "lat"), A(b, 2), start=True, stop=True).then_inc(*done("pe", b, "lat"))
                mm(own(b, 2), w("mla", "kr"), A(b, 2), start=True, stop=False)
                mm(own(b, 3), w("mla", "ks"), A(b, 2), start=True, stop=True)
                pe.wait_ge(*after("act", b, "lat"))
                mm(own(b, 2), w("mla", "kx")[0:32, :], A(b, 3)[0:32, :], start=False, stop=True)\
                    .then_inc(*done("pe", b, "kf"))
                mm(own(b, 0), w("mla", "q")[32:64, :], A(b, 3)[32:64, :], start=True, stop=True)\
                    .then_inc(*done("pe", b, "q0"))
                mm(own(b, 1), w("mla", "qs")[32:64, :], A(b, 3)[32:64, :], start=True, stop=True)\
                    .then_inc(*done("pe", b, "q1"))
                pe.wait_ge(*after("dve", b, "k2"))
                for i in range(NT):
                    last = mm(own(b, 3)[:, 128 * i:128 * i + 128], A(b, 3)[0:32, 128 * i:128 * i + 128],
                              w("mla", "v")[0:32, :], start=True, stop=True)
                last.then_inc(*done("pe", b, "v"))

            def blocks(ap, which):
                step = which[-1] - which[0]
                return grid(ap, 128)[:, which[0]:which[-1] + 1:step or 1, :]

            def max_unit(b, pair, u):
                hs = (2 * pair, 2 * pair + 1)
                n = 5 * pair + "ABCDE".index(u)
                ring = bank(n % 3)
                if n >= 3:
                    pe.wait_ge(*after("dve", b, f"mx{(n - 3) // 5}.{'ABCDE'[(n - 3) % 5]}"))
                elif b:
                    pe.wait_ge(*after("dve", 0, f"mx{NH // 2 - 1}.E"))
                    if n == 0:
                        pe.wait_ge(*after("act", 0, "nmt"))
                segs = {"A": [(hs[0], 3, 0)], "B": [(hs[0], 2, 0), (hs[0], 0, 384)],
                        "C": [(hs[1], 3, 0)], "D": [(hs[1], 2, 0), (hs[1], 0, 384)],
                        "E": [(hs[0], 1, 0), (hs[1], 1, 256)]}[u]
                for h, qt, c in segs:
                    n_ = 128 * (qt + 1)
                    mm(ring[:, c:c + n_], Qst[b][0:MROWS, h, 128 * qt:128 * qt + 128], Kst[b][0:MROWS, h, 0:n_],
                       start=(qt, c) == segs[0][1:], stop=False)
                masked = {"A": [3], "B": [2, 3], "C": [3], "D": [2, 3], "E": [1, 3]}[u]
                last = mm(blocks(ring, masked), w("bf", "id"), over(w("bf", "mS"), [128, len(masked), 128], 1),
                          start=False, stop=True)
                last.then_inc(*done("pe", b, f"mx{pair}.{u}"))

            def stream(i):
                b, n = divmod(i, GROUPS * UNITS)
                if b < B:
                    g, r_ = divmod(n, UNITS)
                    if i == 0:
                        pe.wait_ge(stack["m", 0], 16)
                    if n == 0 and b:
                        pe.wait_ge(stack["m", 1], 16)
                    if i >= 3:
                        bb, m = divmod(i - 3, GROUPS * UNITS)
                        pe.wait_ge(*after("act", bb, f"su{m}"))
                    segs = ([(r_, 0, 0)] if r_ < 4 else [(r_ - 4, 1, 0), (r_ - 4, 3, 384)] if r_ < 8 else
                            [(2 * (r_ - 8), 2, 0), (2 * (r_ - 8) + 1, 2, 256)])
                    for j, kb, c in segs:
                        n_ = T - 128 * kb
                        o = bank(3 + i % 3)[:, c:c + n_]
                        h = 4 * g + j
                        mm(o, Kst[b][0:KROWS, h, 128 * kb:128 * kb + 128], Qst[b][0:KROWS, h, 128 * kb:T],
                           start=(c == 0), stop=False)
                    masked = [c // 128 for _, _, c in segs]
                    last = mm(blocks(bank(3 + i % 3), masked), w("bf", "id"),
                              over(w("bf", "mT"), [128, len(masked), 128], 1), start=False, stop=True)
                    last.then_inc(*done("pe", b, f"su{n}"))
                for lane in ((b, n), (b - 1, n + GROUPS * UNITS)):
                    if 0 <= lane[0] < B and (lane[1] < GROUPS * UNITS + LAG):
                        for kind, g, stage in attention_events(lane[1]):
                            (values if kind == "pv" else turn_values)(lane[0], g, stage)

            def values(b, g, stage):
                pe.wait_ge(*after("act", b, f"su{g * UNITS + {0: 3, 1: 7, 2: 9}[stage]}"))
                if stage == 0 and (g or b):
                    pe.wait_ge(*after("act", *((b, f"yc{g - 1}") if g else (b - 1, f"yc{GROUPS - 1}"))))
                for kb in ((0,), (1, 3), (2,))[stage]:
                    for j in range(4):
                        n_ = T - 128 * kb
                        u, c = {0: (j, 0), 1: (4 + j, 0), 3: (4 + j, 384), 2: (8 + j // 2, 256 * (j % 2))}[kb]
                        last = mm(bank(6)[32 * j:32 * j + HD + 1, 128 * kb:T], Vaug[b][:, kb, 4 * g + j, :],
                                  P[u][:, c:c + n_], start=(kb == 0), stop=(kb == 2))
                last.then_inc(*done("pe", b, f"pv{g}.{stage}"))

            def turn_values(b, g, _):
                pe.wait_ge(*after("act", b, f"yc{g}"))
                if g or b:
                    pe.wait_ge(*after("dve", *((b, f"y{g - 1}") if g else (b - 1, f"y{GROUPS - 1}"))))
                for t in range(NT):
                    last = tr(bank(7)[:, 128 * t:128 * t + 128], A(b, 6)[:, 128 * t:128 * t + 128], w("sq", "id"))
                last.then_inc(*done("pe", b, f"yT{g}"))

            def minus_max(b):
                pe.wait_ge(*after("dve", b, "nl"))
                for i in range(NT):
                    last = tr(bank(0).bitcast(BF16)[0:48, 128 * i:128 * i + 128], spb[b][:, i, :], w("bf", "id"))
                last.then_inc(*done("pe", b, "nmt"))

            def attention_out(b):
                pe.wait_ge(*after("dve", b, f"y{GROUPS - 1}"))
                for i in range(NT):
                    last = tr(own(b, 0)[:, 128 * i:128 * i + 128], A(b, 4)[:, 128 * i:128 * i + 128], w("sq", "id"))
                last.then_inc(*done("pe", b, "yt"))

            def project_out(b):
                pe.wait_ge(*after("act", b, "yt"))
                mm(own(b, 1), w("mla", "o"), A(b, 5), start=True, stop=True).then_inc(*done("pe", b, "mo"))

            pe.wait_ge(*after("act", 0, "v"))
            pe.wait_ge(*after("dve", 0, "q2"))
            pe.wait_ge(stack["k", 0], 16 * (PRODUCTS + 1))
            pe.wait_ge(stack["q", 0], 16 * (PRODUCTS + 1))
            for pair in PAIRS:
                for u in "ABCDE":
                    max_unit(0, pair, u)
            minus_max(0)
            pe.wait_ge(*after("act", 1, "v"))
            pe.wait_ge(*after("dve", 1, "q2"))
            pe.wait_ge(stack["k", 1], 16 * (PRODUCTS + 1))
            pe.wait_ge(stack["q", 1], 16 * (PRODUCTS + 1))
            total = GROUPS * UNITS
            for k in range(5 * NH // 2):
                max_unit(1, k // 5, "ABCDE"[k % 5])
                if k >= 6:
                    stream(k - 6)
            for i in range(total - 6, total - 2):
                stream(i)
            minus_max(1)
            def route(b, r, group, name, n, i):
                for t in range(NT):
                    last = mm(own(b, i)[:, n * t:n * t + n], A(b, 2)[:, 128 * t:128 * t + 128], w(group, name),
                              start=True, stop=True)
                last.then_inc(*done("pe", b, r))

            for i in range(total - 2, 2 * total + LAG):
                stream(i)
                if i == total + 14:
                    pe.wait_ge(*after("act", 1, "nmt"))
                    attention_out(0)
                if i == total + 17:
                    project_out(0)
                if i == total + 22:
                    squares(0, "f1", 0)
                if i == total + 35:
                    pe.wait_ge(loads["moe0"], 16)
                    pe.wait_ge(*after("dve", 0, "xf"))
                    route(0, "rt", "moe0", "r", E0, 2)
            attention_out(1)
            project_out(1)

            def turn_weights(b, name, ready, n, i):
                pe.wait_ge(*after("dve", "w", ready))
                for t in range(NT):
                    last = tr(own(b, i).bitcast(BF16)[0:n, 128 * t:128 * t + 128], spb[b][:, t, 0:n], w("bf", "id"))
                last.then_inc(*done("pe", b, name))


            def unit(b, k, units, shared, group, sel, e, x, p, silu, up, weighted, wl, wt):
                if k < units:
                    if k:
                        pe.wait_ge(*after("act", b, f"{silu}{k - 1}"))
                    mm(own(b, 0), w(group, "g", 128 * k, 128), x, start=True, stop=True)\
                        .then_inc(*done("pe", b, f"{p}g{k}"))
                    if k:
                        pe.wait_ge(*after("dve", b, f"{up}{k - 1}"))
                    mm(own(b, 1), w(group, "u", 128 * k, 128), x, start=True, stop=True)\
                        .then_inc(*done("pe", b, f"{p}u{k}"))
                    if k == shared:
                        turn_weights(b, f"{p}wt", wl, 3 * e, 2)
                        pe.wait_ge(*after("act", b, wt))
                    elif k > shared:
                        pe.wait_ge(*after("dve", b, f"{weighted}{k - 1}"))
                    if k >= shared:
                        mm(own(b, 2), w(sel, "s", 128 * (k - shared), 128)[0:3 * e, :], wT[b][0:3 * e, :], start=True,
                           stop=True).then_inc(*done("pe", b, f"{p}w{k}"))
                if k:
                    j = k - 1
                    pe.wait_ge(*after("dve", b, f"{weighted if j >= shared else up}{j}"))
                    mm(own(b, 3), w(group, "d", 128 * j, 128), A(b, 6 + j % 2), start=(j == 0), stop=(k == units))\
                        .then_inc(*done("pe", b, f"{p}d{k}"))

            def first_unit(b, k):
                unit(b, k, U0, SH0, "moe0", "sel0", E0, A(b, 2), "f", "sl", "hu", "hw", "wl", "wt")

            squares(1, "f1", 0)
            first_unit(0, 0)
            pe.wait_ge(*after("dve", 1, "xf"))
            route(1, "rt", "moe0", "r", E0, 2)
            first_unit(1, 0)
            pe.wait_ge(loads["sel0"], 16)
            for k in range(1, U0 + 1):
                for b in range(B):
                    first_unit(b, k)
            layernorm("ln3", "s3", 0)

            pe.wait_ge(loads["selA"], 16)
            for b in range(B):
                pe.wait_ge(*after("dve", b, "X3"))
                mm(own(b, 0)[0:96, :], w("late", "WBC"), Xin[b][:, :], start=True, stop=True)\
                    .then_inc(*done("pe", b, "bc"))
                mm(own(b, 1), w("late", "Wd"), Xin[b][:, :], start=True, stop=True).then_inc(*done("pe", b, "de"))
            def state_products(b, i):
                parts_bc = A(b, 3)[:, 0:256].bitcast(BF16)
                if i < 0:
                    pe.wait_ge(*after("dve", b, "bl"))
                elif i == 0:
                    pe.wait_ge(*after("dve", b, "rl"))
                if i + 1 < NS:
                    if i >= 1:
                        pe.wait_ge(*after("act", b, f"bb{i - 1}"))
                    mm(own(b, 3 * ((i + 1) % 2)), w("selA", "s", 128 * (i + 1), 128)[0:96, :], parts_bc[0:96, :],
                       start=True, stop=True).then_inc(*done("pe", b, f"bn{i + 1}"))
                if 0 <= i < NS:
                    if i:
                        pe.wait_ge(*after("dve", b, f"hc{i - 1}"))
                    mm(own(b, 1), w("selA", "s", 128 * (NS + i), 128)[0:96, :], parts_bc[0:96, :], start=True,
                       stop=True).then_inc(*done("pe", b, f"cn{i}"))
                if i > 0:
                    pe.wait_ge(*after("dve", b, f"hc{i - 1}"))
                    mm(own(b, 2), w("sq", "id"), A(b, 12 + (i - 1) % 2), start=(i == 1), stop=(i == NS))\
                        .then_inc(*done("pe", b, f"yn{i}"))

            for b in range(B):
                for i in (-1, 0):
                    state_products(b, i)
            for i in range(1, NS + 1):
                for b in range(B):
                    state_products(b, i)
            layernorm("ln4", "s4", 0)

            for b in range(B):
                pe.wait_ge(*after("dve", b, "X4"))
            pe.wait_ge(loads["dft"], 16)

            def forward(o, c, f, rhs):
                for j in range(NT):
                    last = mm(o, w("dft", "F", 1024 * j + 512 * c + 128 * f, 128), rhs(j), start=(j == 0),
                              stop=(j == NT - 1))
                return last

            for b in range(B):
                mm(own(b, 0), w("sq", "Cm"), Xin[b][:, :], start=True, stop=True).then_inc(*done("pe", b, "lni.c"))
            for b in range(B):
                for i in range(NT):
                    c = own(b, 2)[:, 128 * i:128 * i + 128]
                    mm(c, Xin[b][:, 128 * i:128 * i + 128], M1[:, b, :], start=True, stop=False)
                    last = mm(c, w("bf", "one")[0:1, :], krowb[:, 512 + 128 * b:640 + 128 * b], start=False, stop=True)
                last.then_inc(*done("pe", b, "xb.s"))
            mean_squares("lni", 1)
            for c in range(2):
                pe.wait_ge(*after("dve", c, "xb.d"))
                for f in range(NFB):
                    last = forward(bank((2, 6)[c])[:, 128 * f:128 * f + 128], c, f, lambda j: KL[:, j, :])
                last.then_inc(*done("pe", "w", f"kf{c}"))
            for b in range(B):
                pe.wait_ge(*after("dve", b, "xb.p"))
                for i in range(NT):
                    last = tr(own(b, 3)[:, 128 * i:128 * i + 128], A(b, 2)[:, 128 * i:128 * i + 128], w("sq", "id"))
                last.then_inc(*done("pe", b, "xb.t"))
            pe.wait_ge(*after("act", "w", "kf1"))
            for b in range(B):
                pe.wait_ge(*after("act", b, "xb.a"))
                pe.wait_ge(*after("dve", b, "lni.x"))
                for o in range(4):
                    mm(own(b, o), VF[:, b, 128 * o:128 * o + 128], A(b, 3), start=True, stop=True)\
                        .then_inc(*done("pe", b, f"fl{o}"))
            for b in range(B):
                pe.wait_ge(*after("dve", b, "xin"))
                pe.wait_ge(*after("act", b, "s3"))
                for j in range(NT):
                    last = tr(own(b, 2)[:, 128 * j:128 * j + 128], A(b, 2)[:, 128 * j:128 * j + 128], w("sq", "id"))
                last.then_inc(*done("pe", b, "xit"))

            for b in range(B):
                pe.wait_ge(*after("act", b, "xit"))
                pe.wait_ge(*after("dve", b, "lni.x"))
            for h in range(2):
                for c in range(2):
                    for f in range(2):
                        last = forward(bank(4 * h + 2 * c)[:, 256 * f:256 * f + 256], c, 2 * h + f,
                                       lambda j: XT[:, j, :, :].rearrange("p b d -> p (b d)"))
                    last.then_inc(*done("pe", "w", f"xf{h}{c}"))
            for h in range(2):
                pe.wait_ge(*after("dve", "w", f"yi{h}"))
                for b in range(B):
                    for c in range(2):
                        for f in (2 * h, 2 * h + 1):
                            last = mm(own(b, 1), Yf[:, c, f, 128 * b:128 * b + 128],
                                      w("dft", "G", (NFB * c + f) * T, T), start=(h == c == 0 and f == 0),
                                      stop=(h == c == 1 and f == 3))
                    if h:
                        last.then_inc(*done("pe", b, "inv"))
            layernorm("lnf", "xt", 2)
            for b in range(B):
                pe.wait_ge(*after("act", b, "lnf.g"))
                for o in range(4):
                    mm(own(b, o), w("late", "W1", 128 * o, 128), A(b, 2), start=True, stop=True)\
                        .then_inc(*done("pe", b, f"w1{o}"))
            for b in range(B):
                for k in range(4):
                    pe.wait_ge(*after("act", b, f"u{k}"))
                    last = mm(own(b, 0), w("late", "W2", 128 * k, 128), A(b, 6 + k), start=(k == 0), stop=(k == 3))
                last.then_inc(*done("pe", b, "w2"))
            layernorm("lno", "xt2", 1)
            layernorm("ln5", "s5", 1)

            def second_unit(b, k):
                unit(b, k, UB1, SH1, "ffn1", "sel1", E1, Xin[b][:, :], "e", "el", "eu", "ew", "wl1", "wt1")

            for b in range(B):
                pe.wait_ge(*after("dve", b, "X5"))
                for t in range(NT):
                    last = mm(own(b, 2)[:, E1 * t:E1 * t + E1], Xin[b][:, 128 * t:128 * t + 128], w("late", "gate"),
                              start=True, stop=True)
                last.then_inc(*done("pe", b, "rt1"))
                if b == 0:
                    pe.wait_ge(loads["ffn1"], 16)
                second_unit(b, 0)
            pe.wait_ge(loads["sel1"], 16)
            for k in range(1, UB1 + 1):
                for b in range(B):
                    second_unit(b, k)
            layernorm("ln6", "s6", 0)

        @block.scalar
        def _(act):
            def f(out_, in_, func, step, bias=0.0, scale=1.0):
                nc.scalar.activation(out_, in_, func, bias=bias, scale=scale).then_inc(*done("act", *step))

            def layernorm(t, i=0):
                for b in range(B):
                    act.wait_ge(*after("pe", b, f"{t}.c"))
                    f(A(b, 1), own(b, i), ACT.Square, (b, f"{t}.sq"))
                for b in range(B):
                    act.wait_ge(*after("pe", b, f"{t}.v"))
                    f(A(b, 7), own(b, i + 1), ACT.Ln, (b, f"{t}.l"), scale=1.0 / D, bias=vec("eps"))
                    act.wait_ge(*after("act", b, f"{t}.l"))
                    f(A(b, 7), A(b, 7), ACT.Exp, (b, f"{t}.r"), scale=-0.5)

            def root_mean_square(t, i):
                for b in range(B):
                    act.wait_ge(*after("pe", b, f"{t}.ss"))
                    f(A(b, 7), own(b, i), ACT.Ln, (b, f"{t}.l"), scale=1.0 / D)
                    act.wait_ge(*after("act", b, f"{t}.l"))
                    f(A(b, 7), A(b, 7), ACT.Exp, (b, f"{t}.r"), scale=-0.5)

            def root_plus_eps(b, t, step):
                if step == "l":
                    act.wait_ge(*after("pe", b, f"{t}.ss"))
                    f(A(b, 7), own(b, 0), ACT.Ln, (b, f"{t}.l"), scale=1.0 / D)
                elif step == "n":
                    act.wait_ge(*after("act", b, f"{t}.l"))
                    f(A(b, 7), A(b, 7), ACT.Exp, (b, f"{t}.n"), scale=0.5)
                elif step == "m":
                    act.wait_ge(*after("act", b, f"{t}.n"))
                    f(A(b, 7), A(b, 7), ACT.Ln, (b, f"{t}.m"), bias=vec("eps"))
                else:
                    act.wait_ge(*after("act", b, f"{t}.m"))
                    f(A(b, 7), A(b, 7), ACT.Exp, (b, f"{t}.r"), scale=-1.0)

            def table(name):
                nc.scalar.preload_act_table_set(
                    {"exp": "natural_log_exp_and_others", "gelu": "gelu_and_others", "silu": "silu_and_others"}[name])

            table("exp")
            for b in range(B):
                act.wait_ge(loads[f"x{b}"], 16)
                f(A(b, 1), Xin[b][:, :], ACT.Square, (b, "h1.sq"))
            act.wait_ge(loads["vec"], 16)
            f(fb_a, w("vec", "fb"), ACT.Abs, ("w", "fb.a"))
            act.wait_ge(*after("act", "w", "fb.a"))
            f(fb_e, fb_a, ACT.Exp, ("w", "fb.e"), scale=-1.0)
            act.wait_ge(*after("act", "w", "fb.e"))
            f(fb_l, fb_e, ACT.Ln, ("w", "fb.l"), bias=vec("one"))
            act.wait_ge(loads["s4d"], 16)
            f(dct(0), w("s4d", "ldt"), ACT.Exp, ("w", "dt"))
            root_mean_square("h1", 0)

            table("silu")
            act.wait_ge(*after("dve", "w", "z9"))
            f(dct(3), dct(1), ACT.Tanh, ("w", "th"), scale=0.5)
            f(dct(6), dct(5), ACT.Sin, ("w", "sh"), scale=TWO_PI)
            f(dct(7), dct(7), ACT.Sin, ("w", "sy"), scale=TWO_PI)
            table("gelu")
            for b in range(B):
                for k in range(2):
                    act.wait_ge(*after("pe", b, f"z{k}"))
                    f(A(b, 5 + k), own(b, k), ACT.Identity, (b, f"cv{k}"), scale=vec("cw", 4 * k + 3), bias=vec("cb", k))
                for k in range(2):
                    act.wait_ge(*after("pe", b, f"z{2 + k}"))
                    f(A(b, 3 + k), own(b, 2 + k), ACT.Gelu, (b, f"gg{k}"))
            act.wait_ge(*after("pe", "w", "kv"))
            f(KTs, bank(2)[:, 0:256], ACT.Copy, ("w", "kv0"))
            f(VTs, bank(3)[:, 0:256], ACT.Copy, ("w", "kv"))
            table("silu")
            act.wait_ge(*after("pool", "w", "bh"))
            act.wait_ge(*after("pool", "w", "fb.c"))
            for b in range(B):
                for o, name in enumerate(("tf0", "tf1", "ti0", "ti1")):
                    act.wait_ge(*after("pe", b, f"g{o}"))
                    f(A(b, 7 + o), own(b, o), ACT.Tanh, (b, name), scale=0.5, bias=bhalf[:, o:o + 1])
            act.wait_ge(*after("dve", "w", "q2"))
            f(tb("p1"), tb("p1"), ACT.Sin, ("w", "s1"), scale=-TWO_PI, bias=vec("ra1"))
            f(tb("p2"), tb("p2"), ACT.Sin, ("w", "s2"), scale=-TWO_PI, bias=vec("ra2"))
            table("exp")
            for b in range(B):
                for k in range(2):
                    act.wait_ge(*after("act", b, f"tf{k}"))
                    f(A(b, 7 + k), A(b, 7 + k), ACT.Exp, (b, f"al{k}"), scale=fcoef[:, k:k + 1], bias=fcoef[:, k:k + 1])
                for k in range(2):
                    act.wait_ge(*after("act", b, f"al{k}"))
                    f(A(b, 1 + k), A(b, 7 + k), ACT.Square, (b, f"sa{k}"))
                for k in range(2):
                    act.wait_ge(*after("act", b, f"sa{k}"))
                    f(A(b, 1 + k), A(b, 1 + k), ACT.Ln, (b, f"lb{k}"), scale=-0.25, bias=vec("q25"))
                for k in range(2):
                    act.wait_ge(*after("act", b, f"lb{k}"))
                    f(A(b, 1 + k), A(b, 1 + k), ACT.Exp, (b, f"hb{k}"), scale=0.5)
            act.wait_ge(*after("pool", "w", "aP"))
            f(PT, PT, ACT.Exp, ("w", "eP"))
            act.wait_ge(*after("pool", "w", "aQ"))
            f(QT, QT, ACT.Exp, ("w", "eQ"))
            for b in range(B):
                act.wait_ge(*after("dve", b, "x1"))
                f(A(b, 1), A(b, 5), ACT.Square, (b, "h4.sq"))
            root_mean_square("h4", 1)
            table("gelu")

            for b in range(B):
                for k in range(2):
                    act.wait_ge(*after("pe", b, f"gr{k}"))
                    f(A(b, 3 + k), own(b, k), ACT.Gelu, (b, f"gm{k}"))
            table("silu")
            act.wait_ge(*after("dve", "w", "qQ1"))
            f(tb("tQ"), tb("tQ"), ACT.Sin, ("w", "sQ"), scale=-TWO_PI, bias=vec("raq"))
            table("exp")
            layernorm("ln1", 1)

            for b in range(B):
                for p in range(2):
                    act.wait_ge(*after("dve", b, f"xa.d{p}"))
                    f(A(b, 2 + p), A(b, 2 + p), ACT.Exp, (b, f"xa.e{p}"))
            act.wait_ge(*after("pe", "w", "kp"))
            f(Ksb, PS[:, 2:4, :].rearrange("p a t -> p (a t)"), ACT.Copy, ("w", "kp"))
            for b in range(B):
                act.wait_ge(*after("pe", b, "xa.t1"))
                for g in range(2):
                    f(A(b, 4 + g), own(b, 2 + g), ACT.Copy, (b, f"xa.a{g}"))
            layernorm("ln2", 1)

            for b in range(B):
                act.wait_ge(*after("dve", b, "X2"))
                f(A(b, 1), Xin[b][:, :], ACT.Square, (b, "m1.sq"))
            act.wait_ge(*after("pe", "w", "kt"))
            f(KL[:, :, :].rearrange("p j d -> p (j d)"), bank(3), ACT.Copy, ("w", "kl"))
            for b in range(B):
                for step in "lnmr":
                    root_plus_eps(b, "m1", step)
            for b in range(B):
                act.wait_ge(*after("pe", b, "lat"))
                f(A(b, 3)[0:64, :], own(b, 1)[0:64, :], ACT.Copy, (b, "lat"))
            for b in range(B):
                for whole, rest, parts, n in (("kk", "kr", KP[b], "k"), ("qq", "qr", QP[b], "q")):
                    act.wait_ge(*after(splitter(b), b, whole))
                    f(parts[0], A(b, {"k": 5, "q": 4}[n]), ACT.Copy, (b, f"{n}h"))
                for whole, rest, parts, n in (("kk", "kr", KP[b], "k"), ("qq", "qr", QP[b], "q")):
                    act.wait_ge(*after(splitter(b), b, rest))
                    f(parts[1], A(b, {"k": 6, "q": 1}[n]), ACT.Copy, (b, f"{n}m"))
                act.wait_ge(*after("pe", b, "v"))
                act.wait_ge(*after("pool", "w", f"va{b}"))
                f(Vaug[b][:, :, :, 0:HD], own(b, 3).rearrange("p (i h d) -> p i h d", i=NT, d=HD), ACT.Copy, (b, "v"))

            def parts_of_max(b):
                act.wait_ge(*after("pe", b, "nmt"))
                f(wT[b][0:48, :], bank(0).bitcast(BF16)[0:48, 0:T], ACT.Copy, (b, "nmt"))

            def stream(i):
                b, n = divmod(i, GROUPS * UNITS)
                if b < B:
                    act.wait_ge(*after("pe", b, f"su{n}"))
                    g, r_ = divmod(n, UNITS)
                    if g or b:
                        stage = 0 if r_ < 4 else 1 if r_ < 8 else 2
                        act.wait_ge(*after("pe", *((b, f"pv{g - 1}.{stage}") if g
                                                   else (b - 1, f"pv{GROUPS - 1}.{stage}"))))
                    f(P[r_], bank(3 + i % 3), ACT.Exp, (b, f"su{n}"))
                for lane, m in ((b, n - YC_LAG), (b - 1, n - YC_LAG + GROUPS * UNITS)):
                    if 0 <= lane < B and m % UNITS == 0 and 0 <= m < GROUPS * UNITS:
                        sums(lane, m // UNITS)

            def sums(b, g):
                act.wait_ge(*after("pe", b, f"pv{g}.2"))
                if g:
                    act.wait_ge(*after("pe", b, f"yT{g - 1}"))
                f(A(b, 6), bank(6), ACT.Copy, (b, f"yc{g}"))

            parts_of_max(0)
            total = GROUPS * UNITS
            for i in range(total - 2):
                stream(i)
            parts_of_max(1)

            def attention_out(b):
                act.wait_ge(*after("pe", b, "yt"))
                f(A(b, 5), own(b, 0), ACT.Copy, (b, "yt"))

            def squared(b):
                act.wait_ge(*after("dve", b, "x2a"))
                f(A(b, 1), A(b, 3), ACT.Square, (b, "f1.sq"))

            for i in range(total - 2, 2 * total + LAG):
                stream(i)
                if i == total + 14:
                    attention_out(0)
                if i == total + 20:
                    squared(0)
                if total + 23 <= i < total + 27:
                    root_plus_eps(0, "f1", "lnmr"[i - total - 23])
            attention_out(1)

            squared(1)
            for step in "lnmr":
                root_plus_eps(1, "f1", step)
            for b in range(B):
                act.wait_ge(*after("dve", b, "lg"))
            f(routing(64, B * NT * E0), routing(0, B * NT * E0), ACT.Exp, ("w", "rt"), scale=-1.0)
            table("silu")

            def gates(units, shared, p, silu, up, wt, e):
                for k in range(units):
                    for b in range(B):
                        act.wait_ge(*after("pe", b, f"{p}g{k}"))
                        if k >= 2:
                            act.wait_ge(*after("dve", b, f"{up}{k - 2}"))
                        f(A(b, 4 + k % 2), own(b, 0), ACT.Silu, (b, f"{silu}{k}"))
                        if k == shared:
                            act.wait_ge(*after("pe", b, f"{p}wt"))
                            f(wT[b][0:3 * e, :], own(b, 2).bitcast(BF16)[0:3 * e, 0:T], ACT.Copy, (b, wt))

            gates(U0, SH0, "f", "sl", "hu", "wt", E0)
            table("exp")
            layernorm("ln3")

            def scan_input(b, name):
                if name == "bc":
                    act.wait_ge(*after("pe", b, "bc"))
                    f(A(b, 2)[0:96, :], own(b, 0)[0:96, :], ACT.Identity, (b, "bc"), bias=vec("bBC")[0:96, :])
                elif name == "ab":
                    act.wait_ge(*after("pe", b, "de"))
                    f(A(b, 7), own(b, 1), ACT.Abs, (b, "ab"), bias=vec("bd"))
                elif name == "ex":
                    act.wait_ge(*after("act", b, "ab"))
                    f(A(b, 7), A(b, 7), ACT.Exp, (b, "ex"), scale=-1.0)
                else:
                    act.wait_ge(*after("act", b, "ex"))
                    f(A(b, 7), A(b, 7), ACT.Ln, (b, "sp"), bias=vec("one"))

            for b, name in ((0, "bc"), (0, "ab"), (0, "ex"), (1, "bc"), (0, "sp"), (1, "ab"), (1, "ex"), (1, "sp")):
                scan_input(b, name)
            for i in range(NS):
                for b in range(B):
                    if i == 0:
                        act.wait_ge(*after("dve", b, "dl"))
                    if i >= 2:
                        act.wait_ge(*after("dve", b, f"sc{i - 2}"))
                    f(A(b, 9 + i % 2), A(b, 8), ACT.Exp, (b, f"aa{i}"), scale=w("vec", "A", i, 1))
                    act.wait_ge(*after("pe", b, f"bn{i}"))
                    f(A(b, 4 + i % 2), own(b, 3 * (i % 2)), ACT.Copy, (b, f"bb{i}"))
            layernorm("ln4")
            def affine(b, t, src, dst, g, off):
                act.wait_ge(*after("dve", b, f"{t}.x"))
                f(A(b, dst), A(b, src), ACT.Identity, (b, f"{t}.g"), scale=vec(g), bias=vec(off))

            layernorm("lni")
            for b in range(B):
                act.wait_ge(*after("dve", b, "xb.d"))
                f(A(b, 2), A(b, 2), ACT.Exp, (b, "xb.e"))
            for b in range(B):
                affine(b, "lni", 9, 10, "gni", "bni")
            for c in range(2):
                act.wait_ge(*after("pe", "w", f"kf{c}"))
                f(Kf[:, c, :, :].rearrange("p f d -> p (f d)"), bank((2, 6)[c]), ACT.Copy, ("w", f"kf{c}"))
            for b in range(B):
                act.wait_ge(*after("pe", b, "xb.t"))
                f(A(b, 3), own(b, 3), ACT.Copy, (b, "xb.a"))
            act.wait_ge(*after("pool", "w", "bf1"))
            for b in range(B):
                for o, to in enumerate((4, 5, 6, 8)):
                    act.wait_ge(*after("pe", b, f"fl{o}"))
                    f(A(b, to), own(b, o), ACT.Identity, (b, f"s{o}"), bias=bfilm[:, o:o + 1])

            for b in range(B):
                act.wait_ge(*after("pe", b, "xit"))
                f(XT[:, :, b, :], own(b, 2).rearrange("p (j d) -> p j d", d=128), ACT.Copy, (b, "xit"))
            layernorm("lnf", 2)
            for b in range(B):
                affine(b, "lnf", 9, 2, "gff", "bff")
            table("gelu")
            for b in range(B):
                for k in range(4):
                    act.wait_ge(*after("pe", b, f"w1{k}"))
                    f(A(b, 6 + k), own(b, k), ACT.Gelu, (b, f"u{k}"), bias=vec("b1", k))
            table("exp")
            layernorm("lno", 1)
            for b in range(B):
                affine(b, "lno", 9, 10, "gno", "bno")
            layernorm("ln5", 1)

            for b in range(B):
                act.wait_ge(*after("dve", b, "ms"))
            f(routing(64, B * NT * E1), routing(0, B * NT * E1), ACT.Exp, ("w", "rt1"))
            table("silu")
            gates(UB1, SH1, "e", "el", "eu", "wt1", E1)
            table("exp")
            layernorm("ln6")

        @block.vector
        def _(dve):
            def tt(out_, a, b_, op, step):
                nc.vector.tensor_tensor(out_, a, b_, op).then_inc(*done("dve", *step))

            def ts(out_, a, s1, s2, op0, op1, step):
                nc.vector.tensor_scalar(out_, a, s1, s2, op0, op1).then_inc(*done("dve", *step))

            def stt(out_, a, s1, b_, op0, op1, step):
                nc.vector.scalar_tensor_tensor(out_, a, s1, b_, op0, op1).then_inc(*done("dve", *step))

            def red(out_, a, op, step):
                nc.vector.tensor_reduce(out_, a, X, op).then_inc(*done("dve", *step))

            def inv(out_, a, step):
                nc.vector.reciprocal(out_, a).then_inc(*done("dve", *step))

            def mine(lane, name):
                dve.wait_ge(*after("dve", lane, name))

            def normed(b, t, name, i, x=None):
                dve.wait_ge(*after("act", b, f"{t}.r"))
                tt(Xin[b][:, :], own(b, i), A(b, 7), ALU.mult, (b, name))

            for n in ("km", "kr", "tm"):
                dve.wait_ge(loads[n], 16)
            nc.vector.tensor_copy(kmaskf, kmask).then_inc(*done("dve", "w", "km"))
            nc.vector.tensor_copy(krowb[:, :], krow).then_inc(*done("dve", "w", "kb0"))
            mine("w", "kb0")
            ts(krowb[:, :], krowb[:, :], -1.0, BIG, ALU.add, ALU.mult, ("w", "kb1"))
            nc.vector.tensor_copy(tmaskf[:, :], tmask).then_inc(*done("dve", "w", "tm"))

            link = [0]

            def chain(prefix, op, *a):
                link[0] += 1
                op(*a, ("w", f"{prefix}{link[0]}"))
                mine("w", f"{prefix}{link[0]}")

            for b in range(B):
                dve.wait_ge(*after("act", b, "h1.r"))
                stt(A(b, 2), Xin[b][:, :], vec("g1"), A(b, 7), ALU.mult, ALU.mult, (b, "xn1"))
            dve.wait_ge(*after("act", "w", "dt"))
            chain("z", tt, dct(1), w("s4d", "Are"), dct(0), ALU.mult)
            chain("z", tt, dct(2), w("s4d", "Aim"), dct(0), ALU.mult)
            chain("z", ts, dct(4), dct(2), 1.0 / (2.0 * math.pi), None, ALU.mult, ALU.bypass)
            chain("z", ts, dct(5), dct(4), 0.5, None, ALU.mult, ALU.bypass)
            chain("z", ts, dct(6), dct(5), ROUND, None, ALU.add, ALU.bypass)
            chain("z", stt, dct(6), dct(6), ROUND, dct(5), ALU.subtract, ALU.subtract)
            chain("z", ts, dct(5), dct(6), -1.0, None, ALU.mult, ALU.bypass)
            chain("z", ts, dct(7), dct(4), ROUND, ROUND, ALU.add, ALU.subtract)
            chain("z", tt, dct(7), dct(4), dct(7), ALU.subtract)

            link[0] = 0
            chain("a", tt, dct(11), w("s4d", "Are"), w("s4d", "Are"), ALU.mult)
            chain("a", tt, dct(9), w("s4d", "Aim"), w("s4d", "Aim"), ALU.mult)
            chain("a", tt, dct(11), dct(11), dct(9), ALU.add)
            chain("a", inv, dct(11), dct(11))

            def turns(t_, to, r_, ph, names):
                ts(r_, t_, vec(ph), ROUND, ALU.add, ALU.add, ("w", names[0]))
                mine("w", names[0])
                stt(to, r_, ROUND, t_, ALU.subtract, ALU.subtract, ("w", names[1]))

            dve.wait_ge(*after("act", "w", "sy"))
            chain("a", ts, dct(8), dct(3), -1.0, 1.0, ALU.mult, ALU.add)
            chain("a", inv, dct(8), dct(8))
            for b in range(B):
                for tap in (2, 1, 0):
                    for k in range(2):
                        if tap == 2:
                            dve.wait_ge(*after("act", b, f"cv{k}"))
                        else:
                            mine(b, f"cw{k}.{tap + 1}")
                        n = T - (3 - tap)
                        stt(A(b, 5 + k)[:, 3 - tap:T], own(b, k)[:, 0:n], vec("cw", 4 * k + tap),
                            A(b, 5 + k)[:, 3 - tap:T], ALU.mult, ALU.add, (b, f"cw{k}.{tap}"))
            rP = tb("rQ").rearrange("p d l -> p (d l)").rearrange("p (d l) -> p d l", l=PA)
            dve.wait_ge(*after("pool", "w", "tP"))
            turns(tb("p2"), tb("p1"), rP, "ph1", ("r1", "q1"))
            mine("w", "q1")
            turns(tb("p2"), tb("p2"), rP, "ph2", ("r2", "q2"))
            dve.wait_ge(*after("pool", "w", "tQ"))
            mine("w", "q2")

            def turns_q(c):
                d = slice(64 * c, 64 * c + 64)
                turns(tb("tQ")[:, d, :], tb("tQ")[:, d, :], tb("rQ"), "phq", (f"rQ{c}", f"qQ{c}"))

            turns_q(0)
            mine("w", "km")
            dve.wait_ge(*after("pe", "w", "m0"))
            for par in range(2):
                for b in range(B):
                    last = nc.vector.scalar_tensor_tensor(
                        M0[:, b, :].rearrange("p (k two j) -> p two k j", two=2, j=J)[:, par],
                        bank(6 + par)[:, 0:256].rearrange("p (k b j) -> p b k j", b=B, j=J)[:, b], 64.0 ** -0.5,
                        kmaskf.rearrange("p (b k two j) -> p b two k j", b=B, two=2, j=J)[:, b, par],
                        ALU.mult, ALU.mult)
                last.then_inc(*done("dve", "w", "m0" + "ab"[par]))
            for b in range(B):
                for k in range(2):
                    dve.wait_ge(*after("act", b, f"ti{k}"))
                    stt(A(b, 9 + k), A(b, 9 + k), 1.0, A(b, 5 + k), ALU.add, ALU.mult, (b, f"in{k}"))
            mine("w", "qQ0")
            turns_q(1)
            dve.wait_ge(*after("pe", "w", "v0"))
            for q in range(4):
                last = nc.vector.tensor_copy(V0[32 * q:32 * q + 32, :, :, :].rearrange("p b g n -> p (b g n)"),
                                             bank((1, 5)[q % 2])[32 * q:32 * q + 32, :])
            last.then_inc(*done("dve", "w", "v0"))
            dve.wait_ge(*after("pe", "w", "k1"))
            nc.vector.tensor_copy(K1s, bank(2)[:, 0:64]).then_inc(*done("dve", "w", "k1"))
            for c in range(B):
                last = nc.vector.tensor_copy(Vrep[:, 128 * c:128 * c + 128].rearrange("p (h g) -> p h g", g=J),
                                             over(bank(2)[:, 64 + J * c:64 + J * c + J], [128, H1, J], 1))
            last.then_inc(*done("dve", "w", "vr"))
            dve.wait_ge(*after("pe", "w", "m1"))
            for h in range(H1):
                last = nc.vector.tensor_scalar(M1[:, :, J * h:J * h + J], grid(bank(M1_BANKS[h])[:, 0:64], J),
                                               32.0 ** -0.5, None, ALU.mult)
            last.then_inc(*done("dve", "w", "m1"))
            for b in range(B):
                dve.wait_ge(*after("pe", "w", f"f{b}"))
                ts(VF[:, b, :], bank((2, 5)[b]), vec("mg"), 1.0 / H1, ALU.mult, ALU.mult, ("w", f"VF{b}"))
            for b in range(B):
                for k in range(2):
                    dve.wait_ge(*after("act", b, f"hb{k}"))
                    mine(b, f"in{k}")
                    tt(A(b, 9 + k), A(b, 9 + k), A(b, 1 + k), ALU.mult, (b, f"xs{k}"))
                for k in range(2):
                    mine(b, f"xs{k}")
                    nc.vector.tensor_tensor_scan(A(b, 9 + k), A(b, 7 + k), A(b, 9 + k), 0.0, ALU.mult, ALU.add)\
                        .then_inc(*done("dve", b, f"h{k}"))
                for k in range(2):
                    mine(b, f"h{k}")
                    tt(A(b, 3 + k), A(b, 3 + k), A(b, 9 + k), ALU.mult, (b, f"gh{k}"))
            for b in range(B):
                dve.wait_ge(*after("pe", b, "rg"))
                tt(A(b, 5), own(b, 0), Xin[b][:, :], ALU.add, (b, "x1"))
                mine(b, "x1")
                tt(A(b, 6), A(b, 5), Xin[b][:, :], ALU.add, (b, "xx"))
            for b in range(B):
                dve.wait_ge(*after("act", b, "h4.r"))
                stt(A(b, 2), A(b, 5), vec("g2"), A(b, 7), ALU.mult, ALU.mult, (b, "xn2"))
            dve.wait_ge(*after("act", "w", "eP"))
            dve.wait_ge(*after("pool", "w", "V"))
            tt(PT, PT, tb("p1"), ALU.mult, ("w", "P"))
            for b in range(B):
                for k in range(2):
                    dve.wait_ge(*after("act", b, f"gm{k}"))
                    dve.wait_ge(*after("pe", b, f"gr{2 + k}"))
                    tt(A(b, 3 + k), own(b, 2 + k), A(b, 3 + k), ALU.mult, (b, f"hm{k}"))
            for b in range(B):
                dve.wait_ge(*after("pe", b, "shr"))
                tt(A(b, 0), own(b, 0), A(b, 6), ALU.add, (b, "s1"))
            for b in range(B):
                normed(b, "ln1", "X1", 1)

            for b in range(B):
                for p in range(2):
                    dve.wait_ge(*after("pe", b, f"xa.s{p}"))
                    red(S(b, 16 * p, 16), grid(own(b, p), J), ALU.max, (b, f"xa.m{p}"))
                    mine(b, f"xa.m{p}")
                    tt(grid(A(b, 2 + p), J), grid(own(b, p), J), over(S(b, 16 * p, 16), [128, 16, J], 2),
                       ALU.subtract, (b, f"xa.d{p}"))
            for b in range(B):
                for p in range(2):
                    dve.wait_ge(*after("act", b, f"xa.e{p}"))
                    red(S(b, 32 + 16 * p, 16), grid(A(b, 2 + p), J), ALU.add, (b, f"xa.u{p}"))
                    mine(b, f"xa.u{p}")
                    inv(S(b, 32 + 16 * p, 16), S(b, 32 + 16 * p, 16), (b, f"xa.i{p}"))
                    mine(b, f"xa.i{p}")
                    tt(grid(A(b, 2 + p), J), grid(A(b, 2 + p), J), over(S(b, 32 + 16 * p, 16), [128, 16, J], 2),
                       ALU.mult, (b, f"xa.p{p}"))
            for b in range(B):
                dve.wait_ge(*after("pe", b, "xa.o"))
                stt(A(b, 0), own(b, 0), vec("bo"), Xin[b][:, :], ALU.add, ALU.add, (b, "s2"))
            for b in range(B):
                normed(b, "ln2", "X2", 1)

            for b in range(B):
                dve.wait_ge(*after("act", b, "m1.r"))
                stt(A(b, 2), Xin[b][:, :], vec("wl1"), A(b, 7), ALU.mult, ALU.mult, (b, "xm"))
            for b in range(B):
                dve.wait_ge(*after("pe", b, "kf"))
                tt(A(b, 5), own(b, 2), w("mla", "COSk"), ALU.mult, (b, "k1"))
                tt(A(b, 6), own(b, 3), w("mla", "SINk"), ALU.mult, (b, "k2"))
                dve.wait_ge(*after("pe", b, "q1"))
                tt(A(b, 4), own(b, 0), w("mla", "COSq"), ALU.mult, (b, "q1"))
                tt(A(b, 1), own(b, 1), w("mla", "SINq"), ALU.mult, (b, "q2"))
                if b == 0:
                    split(dve, tt, b)

            def maxima(b, pair):
                h = 2 * pair
                m = S(b, 64, NT * NH).rearrange("p (t h) -> p t h", h=NH)
                for i, u in enumerate("ABCDE"):
                    ring = bank((5 * pair + i) % 3)
                    dve.wait_ge(*after("pe", b, f"mx{pair}.{u}"))
                    hh = h + (u in "CD")
                    if u in "AC":
                        red(m[:, 3, hh:hh + 1], ring, ALU.max, (b, f"mx{pair}.{u}"))
                    elif u in "BD":
                        nc.vector.tensor_reduce(m[:, 2, hh:hh + 1], ring[:, 0:384], X, ALU.max)
                        red(m[:, 0, hh:hh + 1], ring[:, 384:512], ALU.max, (b, f"mx{pair}.{u}"))
                    else:
                        red(m[:, 1, h:h + 2], grid(ring, 256), ALU.max, (b, f"mx{pair}.{u}"))

            def split_max(b):
                mine(b, f"mx{NH // 2 - 1}.E")
                m = S(b, 64, NT * NH).rearrange("p (t h) -> p t h", h=NH)
                res = S(b, 128, NT * NH).rearrange("p (t h) -> p t h", h=NH)
                hi, mid, lo = (spb[b][:, :, NH * c:NH * c + NH] for c in range(3))
                ts(hi, m, -1.0, None, ALU.mult, ALU.bypass, (b, "nh"))
                mine(b, "nh")
                stt(res, m, -1.0, hi, ALU.mult, ALU.subtract, (b, "nr"))
                mine(b, "nr")
                nc.vector.tensor_copy(mid, res).then_inc(*done("dve", b, "nm"))
                mine(b, "nm")
                tt(lo, res, mid, ALU.subtract, (b, "nl"))

            def attended(b, g):
                dve.wait_ge(*after("pe", b, f"yT{g}"))
                o = bank(7).rearrange("p (t j e) -> p t j e", t=NT, e=32)
                r_ = S(b, 192 + 16 * g, 16).rearrange("p (t j) -> p t j", t=NT)
                inv(r_.unsqueeze(3), o[:, :, :, HD:HD + 1], (b, f"ri{g}"))
                mine(b, f"ri{g}")
                y = A(b, 4).rearrange("p (t g j d) -> p g t j d", t=NT, g=GROUPS, d=HD)[:, g]
                tt(y, o[:, :, :, 0:HD], r_.unsqueeze(3).to_broadcast([128, NT, 4, HD]), ALU.mult, (b, f"y{g}"))

            def attention_out(b):
                dve.wait_ge(*after("pe", b, "mo"))
                tt(A(b, 3), own(b, 1), Xin[b][:, :], ALU.add, (b, "x2a"))
                mine(b, "x2a")
                tt(A(b, 9), A(b, 3), Xin[b][:, :], ALU.add, (b, "x2x"))

            def normed_input(b):
                dve.wait_ge(*after("act", b, "f1.r"))
                stt(A(b, 2), A(b, 3), vec("wl2"), A(b, 7), ALU.mult, ALU.mult, (b, "xf"))

            def logits(b):
                dve.wait_ge(*after("pe", b, "rt"))
                tt(routing(NT * E0 * b, NT * E0), own(b, 2)[:, 0:NT * E0], w("vec", "rb"), ALU.add, (b, "lg"))

            for pair in PAIRS:
                maxima(0, pair)
            split_max(0)
            for pair in PAIRS:
                maxima(1, pair)
                if pair in (4, 6):
                    attended(0, (pair - 4) // 2)
            split_max(1)
            for g in range(2, GROUPS):
                attended(0, g)
            attention_out(0)
            for g in range(GROUPS):
                attended(1, g)
                if g == 1:
                    normed_input(0)
                elif g == 2:
                    logits(0)
            attention_out(1)

            def pick(p, e, tri, t, guard, between):
                bt = B * NT
                n3 = [128, bt, e, e]
                p3 = p.rearrange("p (t e) -> p t e", e=e)
                pj = p3.unsqueeze(2).to_broadcast(n3)
                pe_ = p3.unsqueeze(3).to_broadcast(n3)
                gt, ge = (routing(c, bt * e * e).rearrange("p (t e j) -> p t e j", t=bt, j=e) for c in (128, 640))
                m3 = w("vec", tri).rearrange("p (e j) -> p e j", j=e).unsqueeze(1).to_broadcast(n3)
                rk, we, ws, wi, wn, wr = (routing(c, n_) for c, n_ in
                                          ((1152, bt * e), (1216, bt * e), (1280, bt), (1288, bt), (1296, bt * e),
                                           (1360, bt * e)))
                tt(gt, pj, pe_, ALU.is_gt, ("w", f"gt{t}"))
                tt(ge, pj, pe_, ALU.is_ge, ("w", f"ge{t}"))
                mine("w", f"ge{t}")
                tt(ge, ge, m3, ALU.mult, ("w", f"gx{t}"))
                mine("w", f"gx{t}")
                tt(gt, gt, ge, ALU.max, ("w", f"gm{t}"))
                mine("w", f"gm{t}")
                red(rk, routing(128, bt * e * e).rearrange("p (k j) -> p k j", j=e), ALU.add, ("w", f"rk{t}"))
                between()
                mine("w", f"rk{t}")
                stt(we, rk, 2.0, p, ALU.is_lt, ALU.mult, ("w", f"we{t}"))
                mine("w", f"we{t}")
                red(ws, grid(we, e), ALU.add, ("w", f"ws{t}"))
                mine("w", f"ws{t}")
                if guard:
                    ts(ws, ws, 1e-20, None, ALU.add, ALU.bypass, ("w", f"wa{t}"))
                    mine("w", f"wa{t}")
                inv(wi, ws, ("w", f"wi{t}"))
                mine("w", f"wi{t}")
                tt(grid(wn, e), grid(we, e), over(wi, [128, bt, e], 2), ALU.mult, ("w", f"wn{t}"))
                mine("w", f"wn{t}")
                flat_parts = parts48.rearrange("p b t c -> p (b t) c")
                hi, mid, lo = (flat_parts[:, :, e * c:e * c + e] for c in range(3))
                nc.vector.tensor_copy(hi, grid(wn, e)).then_inc(*done("dve", "w", f"wh{t}"))
                mine("w", f"wh{t}")
                tt(grid(wr, e), grid(wn, e), hi, ALU.subtract, ("w", f"wr{t}"))
                mine("w", f"wr{t}")
                nc.vector.tensor_copy(mid, grid(wr, e)).then_inc(*done("dve", "w", f"wm{t}"))
                mine("w", f"wm{t}")
                tt(lo, grid(wr, e), mid, ALU.subtract, ("w", f"wl{t}"))

            def experts(first, last_, shared, p, s, up, weighted):
                for k in range(first, last_):
                    for b in range(B):
                        dve.wait_ge(*after("act", b, f"{s}{k}"))
                        dve.wait_ge(*after("pe", b, f"{p}u{k}"))
                        if k >= 2:
                            dve.wait_ge(*after("pe", b, f"{p}d{k - 1}"))
                        tt(A(b, 6 + k % 2), own(b, 1), A(b, 4 + k % 2), ALU.mult, (b, f"{up}{k}"))
                        if k >= shared:
                            dve.wait_ge(*after("pe", b, f"{p}w{k}"))
                            mine(b, f"{up}{k}")
                            tt(A(b, 6 + k % 2), own(b, 2), A(b, 6 + k % 2), ALU.mult, (b, f"{weighted}{k}"))

            normed_input(1)
            logits(1)
            dve.wait_ge(*after("act", "w", "rt"))
            p0 = routing(64, B * NT * E0)
            ts(p0, p0, 1.0, None, ALU.add, ALU.bypass, ("w", "pd"))
            mine("w", "pd")
            inv(p0, p0, ("w", "pr"))
            mine("w", "pr")
            pick(p0, E0, "tri0", "", False, lambda: experts(0, SH0, SH0, "f", "sl", "hu", "hw"))
            experts(SH0, U0, SH0, "f", "sl", "hu", "hw")
            for b in range(B):
                dve.wait_ge(*after("pe", b, f"fd{U0}"))
                tt(A(b, 0), own(b, 3), A(b, 9), ALU.add, (b, "s3"))
            for b in range(B):
                normed(b, "ln3", "X3", 0)

            def parts_bc(b, n):
                return A(b, 3)[:, 0:256].bitcast(BF16)[0:n, :]

            def upper(b):
                dve.wait_ge(*after("act", b, "bc"))
                nc.vector.tensor_copy(parts_bc(b, 96), A(b, 2)[0:96, :]).then_inc(*done("dve", b, "bh"))

            def rest(b):
                mine(b, "bh")
                tt(A(b, 5)[0:64, :], A(b, 2)[0:64, :], parts_bc(b, 64), ALU.subtract, (b, "br"))

            def positive(b):
                dve.wait_ge(*after("pe", b, "de"))
                dve.wait_ge(*after("act", b, "ab"))
                ts(A(b, 8), own(b, 1), vec("bd"), 0.0, ALU.add, ALU.max, (b, "rl"))

            def middle(b):
                mine(b, "br")
                nc.vector.tensor_copy(parts_bc(b, 64), A(b, 5)[0:64, :]).then_inc(*done("dve", b, "bm"))

            def lower(b):
                mine(b, "bm")
                tt(parts_bc(b, 32), A(b, 5)[0:32, :], parts_bc(b, 32), ALU.subtract, (b, "bl"))

            def step_size(b):
                dve.wait_ge(*after("act", b, "sp"))
                mine(b, "rl")
                tt(A(b, 8), A(b, 8), A(b, 7), ALU.add, (b, "dl"))

            upper(0)
            rest(0)
            positive(0)
            middle(0)
            upper(1)
            lower(0)
            rest(1)
            step_size(0)
            positive(1)
            middle(1)
            lower(1)
            step_size(1)
            for i in range(NS):
                for b in range(B):
                    dve.wait_ge(*after("act", b, f"aa{i}"))
                    dve.wait_ge(*after("pool", b, f"by{i}"))
                    nc.vector.tensor_tensor_scan(A(b, 14 + i % 2), A(b, 9 + i % 2), A(b, 4 + i % 2), 0.0, ALU.mult,
                                                 ALU.add).then_inc(*done("dve", b, f"sc{i}"))
                    mine(b, f"sc{i}")
                    dve.wait_ge(*after("pe", b, f"cn{i}"))
                    if i >= 2:
                        dve.wait_ge(*after("pe", b, f"yn{i - 1}"))
                    tt(A(b, 12 + i % 2), own(b, 1), A(b, 14 + i % 2), ALU.mult, (b, f"hc{i}"))
            for b in range(B):
                dve.wait_ge(*after("pe", b, f"yn{NS}"))
                tt(A(b, 0), own(b, 2), Xin[b][:, :], ALU.add, (b, "s4"))
            for b in range(B):
                normed(b, "ln4", "X4", 0)

            for b in range(B):
                dve.wait_ge(*after("pe", b, "xb.s"))
                red(S(b, 0, 16), grid(own(b, 2), J), ALU.max, (b, "xb.m"))
                mine(b, "xb.m")
                tt(grid(A(b, 2), J), grid(own(b, 2), J), over(S(b, 0, 16), [128, 16, J], 2), ALU.subtract,
                   (b, "xb.d"))
            for b in range(B):
                if b == 0:
                    for l in range(B):
                        dve.wait_ge(*after("act", l, "lni.r"))
                        tt(A(l, 9), own(l, 0), A(l, 7), ALU.mult, (l, "lni.x"))
                dve.wait_ge(*after("act", b, "xb.e"))
                red(S(b, 32, 16), grid(A(b, 2), J), ALU.add, (b, "xb.u"))
                mine(b, "xb.u")
                inv(S(b, 32, 16), S(b, 32, 16), (b, "xb.i"))
                mine(b, "xb.i")
                tt(grid(S(b, 32, 16), H1), grid(S(b, 32, 16), H1),
                   over(tmaskf[:, NT * b:NT * b + NT], [128, NT, H1], 2), ALU.mult, (b, "xb.k"))
                mine(b, "xb.k")
                tt(grid(A(b, 2), J), grid(A(b, 2), J), over(S(b, 32, 16), [128, 16, J], 2), ALU.mult, (b, "xb.p"))
            for b in range(B):
                dve.wait_ge(*after("act", b, "s1"))
                tt(A(b, 10), A(b, 10), A(b, 4), ALU.mult, (b, "lni.z"))
                mine(b, "lni.z")
                tt(A(b, 2), A(b, 10), A(b, 5), ALU.add, (b, "xin"))

            for h in range(2):
                Kh = [Kf[:, c, 2 * h:2 * h + 2, :].unsqueeze(2).to_broadcast([128, 2, B, 128]) for c in range(2)]
                Xh = [bank(4 * h + 2 * c).rearrange("p (f b d) -> p f b d", f=2, b=B) for c in range(2)]
                Y = [Yf[:, c, 2 * h:2 * h + 2, :] for c in range(2)]
                Y4 = [y.rearrange("p f (b d) -> p f b d", b=B) for y in Y]
                Z4 = [Zt[:, c, :].rearrange("p (f b d) -> p f b d", f=2, b=B) for c in range(2)]
                Z = [Zt[:, c, :].rearrange("p (f n) -> p f n", f=2) for c in range(2)]
                dve.wait_ge(*after("act", "w", "kf1"))
                dve.wait_ge(*after("pe", "w", f"xf{h}1"))
                if h:
                    mine("w", "yi0")
                tt(Y4[0], Xh[0], Kh[0], ALU.mult, ("w", f"rr{h}"))
                tt(Z4[0], Xh[1], Kh[1], ALU.mult, ("w", f"ii{h}"))
                tt(Y4[1], Xh[0], Kh[1], ALU.mult, ("w", f"ri{h}"))
                tt(Z4[1], Xh[1], Kh[0], ALU.mult, ("w", f"ir{h}"))
                mine("w", f"ii{h}")
                tt(Y[0], Y[0], Z[0], ALU.subtract, ("w", f"yr{h}"))
                mine("w", f"ir{h}")
                tt(Y[1], Y[1], Z[1], ALU.add, ("w", f"yi{h}"))
            for b in range(B):
                dve.wait_ge(*after("pe", b, "inv"))
                stt(A(b, 4), A(b, 2), vec("Ds"), own(b, 1), ALU.mult, ALU.add, (b, "sk"))
                mine(b, "sk")
                dve.wait_ge(*after("act", b, "s3"))
                tt(A(b, 4), A(b, 4), A(b, 6), ALU.mult, (b, "fo"))
                mine(b, "fo")
                tt(A(b, 4), A(b, 4), A(b, 8), ALU.add, (b, "fp"))
                mine(b, "fp")
                tt(A(b, 0), A(b, 4), Xin[b][:, :], ALU.add, (b, "xt"))
            for b in range(B):
                dve.wait_ge(*after("act", b, "lnf.r"))
                tt(A(b, 9), own(b, 2), A(b, 7), ALU.mult, (b, "lnf.x"))
            for b in range(B):
                dve.wait_ge(*after("pe", b, "w2"))
                stt(A(b, 0), own(b, 0), vec("b2"), A(b, 0), ALU.add, ALU.add, (b, "xt2"))
            for b in range(B):
                dve.wait_ge(*after("act", b, "lno.r"))
                tt(A(b, 9), own(b, 1), A(b, 7), ALU.mult, (b, "lno.x"))
            for b in range(B):
                dve.wait_ge(*after("act", b, "lno.g"))
                tt(A(b, 0), A(b, 10), Xin[b][:, :], ALU.add, (b, "s5"))
            for b in range(B):
                normed(b, "ln5", "X5", 1)

            for b in range(B):
                dve.wait_ge(*after("pe", b, "rt1"))
                lg = grid(own(b, 2)[:, 0:NT * E1], E1)
                red(routing(1424 + NT * b, NT), lg, ALU.max, (b, "mx"))
                mine(b, "mx")
                tt(grid(routing(NT * E1 * b, NT * E1), E1), lg, over(routing(1424 + NT * b, NT), [128, NT, E1], 2),
                   ALU.subtract, (b, "ms"))
            experts(0, 1, SH1, "e", "el", "eu", "ew")
            dve.wait_ge(*after("act", "w", "rt1"))
            p1, total_ = routing(64, B * NT * E1), routing(1432, B * NT)
            red(total_, grid(p1, E1), ALU.add, ("w", "su"))
            mine("w", "su")
            inv(total_, total_, ("w", "iv"))
            mine("w", "iv")
            tt(grid(p1, E1), grid(p1, E1), over(total_, [128, B * NT, E1], 2), ALU.mult, ("w", "pr1"))
            mine("w", "pr1")
            pick(p1, E1, "tri1", "1", True, lambda: experts(1, SH1, SH1, "e", "el", "eu", "ew"))
            experts(SH1, UB1, SH1, "e", "el", "eu", "ew")
            for b in range(B):
                dve.wait_ge(*after("pe", b, f"ed{UB1}"))
                tt(A(b, 0), own(b, 3), Xin[b][:, :], ALU.add, (b, "s6"))
            for b in range(B):
                normed(b, "ln6", "X6", 0)

        @block.gpsimd
        def _(pool):
            def tt(out_, a, b_, op, step):
                nc.gpsimd.tensor_tensor(out_, a, b_, op).then_inc(*done("pool", *step))

            def ts(out_, a, s1, s2, op0, op1, step):
                nc.gpsimd.tensor_scalar(out_, a, s1, s2, op0, op1).then_inc(*done("pool", *step))

            def mine(lane, name):
                pool.wait_ge(*after("pool", lane, name))

            for b in range(B):
                nc.gpsimd.memset(Vaug[b][:, :, :, :], 1.0).then_inc(*done("pool", "w", f"va{b}"))
            pool.wait_ge(loads["vec"], 16)
            ts(fb_r, w("vec", "fb"), 0.0, None, ALU.max, ALU.bypass, ("w", "fb.r"))
            pool.wait_ge(*after("act", "w", "fb.l"))
            mine("w", "fb.r")
            tt(fb_r, fb_r, fb_l, ALU.add, ("w", "fb.s"))
            mine("w", "fb.s")
            ts(fcoef, fb_r, -4.0, None, ALU.mult, ALU.bypass, ("w", "fb.c"))
            ts(bhalf, w("vec", "bg"), 0.5, None, ALU.mult, ALU.bypass, ("w", "bh"))
            ts(bfilm, w("vec", "bfi"), vec("mg"), None, ALU.mult, ALU.bypass, ("w", "bf"))
            mine("w", "bf")
            scales = bfilm.rearrange("p (a two) -> p two a", two=2)[:, 0]
            ts(scales, scales, 1.0, None, ALU.add, ALU.bypass, ("w", "bf1"))

            def spread(i, l):
                return dct(i).unsqueeze(2).to_broadcast([128, 128, l])

            def lags(name, l):
                return w("s4d", name).unsqueeze(1).to_broadcast([128, 128, l])

            pool.wait_ge(*after("dve", "w", "z3"))
            tt(tb("p2"), spread(4, PA), lags("la", PA), ALU.mult, ("w", "tP"))
            tt(tb("tQ"), spread(4, PB_), lags("lb", PB_), ALU.mult, ("w", "tQ"))
            tt(PT, spread(1, PA), lags("la", PA), ALU.mult, ("w", "aP"))
            tt(QT, spread(1, PB_), lags("lb", PB_), ALU.mult, ("w", "aQ"))

            link = [0]

            def chain(out_, a, b_, op):
                link[0] += 1
                if b_ is None:
                    ts(out_, a, op, None, ALU.mult, ALU.bypass, ("w", f"dc{link[0]}"))
                else:
                    tt(out_, a, b_, op, ("w", f"dc{link[0]}"))
                mine("w", f"dc{link[0]}")

            Are, Aim, Cre, Cim = (w("s4d", k) for k in ("Are", "Aim", "Cre", "Cim"))
            pool.wait_ge(*after("dve", "w", "a6"))
            chain(dct(8), dct(3), dct(8), ALU.mult)
            chain(dct(8), dct(8), None, 2.0)
            chain(dct(9), dct(6), dct(6), ALU.mult)
            chain(dct(9), dct(9), None, 2.0)
            chain(dct(3), dct(8), dct(9), ALU.mult)
            chain(dct(3), dct(8), dct(3), ALU.subtract)
            chain(dct(3), dct(3), dct(9), ALU.subtract)
            chain(dct(10), dct(8), dct(7), ALU.mult)
            chain(dct(10), dct(10), dct(7), ALU.add)
            for to, x, y, op in ((8, Cre, Cim, ALU.subtract), (7, Cim, Cre, ALU.add)):
                tt(dct(to), x, dct(3), ALU.mult, ("w", f"dc{link[0] + 1}"))
                link[0] += 1
                tt(dct(9), y, dct(10), ALU.mult, ("w", f"dc{link[0] + 1}"))
                link[0] += 1
                mine("w", f"dc{link[0]}")
                chain(dct(to), dct(to), dct(9), op)
            chain(dct(3), dct(8), dct(11), ALU.mult)
            chain(dct(6), dct(7), dct(11), ALU.mult)
            chain(dct(8), dct(3), Are, ALU.mult)
            chain(dct(9), dct(6), Aim, ALU.mult)
            chain(dct(8), dct(8), dct(9), ALU.add)
            chain(dct(5), dct(6), Are, ALU.mult)
            chain(dct(9), dct(3), Aim, ALU.mult)
            chain(dct(5), dct(5), dct(9), ALU.subtract)
            pool.wait_ge(*after("act", "w", "s2"))
            tt(tb("p1"), tb("p1"), spread(8, PA), ALU.mult, ("w", "U1"))
            tt(tb("p2"), tb("p2"), spread(5, PA), ALU.mult, ("w", "U2"))
            mine("w", "U2")
            tt(tb("p1"), tb("p1"), tb("p2"), ALU.add, ("w", "V"))
            pool.wait_ge(*after("act", "w", "sQ"))
            pool.wait_ge(*after("act", "w", "eQ"))
            tt(QT, QT, tb("tQ"), ALU.mult, ("w", "Q"))

            split(pool, tt, 1)

            for i in range(NS):
                for b in range(B):
                    if i == 0:
                        pool.wait_ge(*after("dve", b, "dl"))
                        tt(A(b, 7), A(b, 8), Xin[b][:, :], ALU.mult, (b, "dx"))
                        mine(b, "dx")
                    pool.wait_ge(*after("act", b, f"bb{i}"))
                    tt(A(b, 4 + i % 2), A(b, 4 + i % 2), A(b, 7), ALU.mult, (b, f"by{i}"))

        for k, v in order.items():
            assert said[k] == len(v), (k, v[said[k]])


def lay_out(i):
    f4 = np.float32
    lay = layouts()
    a = {k: np.asarray(v) for k, v in i.items()}

    def bf16_words(table):
        return (np.ascontiguousarray(table, f4).view(np.uint32) >> 16).astype(np.uint16).view(f4)

    def pack(group, parts):
        d, n = lay[group]
        out = np.zeros((128, n), f4)
        assert set(parts) == set(d), (group, set(parts) ^ set(d))
        for name, v in parts.items():
            c, m = d[name]
            r0, v = v if isinstance(v, tuple) else (0, v)
            v = np.asarray(v).reshape(v.shape[0], -1)
            assert v.shape[1] == m and v.dtype == f4, (group, name, v.shape, m, v.dtype)
            out[r0:r0 + v.shape[0], c:c + m] = v
        return bf16_words(out) if group in BF_GROUPS else out

    def cols(v):
        return v.reshape(-1, 128).T

    def rows(v):
        return v.reshape(-1, 128, v.shape[1]).transpose(1, 0, 2).reshape(128, -1)

    def full(v, n=1):
        return np.broadcast_to(np.asarray(v, f4).reshape(1, -1), (128, n)).astype(f4)

    def halves(x, y):
        return np.repeat(np.array([x, y], f4), 64)[:, None]

    def tri(e):
        return full(np.tril(np.ones((e, e), f4), -1), e * e)

    bbc = np.concatenate([a["L1_attn_bb"], a["L1_attn_bc"]])
    wbc = np.concatenate([a["L1_attn_Wb"], a["L1_attn_Wc"]]).T
    out = {"x": a["x"].reshape(B * T, D).T}
    out["vec"] = pack("vec", {
        "g1": cols(a["L0_attn_gamma1"]), "g2": cols(a["L0_attn_gamma2"]),
        "cw": a["L0_attn_conv_w"].reshape(2, 128, 4).transpose(1, 0, 2), "cb": cols(a["L0_attn_conv_b"]),
        "bg": cols(a["L0_attn_b_gates"]), "fb": cols(a["L0_attn_forget_base"]), "bo": cols(a["L0_xattn_b_o"]),
        "wl1": cols(a["L0_ffn_w_ln1"]), "wl2": cols(a["L0_ffn_w_ln2"]), "A": a["L1_attn_A"],
        "bd": cols(a["L1_attn_bd"]), "bBC": np.tile(bbc, 3)[:, None], "gni": cols(a["L1_xattn_g_norm_in"]),
        "bni": cols(a["L1_xattn_b_norm_in"]), "gff": cols(a["L1_xattn_g_ffn"]), "bff": cols(a["L1_xattn_b_ffn"]),
        "gno": cols(a["L1_xattn_g_norm_out"]), "bno": cols(a["L1_xattn_b_norm_out"]), "b1": cols(a["L1_xattn_b1"]),
        "b2": cols(a["L1_xattn_b2"]),
        "bfi": cols(np.concatenate([a["L1_xattn_b_film_in"], a["L1_xattn_b_film_out"]])),
        "Ds": cols(a["L1_xattn_D_skip"]), "mg": full(a["L1_xattn_mod_gate"]), "eps": full(1e-5),
        "q25": full(0.25 * (1.0 + 1e-6)), "one": full(1.0), "phq": halves(0.25, 0.0), "ph1": halves(0.25, 0.5),
        "ph2": halves(0.5, 0.75), "raq": halves(0.25 * TWO_PI, 0.0), "ra1": halves(0.25 * TWO_PI, 0.5 * TWO_PI),
        "ra2": halves(0.5 * TWO_PI, 0.75 * TWO_PI),
        "rb": full(np.tile(a["L0_ffn_routing_bias"], NT), NT * E0), "tri0": tri(E0), "tri1": tri(E1)})
    out["hawk"] = pack("hawk", {
        "Wga": rows(a["L0_attn_W_gates"].T), "Wou": rows(a["L0_attn_W_out"].T),
        "Wgr": a["L0_attn_W_grow"].T, "Wsh": rows(a["L0_attn_W_shrink"].T)})
    out["win"] = pack("win", {"Win": a["L0_attn_W_in"].T})
    out["xa0"] = pack("xa0", {
        "Wk": a["L0_xattn_W_k"], "Wv": a["L0_xattn_W_v"], "WqT": rows(a["L0_xattn_W_q"].T),
        "Wo": rows(a["L0_xattn_W_o"]), "ctx": a["ctx_768"].reshape(B * J, CD).T})
    eye = np.eye(128, dtype=f4)
    out["sq"] = pack("sq", {"Cm": eye - f4(1 / 128), "ones": np.ones((128, 128), f4), "id": eye})

    half = HD // 2
    kv, q, kx, kr, ks = (np.zeros((r_, 128), f4) for r_ in (32, 32, 32, 128, 128))
    qs = np.zeros((32, 128), f4)
    turned = [(d + half // 2) % half for d in range(half)]
    for d in range(half):
        plain, rope, swap = (np.arange(NH) * half + e for e in (d, d, turned[d]))
        kx[:, NH * d:NH * d + NH] = a["L0_ffn_W_ku"][:, plain]
        q[:, NH * d:NH * d + NH] = a["L0_ffn_W_qu"][:, plain]
        r0 = NH * (half + d)
        kr[:, r0:r0 + NH] = a["L0_ffn_W_ropek"][:, rope]
        ks[:, r0:r0 + NH] = a["L0_ffn_W_ropek"][:, swap]
        q[:, r0:r0 + NH] = a["L0_ffn_W_ropeq"][:, rope]
        qs[:, r0:r0 + NH] = a["L0_ffn_W_ropeq"][:, swap]
    freq = (1.0 / 10000.0 ** (np.arange(0, half, 2, dtype=f4) / half)).astype(f4)
    angle = (np.arange(T, dtype=f4)[:, None] * freq[None, :]).astype(f4).astype(np.float64)
    cos, sin = np.ones((128, T)), np.zeros((128, T))
    for d in range(half):
        r0 = NH * (half + d)
        cos[r0:r0 + NH] = np.cos(angle[:, d % 2])
        sin[r0:r0 + NH] = np.sin(angle[:, d % 2]) * (-1 if d < half // 2 else 1)
    sc = HD ** -0.5
    out["mla"] = pack("mla", {
        "lat": np.concatenate([a["L0_ffn_W_kvd"], a["L0_ffn_W_qd"]], 1), "kx": kx, "kr": kr, "ks": ks,
        "q": (32, q), "qs": (32, qs), "v": a["L0_ffn_W_vu"], "o": a["L0_ffn_W_o"],
        "COSk": cos.astype(f4), "SINk": sin.astype(f4), "COSq": (cos * sc).astype(f4),
        "SINq": (sin * sc).astype(f4)})

    def experts(shared, routed):
        return np.concatenate([shared, routed.transpose(1, 0, 2).reshape(128, -1)], 1)

    out["moe0"] = pack("moe0", {
        "g": experts(a["L0_ffn_Wg_s"], a["L0_ffn_Wg_r"]), "u": experts(a["L0_ffn_Wu_s"], a["L0_ffn_Wu_r"]),
        "d": rows(np.concatenate([a["L0_ffn_Wd_s"], a["L0_ffn_Wd_r"].reshape(-1, 128)])),
        "r": a["L0_ffn_W_router"]})
    out["late"] = pack("late", {
        "Wd": a["L1_attn_Wd"].T, "WBC": np.tile(wbc, (1, 3)), "WqT": a["L1_xattn_Wq"].T, "Wk": a["L1_xattn_Wk"],
        "Wv": a["L1_xattn_Wv"], "film": np.concatenate([a["L1_xattn_W_film_in"], a["L1_xattn_W_film_out"]], 1),
        "W1": a["L1_xattn_W1"], "W2": rows(a["L1_xattn_W2"]), "gate": a["L1_ffn_gate_w"].T})
    twice = {k: np.tile(a[f"L1_xattn_{v}"].T, (2, 1)) for k, v in
             (("Are", "A_re"), ("Aim", "A_im"), ("Cre", "C_re"), ("Cim", "C_im"))}
    out["s4d"] = pack("s4d", {**twice, "ldt": full(a["L1_xattn_log_dt"], 128), "lb": full(np.arange(PB_), PB_),
                              "la": full(np.arange(PA) * PB_, PA)})
    theta = 2 * np.pi * np.outer(np.arange(T), np.arange(NF) + 0.5) / (2 * T)
    F = np.concatenate([np.cos(theta), -np.sin(theta)], 1).astype(f4)
    G = (np.concatenate([np.cos(theta.T), -np.sin(theta.T)]) * (2 * 2 / (2 * T))).astype(f4)
    out["dft"] = pack("dft", {"F": rows(F), "G": rows(G)})

    def padded(v, axis):
        z = np.zeros([128 * SH1 - 2 * I1 if k == axis else n for k, n in enumerate(v.shape)], f4)
        return np.concatenate([v, z], axis)

    out["ffn1"] = pack("ffn1", {
        "g": experts(padded(a["L1_ffn_swg"], 1), a["L1_ffn_wg"]), "u": experts(padded(a["L1_ffn_swu"], 1), a["L1_ffn_wu"]),
        "d": rows(np.concatenate([padded(a["L1_ffn_swd"], 0), a["L1_ffn_wd"].reshape(-1, 128)]))})
    k = np.arange(128)
    low = np.where(k[:, None] < k[None, :], -BIG, 0.0).astype(f4)
    out["bf"] = pack("bf", {"id": eye, "mS": low, "mT": low.T,
                            "one": np.ones((128, 128), f4)})
    out["sel0"] = pack("sel0", {"s": np.tile(np.repeat(np.eye(E0, dtype=f4), 128, 1), (3, 1))})
    out["selA"] = pack("selA", {"s": np.tile(np.repeat(np.eye(2 * NS, dtype=f4), 128, 1), (3, 1))})
    out["sel1"] = pack("sel1", {"s": np.tile(np.repeat(np.eye(E1, dtype=f4), I1, 1), (3, 1))})
    out["ones"] = bf16_words(np.repeat(np.array([0] * ZROWS + [1] * 3, f4)[:, None], NH * T, 1))

    def heads(m, h):
        return np.repeat(m.reshape(B, 1, J), h, 1).reshape(1, -1)

    m0, m1 = (a[f"mask_BxS2_{s}"].view(np.uint8) for s in ("bk0", "bf1"))
    out["km"] = np.repeat(heads(m0, H0), 128, 0)
    out["kr"] = np.concatenate([heads(m0, H0), heads(m1, H1)], 1)
    out["tm"] = a["mask_BxS_bf1"].view(np.uint8).reshape(B * NT, 128).T
    out = {k: np.ascontiguousarray(v) for k, v in out.items()}
    for k in ("km", "kr", "tm"):
        out[k] = out[k].view(np.uint32)
    return out


def kernel(**inputs):
    import concourse.bacc as bacc
    from concourse.bass_utils import run_bass_kernel_spmd as run

    arrays = lay_out(inputs)
    nc = bacc.Bacc("TRN2", target_bir_lowering=False, num_devices=1)
    dram = {n: nc.dram_tensor(f"in_{n}", v.shape, mybir.dt.from_np(v.dtype), kind="ExternalInput").ap()
            for n, v in arrays.items()}
    out = nc.dram_tensor("out", (D, B * T), F32, kind="ExternalOutput").ap()
    build(nc, dram, out)
    r = run(nc, [{f"in_{n}": v for n, v in arrays.items()}], core_ids=[0])
    return np.ascontiguousarray(r.results[0]["out"].T).reshape(B, T, D)
```
